# Optimizing a Trainium2 kernel written in Bass

```python
import numpy as np
import jax
import jax.numpy as jnp

def _softmax(x, axis=-1):
    return jax.nn.softmax(x, axis=axis)
def _gelu(x):
    return jax.nn.gelu(x, approximate=True)
def _silu(x):
    return jax.nn.silu(x)
def _sigmoid(x):
    return jax.nn.sigmoid(x)
def _layernorm(x, axis=-1, eps=1e-5):
    m = jnp.mean(x, axis=axis, keepdims=True)
    v = jnp.var(x, axis=axis, keepdims=True)
    return (x - m) / jnp.sqrt(v + eps)
def _scatter_add(tgt, idx, src, axis=0):
    return tgt.at[idx].add(src)
def _segment_sum(src, seg, n):
    return jax.ops.segment_sum(src, seg, n)

kernel_name = 'mk_adj_resnorm_d4_adj_512_0fe55c'

def setup_inputs(seed: int = 0):
    np.random.seed(seed)
    _w = jnp.asarray
    def _rec_inputs():
        import jax
        import jax.numpy as jnp
        _gk = jax.random.key(seed)
        x = -0.0005207 + 1.001 * jax.random.normal(jax.random.fold_in(_gk, 1), (2708, 512), jnp.float32)
        _a = jax.random.bernoulli(jax.random.fold_in(_gk, 2), 0.00590842, (2708, 2708))
        _a = jnp.logical_or(_a, jnp.swapaxes(_a, -1, -2))
        _a = jnp.logical_or(_a, jnp.eye(2708, dtype=bool))
        _af = _a.astype(jnp.float32)
        adj = _af
        return x, adj
    x, adj = _rec_inputs()
    def _L0_gnn_setup():
        import jax, jax.numpy as jnp
        import numpy as np
        N = 4096
        INPUT_DIM = 512
        KEY_DIM = 64
        OUT_DIM = 512
        N_HEADS = 8

        def _xavier_normal(key, shape, gain):
            fan_in, fan_out = (shape[-2], shape[-1])
            std = gain * (2.0 / (fan_in + fan_out)) ** 0.5
            return jax.random.normal(key, shape, dtype=jnp.float32) * std
        key = jax.random.key(seed)
        kx, ka, kk, kq, kv, ko = jax.random.split(key, 6)
        gain = 2.0 ** 0.5
        node_matrix = jax.random.normal(kx, (N, INPUT_DIM), dtype=jnp.float32)
        adjacency_matrix = jax.random.randint(ka, (N, N), 0, 2).astype(jnp.float32)
        Wks = _xavier_normal(kk, (N_HEADS, INPUT_DIM, KEY_DIM), gain)
        Wqs = _xavier_normal(kq, (N_HEADS, INPUT_DIM, KEY_DIM), gain)
        Wvs = _xavier_normal(kv, (N_HEADS, INPUT_DIM, KEY_DIM), gain)
        Wo = _xavier_normal(ko, (N_HEADS, KEY_DIM, OUT_DIM), gain)
        return {'node_matrix': node_matrix, 'adjacency_matrix': adjacency_matrix, 'Wks': Wks, 'Wqs': Wqs, 'Wvs': Wvs, 'Wo': Wo}
    _L0_gnn_all = _L0_gnn_setup()
    _L0_gnn_in = {k: v for k, v in _L0_gnn_all.items() if k in ('Wks', 'Wqs', 'Wvs', 'Wo', )}
    del _L0_gnn_all

    def _L1_gnn_setup():
        import jax, jax.numpy as jnp
        import numpy as np
        N, IN_F, OUT_F = (8192, 512, 512)
        HID = OUT_F // 2
        key = jax.random.key(seed)
        ks = jax.random.split(key, 6)
        x = jax.random.normal(ks[0], (N, IN_F), dtype=jnp.float32)
        adj = jax.random.uniform(ks[1], (N, N), dtype=jnp.float32)
        W1 = jax.random.normal(ks[2], (HID, IN_F), dtype=jnp.float32) * np.sqrt(2.0 / IN_F)
        b1 = jnp.zeros((HID,), dtype=jnp.float32)
        W2 = jax.random.normal(ks[3], (OUT_F, HID), dtype=jnp.float32) * np.sqrt(2.0 / HID)
        b2 = jnp.zeros((OUT_F,), dtype=jnp.float32)
        return {'x': x, 'adj': adj, 'W1': W1, 'b1': b1, 'W2': W2, 'b2': b2}
    _L1_gnn_all = _L1_gnn_setup()
    _L1_gnn_in = {k: v for k, v in _L1_gnn_all.items() if k in ('W1', 'b1', 'W2', 'b2', )}
    del _L1_gnn_all

    def _L2_gnn_setup():
        import jax, jax.numpy as jnp
        import numpy as np
        IN_C, HID_C = (512, 512)
        ALPHA = 0.2
        N = 8192
        NEG_BIG = -9000000000000000.0
        key = jax.random.key(seed)
        k1, k2, k3, k4, k5, k6, k7 = jax.random.split(key, 7)
        h = jax.random.normal(k1, (N, IN_C), dtype=jnp.float32)
        adj = jax.random.randint(k2, (N, N), 0, 2).astype(jnp.float32)
        gain = np.sqrt(2.0 / (1.0 + ALPHA ** 2))
        lim_W = gain * np.sqrt(6.0 / (2 * IN_C + HID_C))
        W = jax.random.uniform(k3, (2 * IN_C, HID_C), jnp.float32, -lim_W, lim_W)
        lim_a = np.sqrt(1.0 / HID_C)
        a_w = jax.random.uniform(k4, (HID_C,), jnp.float32, -lim_a, lim_a)
        a_b = jax.random.uniform(k5, (), jnp.float32, -lim_a, lim_a)
        lim_fc = np.sqrt(1.0 / IN_C)
        fc_w = jax.random.uniform(k6, (IN_C, HID_C), jnp.float32, -lim_fc, lim_fc)
        fc_b = jax.random.uniform(k7, (HID_C,), jnp.float32, -lim_fc, lim_fc)
        return {'h': h, 'adj': adj, 'W': W, 'a_w': a_w, 'a_b': a_b, 'fc_w': fc_w, 'fc_b': fc_b}
    _L2_gnn_all = _L2_gnn_setup()
    _L2_gnn_in = {k: v for k, v in _L2_gnn_all.items() if k in ('W', 'a_w', 'a_b', 'fc_w', 'fc_b', )}
    del _L2_gnn_all

    def _L3_gnn_setup():
        import jax, jax.numpy as jnp
        import numpy as np
        N = 8192
        IN_F = 512
        OUT_F = 512
        key = jax.random.key(seed)
        k1, k2, k3 = jax.random.split(key, 3)
        x = jax.random.normal(k1, (N, IN_F), dtype=jnp.float32)
        adj = jax.random.uniform(k2, (N, N), dtype=jnp.float32)
        W = jax.random.normal(k3, (IN_F, OUT_F), dtype=jnp.float32) * 0.1
        return {'x': x, 'adj': adj, 'W': W}
    _L3_gnn_all = _L3_gnn_setup()
    _L3_gnn_in = {k: v for k, v in _L3_gnn_all.items() if k in ('W', )}
    del _L3_gnn_all

    return {
        "x": x,
        "adj": adj,
        "L0_gnn_Wks": _L0_gnn_in["Wks"],
        "L0_gnn_Wqs": _L0_gnn_in["Wqs"],
        "L0_gnn_Wvs": _L0_gnn_in["Wvs"],
        "L0_gnn_Wo": _L0_gnn_in["Wo"],
        "L1_gnn_W1": _L1_gnn_in["W1"],
        "L1_gnn_b1": _L1_gnn_in["b1"],
        "L1_gnn_W2": _L1_gnn_in["W2"],
        "L1_gnn_b2": _L1_gnn_in["b2"],
        "L2_gnn_W": _L2_gnn_in["W"],
        "L2_gnn_a_w": _L2_gnn_in["a_w"],
        "L2_gnn_a_b": _L2_gnn_in["a_b"],
        "L2_gnn_fc_w": _L2_gnn_in["fc_w"],
        "L2_gnn_fc_b": _L2_gnn_in["fc_b"],
        "L3_gnn_W": _L3_gnn_in["W"],
    }

def reference(x, adj, L0_gnn_Wks, L0_gnn_Wqs, L0_gnn_Wvs, L0_gnn_Wo, L1_gnn_W1, L1_gnn_b1, L1_gnn_W2, L1_gnn_b2, L2_gnn_W, L2_gnn_a_w, L2_gnn_a_b, L2_gnn_fc_w, L2_gnn_fc_b, L3_gnn_W):
    import jax
    import jax.numpy as jnp
    def _L0_gnn_ref(node_matrix, adjacency_matrix, Wks, Wqs, Wvs, Wo):
        import jax, jax.numpy as jnp
        import numpy as np
        N = 4096
        INPUT_DIM = 512
        KEY_DIM = 64
        OUT_DIM = 512
        N_HEADS = 8

        def _xavier_normal(key, shape, gain):
            fan_in, fan_out = (shape[-2], shape[-1])
            std = gain * (2.0 / (fan_in + fan_out)) ** 0.5
            return jax.random.normal(key, shape, dtype=jnp.float32) * std
        n = adjacency_matrix.shape[0]
        adj = jnp.maximum(adjacency_matrix, jnp.eye(n, dtype=adjacency_matrix.dtype))
        keys = jnp.einsum('nj,hjk->hnk', node_matrix, Wks)
        queries = jnp.einsum('nj,hjk->hnk', node_matrix, Wqs)
        values = jnp.einsum('nj,hjk->hnk', node_matrix, Wvs)
        key_dim = Wks.shape[-1]
        atts = jnp.einsum('hqk,hmk->hqm', queries, keys) / key_dim ** 0.5
        atts = atts - 1e+16 * (1.0 - adj)[None, :, :]
        atts = jax.nn.softmax(atts, axis=-1)
        return jnp.einsum('hqm,hmk,hko->qo', atts, values, Wo)

    def _L1_gnn_ref(x, adj, W1, b1, W2, b2):
        import jax, jax.numpy as jnp
        import numpy as np
        N, IN_F, OUT_F = (8192, 512, 512)
        HID = OUT_F // 2
        h = x @ W1.T + b1
        h = h @ W2.T + b2
        A = adj + jnp.eye(adj.shape[0], dtype=adj.dtype)
        rowsum = A.sum(axis=1)
        r_inv_sqrt = jnp.power(rowsum, -0.5)
        r_inv_sqrt = jnp.where(jnp.isinf(r_inv_sqrt), 0.0, r_inv_sqrt)
        A = r_inv_sqrt[:, None] * A * r_inv_sqrt[None, :]
        return A.astype(jnp.float32) @ h.astype(jnp.float32)

    def _L2_gnn_ref(h, adj, W, a_w, a_b, fc_w, fc_b):
        import jax, jax.numpy as jnp
        import numpy as np
        IN_C, HID_C = (512, 512)
        ALPHA = 0.2
        N = 8192
        NEG_BIG = -9000000000000000.0
        Wh1 = h @ W[:IN_C]
        Wh2 = h @ W[IN_C:]
        s1 = Wh1 @ a_w
        s2 = Wh2 @ a_w
        e = s1[:, None] + s2[None, :] + a_b
        e = jnp.where(e >= 0, e, ALPHA * e)
        e = jnp.where(adj > 0, e, NEG_BIG)
        att = jax.nn.softmax(e, axis=1)
        return att @ (h @ fc_w + fc_b)

    def _L3_gnn_ref(x, adj, W):
        import jax, jax.numpy as jnp
        import numpy as np
        N = 8192
        IN_F = 512
        OUT_F = 512
        n = adj.shape[0]
        adj_hat = adj + jnp.eye(n, dtype=adj.dtype)
        degree = adj_hat.sum(axis=1)
        d_inv_sqrt = degree ** (-0.5)
        adj_norm = d_inv_sqrt[:, None] * adj_hat * d_inv_sqrt[None, :]
        return jax.nn.relu(adj_norm @ x @ W)

    x = _layernorm(x + _L0_gnn_ref(x, adj, L0_gnn_Wks, L0_gnn_Wqs, L0_gnn_Wvs, L0_gnn_Wo), axis=-1)
    x = _layernorm(x + _L1_gnn_ref(x, adj, L1_gnn_W1, L1_gnn_b1, L1_gnn_W2, L1_gnn_b2), axis=-1)
    x = _layernorm(x + _L2_gnn_ref(x, adj, L2_gnn_W, L2_gnn_a_w, L2_gnn_a_b, L2_gnn_fc_w, L2_gnn_fc_b), axis=-1)
    x = _layernorm(x + _L3_gnn_ref(x, adj, L3_gnn_W), axis=-1)
    return x


_drawn_inputs = setup_inputs


def setup_inputs(seed=0):
    import zlib

    import numpy as np

    out = dict(_drawn_inputs(seed))
    spreads = {'L1_gnn_b1': (0.0, 0.1), 'L1_gnn_b2': (0.0, 0.1)}
    factors = {}
    for name, (base, spread) in spreads.items():
        noise = np.random.default_rng([zlib.crc32(name.encode()), seed]).standard_normal(out[name].shape)
        drawn = base * np.exp(spread * noise) if base else spread * noise
        out[name] = jnp.asarray(drawn.astype(out[name].dtype))
    for name, factor in factors.items():
        out[name] = (out[name] * factor).astype(out[name].dtype)
    return out
```

```python
import concourse.bass as bass
from concourse import mybir
from contextlib import ExitStack

FP32 = mybir.dt.float32
FP32R = mybir.dt.float32r
FP16 = mybir.dt.float16
BF16 = mybir.dt.bfloat16
ALU = mybir.AluOpType
ACT = mybir.ActivationFunctionType
AXX = mybir.AxisListType.X

P = 128
N = 2708
D = 512
KT = D // P
NT = -(-N // P)
NP = NT * P
BR = 2 * P
NB = NP // BR
H = 8
HD = D // H
PASSES3 = ((0, 0), (0, 1), (1, 0))

V_TOP = 8192.0
P_TOP = 4096.0
MASKED = -1e16


class Scope:

    def __init__(self, nc, stage):
        self.nc, self.stage = nc, stage
        self.stack = ExitStack()

    def __enter__(self):
        return self

    def __exit__(self, *a):
        self.stack.close()

    def sb(self, name, shape, dt):
        return self.stack.enter_context(self.nc.sbuf_tensor(f"{self.stage}_{name}", shape, dt))

    def ps(self, name, shape, dt=FP32):
        return self.stack.enter_context(self.nc.psum_tensor(f"{self.stage}_{name}", shape, dt))

    def sem(self, name):
        return self.stack.enter_context(self.nc.semaphore(f"{self.stage}_{name}"))

    def block(self):
        return self.stack.enter_context(self.nc.Block())



def pairs_of(e, count, step):
    with e.Fori(0, count // 2, 1) as n:
        step(n * 2, 0)
        step(n * 2 + 1, 1)
    if count % 2:
        step(count - 1, 0)


def next_block(v):
    span = NB.bit_length()
    past = (v + ((1 << span) - NB)) >> span
    return v - past * NB if isinstance(v, int) else (v - past * NB).with_bounds(min_val=0, max_val=NB - 1)


def project_qkv(nc, s, xT, wqkv, qk_parts, v_all):
    RING = 4
    M = 2 * KT
    w_raw = s.sb("w_raw", [P, 3, KT, D], FP32)
    w_hi = s.sb("w_hi", [P, 3, KT, D], FP32R)
    w_lo = s.sb("w_lo", [P, 3, KT, D], FP32R)
    x_raw = s.sb("x_raw", [P, 2, KT, BR], FP32)
    x_hi = s.sb("x_hi", [P, 2, KT, BR], FP32R)
    x_lo = s.sb("x_lo", [P, 2, KT, BR], FP32R)
    out_hi = s.sb("out_hi", [P, RING, BR], FP32R)
    out_lo = s.sb("out_lo", [P, RING, BR], FP32R)
    qk_ps = [s.ps(f"qk_ps{i}", [P, D]) for i in range(RING)]
    v_ps = [s.ps(f"v_ps{i}", [P, D]) for i in range(2)]

    w_loaded = s.sem("w_loaded")
    w_hi_ready = s.sem("w_hi_ready")
    w_ready = s.sem("w_ready")
    x_loaded = [s.sem(f"x_loaded{i}") for i in range(2)]
    x_hi_ready = s.sem("x_hi_ready")
    x_ready = s.sem("x_ready")
    qk_done = s.sem("qk_done")
    v_done = s.sem("v_done")
    v_free = s.sem("v_free")
    hi_ready = s.sem("hi_ready")
    lo_ready = s.sem("lo_ready")
    stored = [s.sem(f"stored{i}") for i in range(RING)]
    xT_v = xT.rearrange("(k p) n -> p k n", p=P)
    block = s.block()

    @block.gpsimd
    def _(pool):
        for i in range(3):
            pool.dma_start(w_raw[:, i], wqkv[i].rearrange("(k p) n -> p k n", p=P)).then_inc(w_loaded, 16)

        def step(b, slot):
            pool.wait_ge(x_ready, b + 1)
            pool.dma_start(x_raw[:, slot], xT_v[:, :, bass.ds(b * BR, BR)]).then_inc(x_loaded[slot], 16)

        pairs_of(pool, NB, step)

    @block.sync
    def _(sp):
        def step(b, slot):
            for m in range(M):
                sp.wait_ge(lo_ready, b * M + (m + 1 + RING))
                for part, src in enumerate((out_hi, out_lo)):
                    dst = qk_parts[m // KT, part, (m % KT) * P:(m % KT + 1) * P, bass.ds(b * BR, BR)]
                    sp.dma_start(dst, src[:, m % RING, :].bitcast(FP32)).then_inc(stored[m % RING], 16)

        pairs_of(sp, NB, step)
        for r in range(RING):
            sp.wait_ge(stored[r], 32 * NB * M // RING)

    @block.scalar
    def _(act):
        act.sem_inc(v_free, 2)
        act.wait_ge(w_loaded, 48)
        for i in range(3):
            act.activation(w_hi[:, i], w_raw[:, i], ACT.Copy).then_inc(w_hi_ready, 1)

        def step(b, slot):
            act.wait_ge(x_loaded[slot], (b - slot) * 8 + 16)
            act.wait_ge(v_done, b * 2)
            act.activation(x_hi[:, slot], x_raw[:, slot], ACT.Copy).then_inc(x_hi_ready, 1)
            for m in range(M):
                r = m % RING
                act.wait_ge(qk_done, b * M + (m + 1))
                act.wait_ge(stored[r], b * (32 * M // RING) + 32 * (m // RING))
                act.activation(out_hi[:, r, :], qk_ps[r][:, 0:BR], ACT.Copy).then_inc(hi_ready, 1)
            for t in range(2):
                act.wait_ge(v_done, b * 2 + (t + 3))
                act.activation(v_all[:, bass.ds((b * 2 + t) * D, D)], v_ps[t][:, :], ACT.Copy).then_inc(v_free, 1)

        pairs_of(act, NB, step)

    @block.vector
    def _(dve):
        dve.sem_inc(x_ready, 2)
        dve.sem_inc(lo_ready, RING)
        for i in range(3):
            dve.wait_ge(w_hi_ready, i + 1)
            dve.tensor_tensor(w_lo[:, i], w_raw[:, i], w_hi[:, i], ALU.subtract).then_inc(w_ready, 1)

        def step(b, slot):
            dve.wait_ge(x_hi_ready, b + 1)
            dve.tensor_tensor(x_lo[:, slot], x_raw[:, slot], x_hi[:, slot], ALU.subtract).then_inc(x_ready, 1)
            for m in range(M):
                r = m % RING
                dve.wait_ge(hi_ready, b * M + (m + 1))
                dve.tensor_tensor(out_lo[:, r, :], qk_ps[r][:, 0:BR], out_hi[:, r, :],
                                  ALU.subtract).then_inc(lo_ready, 1)

        pairs_of(dve, NB, step)

    @block.tensor
    def _(pe):
        pe.sem_inc(v_done, 2)
        pe.wait_ge(w_ready, 3)
        xs, ws = (x_hi, x_lo), (w_hi, w_lo)

        def step(b, slot):
            pe.wait_ge(x_ready, b + 3)
            for m in range(M):
                pe.wait_ge(lo_ready, b * M + (m + 1))
                for n, (i, j) in enumerate(PASSES3):
                    for k in range(KT):
                        mm = pe.matmul(qk_ps[m % RING][:, 0:BR],
                                       ws[i][:, m // KT, k, (m % KT) * P:(m % KT + 1) * P],
                                       xs[j][:, slot, k, :], start=(n == 0 and k == 0),
                                       stop=(n == 2 and k == KT - 1))
                mm.then_inc(qk_done, 1)
            for t in range(2):
                pe.wait_ge(v_free, b * 2 + (t + 1))
                for n, (i, j) in enumerate(PASSES3):
                    for k in range(KT):
                        mm = pe.matmul(v_ps[t][:, :], xs[j][:, slot, k, t * P:(t + 1) * P],
                                       ws[i][:, 2, k, :], start=(n == 0 and k == 0),
                                       stop=(n == 2 and k == KT - 1))
                mm.then_inc(v_done, 1)

        pairs_of(pe, NB, step)


def split_values(nc, s, v_all, v_parts, eye, v_inv):
    v_split = s.sb("v_split", [P, NT, H, 2, HD], FP16)
    top = s.sb("top", [P, 1], FP32)
    row = s.sb("row", [1, P], FP32)
    ones = s.sb("ones", [1, P], FP32)
    unit = s.sb("unit", [P, 1], FP32)
    scale = s.sb("scale", [P, 1], FP32)
    t_ps = s.ps("t_ps", [1, P])
    b_ps = s.ps("b_ps", [P, 1])
    step_done = s.sem("step_done")
    t_done = s.sem("t_done")
    b_done = s.sem("b_done")
    hi_ready = s.sem("hi_ready")
    lo_ready = s.sem("lo_ready")
    stored = s.sem("stored")
    v_view = v_all.rearrange("p (t h c) -> p t h c", t=NT, h=H)
    block = s.block()

    @block.vector
    def _(dve):
        dve.memset(ones[:, :], 1.0)
        dve.tensor_reduce(top[:, :], v_all, AXX, ALU.max, apply_absolute_value=True).then_inc(step_done, 1)
        dve.wait_ge(t_done, 1)
        dve.tensor_reduce(row[:, 0:1], t_ps[:, :], AXX, ALU.max).then_inc(step_done, 1)
        dve.wait_ge(b_done, 1)
        dve.tensor_scalar(unit[:, :], b_ps[:, :], 1e-30, 1.0 / V_TOP, ALU.max, ALU.mult).then_inc(step_done, 1)
        dve.wait_ge(step_done, 3)
        dve.tensor_scalar(v_inv, unit[:, :], 1.0 / P_TOP, None, ALU.mult)
        dve.reciprocal(scale[:, :], unit[:, :]).then_inc(step_done, 1)
        dve.wait_ge(step_done, 4)
        for h in range(H):
            dve.wait_ge(hi_ready, h + 1)
            dve.scalar_tensor_tensor(v_split[:, :, h, 1, :], v_view[:, :, h, :], scale[:, :],
                                     v_split[:, :, h, 0, :], ALU.mult, ALU.subtract).then_inc(lo_ready, 1)

    @block.tensor
    def _(pe):
        pe.wait_ge(step_done, 1)
        pe.transpose(t_ps[:, :], top[:, :], eye[:, :]).then_inc(t_done, 1)
        pe.wait_ge(step_done, 2)
        pe.matmul(b_ps[:, :], ones[:, :], row[:, 0:1], start=True, stop=True).then_inc(b_done, 1)

    @block.scalar
    def _(act):
        act.wait_ge(step_done, 4)
        for h in range(H):
            act.activation(v_split[:, :, h, 0, :], v_view[:, :, h, :], ACT.Copy,
                           scale=scale[:, :]).then_inc(hi_ready, 1)

    @block.sync
    def _(sp):
        for h in range(H):
            sp.wait_ge(lo_ready, h + 1)
            sp.dma_start(v_parts[h].rearrange("p (t c) -> p t c", t=NT),
                         v_split[:, :, h].rearrange("p t a c -> p t (a c)")).then_inc(stored, 16)
        sp.wait_ge(stored, 16 * H)


PAIR = 1024
PIECES = [(c, min(PAIR, N - c)) for c in range(0, N, PAIR)]
EXPS = [(0, 5 * BR + 74), (5 * BR + 74, N - 5 * BR - 74)]
GROUPS = NT // 2
ORDER = ["T0", "S0", "T1", "S1", "O", "T2", "V0", "T3", "S2", "V1", "T4", "S3", "V2", "T5", "V3", "T6", "S4",
         "V4", "T7", "S5", "V5", "T8", "V6", "T9", "V7", "T10", "V8", "V9", "V10"]


def attention(nc, s, adj, qk_parts, v_parts, o_rows, eye, fold, v_inv):
    S_RING, T_RING = 2, 3
    keys = s.sb("keys", [P, H, N], FP32R)
    mask = [s.sb(f"mask{t}", [P, N], BF16) for t in range(2)]
    adj_rows = [s.sb(f"adj_rows{t}", [P, NP], FP32) for t in range(2)]
    probs = [[s.sb(f"probs{i}{t}", [P, NP], FP32) for t in range(2)] for i in range(2)]
    vals = s.sb("vals", [P, 2, NT, P], FP16)
    q_st = s.sb("q_st", [P, 2, 2, BR], FP32R)
    pt_hi = s.sb("pt_hi", [P, T_RING, 2 * BR], FP16)
    pt_lo = s.sb("pt_lo", [P, T_RING, 2 * BR], FP16)
    top = s.sb("top", [P, 2, 2, 3], FP32)
    sums = s.sb("sums", [P, 2, 2, 2], FP32)
    r_sum = s.sb("r_sum", [P, 2, 2], FP32)
    r_inv = s.sb("r_inv", [P, 2, 2], FP32)
    acc_sb = s.sb("acc_sb", [P, 2, BR], FP32)
    o_sb = s.sb("o_sb", [P, 2, D], FP32)
    s_ps = [s.ps(f"s_ps{i}", [P, PAIR]) for i in range(S_RING)]
    t_ps = [s.ps(f"t_ps{i}", [P, 2 * BR]) for i in range(T_RING)]
    acc_ps = s.ps("acc_ps", [P, D])

    keys_loaded = [s.sem(f"keys_loaded{h}") for h in range(H)]
    adj_loaded = [s.sem(f"adj_loaded{t}") for t in range(2)]
    adj_fixed = s.sem("adj_fixed")
    mask_ready = s.sem("mask_ready")
    q_loaded = [s.sem(f"q_loaded{i}") for i in range(2)]
    v_loaded = [s.sem(f"v_loaded{i}") for i in range(2)]
    scored = s.sem("scored")
    masked = s.sem("masked")
    weighed = s.sem("weighed")
    turned = s.sem("turned")
    hi_ready = s.sem("hi_ready")
    drained = s.sem("drained")
    used = s.sem("used")
    acc_copied = s.sem("acc_copied")
    folded = s.sem("folded")
    r_done = s.sem("r_done")
    o_stored = s.sem("o_stored")
    padded = s.sem("padded")
    block = s.block()
    SP_, GP = 2 * len(PIECES), GROUPS
    TP = GROUPS + 1

    def stages(e, stage):
        with e.Fori(0, NB, 1) as b:
            for h in range(H):
                stage(b, h)

    @block.sync
    def _(sp):
        def load_q(row0, h, slot):
            for a in range(2):
                for part in range(2):
                    half = part ^ a
                    sp.dma_start(q_st[half * HD:(half + 1) * HD, slot, a, :].bitcast(FP32),
                                 qk_parts[0, part, h * HD:(h + 1) * HD, bass.ds(row0, BR)])\
                      .then_inc(q_loaded[slot], 16)

        def load_keys(h):
            for part in range(2):
                sp.dma_start(keys[part * HD:(part + 1) * HD, h, :].bitcast(FP32),
                             qk_parts[1, part, h * HD:(h + 1) * HD, 0:N]).then_inc(keys_loaded[h], 16)

        def load_v(h, slot):
            sp.dma_start(vals[:, slot], v_parts[h].rearrange("p (t c) -> p t c", t=NT)).then_inc(v_loaded[slot], 16)

        load_q(0, 0, 0)
        load_keys(0)
        load_q(0, 1, 1)
        load_keys(1)
        load_v(0, 0)
        load_v(1, 1)
        for h in range(2, H):
            load_keys(h)

        def stage(b, h):
            sp.wait_ge(scored, b * (H * SP_) + (h + 1) * SP_)
            nxt = b * BR if h + 2 < H else next_block(b + 1) * BR
            load_q(nxt, (h + 2) % H, h % 2)
            if h == 0:
                sp.wait_ge(drained, b * (H * TP) + 3 + T_RING)
                sp.dma_start(o_rows[bass.ds(b * BR, BR), :].rearrange("(t p) c -> p t c", p=P),
                             o_sb[:, :, :]).then_inc(o_stored, 16)
            sp.wait_ge(used, b * (H * GP) + (h + 1) * GP + T_RING)
            load_v((h + 2) % H, h % 2)

        stages(sp, stage)
        sp.wait_ge(drained, NB * H * TP + 1 + T_RING)
        sp.dma_start(o_rows[NB * BR:(NB + 1) * BR, :].rearrange("(t p) c -> p t c", p=P),
                     o_sb[:, :, :]).then_inc(o_stored, 16)
        sp.wait_ge(o_stored, 16 * (NB + 1))
        for i in range(2):
            sp.wait_ge(q_loaded[i], 64 * (1 + NB * H // 2))
            sp.wait_ge(v_loaded[i], 16 * (1 + NB * H // 2))

    @block.gpsimd
    def _(pool):
        def load_adj(row0, t):
            pool.dma_start(adj_rows[t][:, 0:N], adj[bass.ds(row0 + t * P, P), 0:N]).then_inc(adj_loaded[t], 16)

        def make_mask(b, t, first=False):
            pool.wait_ge(adj_fixed, b * 2 + (t + 1))
            if not first:
                pool.wait_ge(masked, b * (H * SP_) - (1 - t) * len(PIECES) + S_RING)
            pool.nop(nofuse=True)
            pool.tensor_scalar(mask[t][:, :], adj_rows[t][:, 0:N], -MASKED, MASKED, ALU.mult, ALU.add)\
                .then_inc(mask_ready, 1)

        for t in range(2):
            pool.memset(adj_rows[t][:, N:NP], 0.0).then_inc(padded, 1)
            for i in range(2):
                pool.memset(probs[i][t][:, N:NP], 0.0).then_inc(padded, 1)
        pool.memset(acc_sb[:, 1, :], 0.0).then_inc(padded, 1)
        pool.memset(sums[:, 1], 1.0).then_inc(padded, 1)
        pool.memset(o_sb[:, :, :], 0.0).then_inc(padded, 1)
        pool.wait_ge(padded, 9)
        for t in range(2):
            load_adj(0, t)
        for t in range(2):
            make_mask(0, t, first=True)
        with pool.Fori(0, NB, 1) as b:
            nxt = next_block(b + 1) * BR
            for t in range(2):
                pool.wait_ge(mask_ready, b * 2 + (t + 1))
                load_adj(nxt, t)
            for t in range(2):
                make_mask(b + 1, t)

    @block.tensor
    def _(pe):
        pe.sem_inc(used, T_RING)

        def scores(base, n_in_block, h, slot, i):
            t, (c0, width) = i // len(PIECES), PIECES[i % len(PIECES)]
            pe.wait_ge(masked, base * (H * SP_) + n_in_block * SP_ + (i + 1))
            for c in range(c0, c0 + width, 512):
                w = min(512, c0 + width - c)
                for a in range(2):
                    mm = pe.matmul(s_ps[i % S_RING][:, c - c0:c - c0 + w], q_st[:, slot, a, t * P:(t + 1) * P],
                                   keys[:, h, c:c + w], start=(a == 0), stop=(a == 1))
            mm.then_inc(scored, 1)

        def fold_heads(b, n_in_block):
            pe.wait_ge(acc_copied, b * H + n_in_block)
            pe.wait_ge(drained, b * (H * TP) + n_in_block * TP + 3)
            for t in range(2):
                mm = pe.matmul(t_ps[2][:, t * HD:(t + 1) * HD], acc_sb[:, (n_in_block + 1) % 2, t * P:(t + 1) * P],
                               fold, start=True, stop=True)
            mm.then_inc(folded, 1)

        pe.wait_ge(q_loaded[0], 64)
        pe.wait_ge(keys_loaded[0], 32)
        for i in range(SP_):
            scores(0, 0, 0, 0, i)

        def stage(b, h):
            cur, nxt = h % 2, (h + 1) % 2
            for what in ORDER:
                kind, i = what[0], int(what[1:] or 0)
                ring = i if i < 2 else i + 1
                if kind == "S":
                    if i == 0:
                        pe.wait_ge(q_loaded[nxt], b * (64 * H // 2) + 64 * ((h + 1) // 2 + 1))
                        pe.wait_ge(keys_loaded[(h + 1) % H], 32)
                    scores(b, h + 1, (h + 1) % H, nxt, i)
                elif kind == "T":
                    late = (i + 1) * BR > EXPS[0][1]
                    pe.wait_ge(weighed, b * (4 * H) + 4 * h + (4 if late else 3))
                    pe.wait_ge(drained, b * (H * TP) + h * TP + (ring + 1))
                    for j in range(2):
                        for t in range(2):
                            mm = pe.transpose(t_ps[ring % T_RING][:, j * BR + t * P:j * BR + (t + 1) * P],
                                              probs[cur][t][:, (2 * i + j) * P:(2 * i + j + 1) * P], eye)
                    mm.then_inc(turned, 1)
                elif kind == "V":
                    if i == 0:
                        pe.wait_ge(v_loaded[cur], b * (16 * H // 2) + 16 * (h // 2 + 1))
                        pe.wait_ge(acc_copied, b * H + h)
                    pe.wait_ge(drained, b * (H * TP) + h * TP + (ring + 1) + T_RING)
                    for j in range(2):
                        for part in (pt_hi, pt_lo):
                            mm = pe.matmul(acc_ps[:, 0:BR], vals[:, cur, 2 * i + j, :],
                                           part[:, i % T_RING, j * BR:(j + 1) * BR],
                                           start=(i == 0 and j == 0 and part is pt_hi),
                                           stop=(i == GROUPS - 1 and j == 1 and part is pt_lo))
                    mm.then_inc(used, 1)
                else:
                    fold_heads(b, h)

        stages(pe, stage)
        fold_heads(NB, 0)

    @block.scalar
    def _(act):
        def exps(b, n_in_block, i):
            cur, t, e = n_in_block % 2, i // 2, i % 2
            act.wait_ge(masked, b * (H * SP_) + n_in_block * SP_ + (t + 1) * len(PIECES) + S_RING)
            c, w = EXPS[e]
            cols = probs[cur][t][:, c:c + w]
            act.activation(cols, cols, ACT.Exp, bias=top[:, cur, t, 2:3], scale=-1.0,
                           accum_out=sums[:, cur, t, e:e + 1]).then_inc(weighed, 1)

        def high_part(b, h, i):
            ring = i if i < 2 else i + 1
            act.wait_ge(turned, b * (H * GP) + h * GP + (i + 1))
            act.wait_ge(used, b * (H * GP) + h * GP + (i + 1))
            act.activation(pt_hi[:, i % T_RING, :], t_ps[ring % T_RING][:, :], ACT.Copy, scale=P_TOP)\
                .then_inc(hi_ready, 1)

        def copy_acc(b, n_in_block):
            act.wait_ge(used, b * (H * GP) + n_in_block * GP + T_RING)
            act.activation(acc_sb[:, (n_in_block + 1) % 2, :], acc_ps[:, 0:BR], ACT.Copy).then_inc(acc_copied, 1)

        act.wait_ge(padded, 9)
        for i in range(4):
            exps(0, 0, i)

        def stage(b, h):
            for i in range(GROUPS):
                high_part(b, h, i)
                if i in (3, 4, 7, 8):
                    exps(b, h + 1, (3, 4, 7, 8).index(i))
            copy_acc(b, h + 1)

        stages(act, stage)

    @block.vector
    def _(dve):
        dve.wait_ge(padded, 9)
        dve.sem_inc(masked, S_RING)
        dve.sem_inc(drained, T_RING)

        def set_diagonal(b, row0):
            for t in range(2):
                dve.wait_ge(adj_loaded[t], b * 16 + 16)
                diag = adj_rows[t][:, bass.ds(row0 + t * P, P)]
                dve.tensor_tensor(diag, diag, eye, ALU.max).then_inc(adj_fixed, 1)

        def mask_scores(b, n_in_block, i):
            cur, t, k = n_in_block % 2, i // len(PIECES), i % len(PIECES)
            c, w = PIECES[k]
            dve.wait_ge(scored, b * (H * SP_) + n_in_block * SP_ + (i + 1))
            if n_in_block in (0, H) and k == 0:
                at_block = b if n_in_block == 0 else b + 1
                dve.wait_ge(mask_ready, at_block * 2 + (t + 1))
            if k > 0:
                dve.wait_ge(masked, b * (H * SP_) + n_in_block * SP_ + i + S_RING)
            dve.nop(nofuse=True)
            dve.tensor_tensor_reduce(out=probs[cur][t][:, c:c + w], in0=s_ps[i % S_RING][:, 0:w],
                                     in1=mask[t][:, c:c + w], scale=-(HD ** -0.5),
                                     scalar=3e38 if k == 0 else top[:, cur, t, k - 1:k],
                                     op0=ALU.add, op1=ALU.min, accum_out=top[:, cur, t, k:k + 1])\
                .then_inc(masked, 1)

        def low_part(b, h, i):
            ring = i if i < 2 else i + 1
            dve.wait_ge(hi_ready, b * (H * GP) + h * GP + (i + 1))
            dve.scalar_tensor_tensor(pt_lo[:, i % T_RING, :], t_ps[ring % T_RING][:, :], P_TOP,
                                     pt_hi[:, i % T_RING, :], ALU.mult, ALU.subtract).then_inc(drained, 1)

        def norm(b, n_in_block):
            h, slot = (n_in_block + H - 1) % H, (n_in_block + 1) % 2
            dve.tensor_tensor(r_sum[:, slot, :], sums[:, slot, :, 0], sums[:, slot, :, 1], ALU.add).then_inc(r_done, 1)
            dve.wait_ge(r_done, b * (2 * H) + n_in_block * 2 + 1)
            dve.reciprocal(r_inv[:, slot, :], r_sum[:, slot, :]).then_inc(r_done, 1)
            dve.wait_ge(r_done, b * (2 * H) + n_in_block * 2 + 2)
            dve.wait_ge(folded, b * H + (n_in_block + 1))
            if h == 0:
                dve.wait_ge(o_stored, b * 16 + 16)
            dve.scalar_tensor_tensor(o_sb[:, :, h * HD:(h + 1) * HD],
                                     t_ps[2][:, 0:2 * HD].rearrange("p (t c) -> p t c", t=2), v_inv,
                                     r_inv[:, slot, :].unsqueeze(2).broadcast_to([P, 2, HD]), ALU.mult, ALU.mult)\
                .then_inc(drained, 1)

        set_diagonal(0, 0)
        for i in range(SP_):
            mask_scores(0, 0, i)

        def stage(b, h):
            for what in ORDER:
                kind, i = what[0], int(what[1:] or 0)
                if kind == "S":
                    mask_scores(b, h + 1, i)
                elif kind == "T":
                    low_part(b, h, i)
                elif kind == "O":
                    norm(b, h)
            if h == H // 2:
                set_diagonal(b + 1, next_block(b + 1) * BR)

        stages(dve, stage)
        norm(NB, 0)


EPS = 1e-5
X_TOP = 256.0
NORM_STEPS = 5


def layer_norm(dve, z, stats, mean_var, rstd, out, chain, at):
    dve.bn_stats(stats, z).then_inc(chain, 1)
    dve.wait_ge(chain, at + 1)
    dve.nop(nofuse=True)
    dve.bn_aggr(mean_var, stats).then_inc(chain, 1)
    dve.wait_ge(chain, at + 4)
    dve.tensor_scalar(out, z, mean_var[:, 0:1], rstd, ALU.subtract, ALU.mult).then_inc(chain, 1)


def inv_std(pool, mean_var, rstd, eps_half, chain, at):
    pool.wait_ge(chain, at + 2)
    pool.tensor_tensor(mean_var[:, 1:2], mean_var[:, 1:2], eps_half[:, 0:1], ALU.add).then_inc(chain, 1)
    pool.wait_ge(chain, at + 3)
    pool.tensor_tensor(rstd, mean_var[:, 1:2], eps_half[:, 1:2], ALU.pow).then_inc(chain, 1)


def project_out(nc, s, x_in, o_rows, wo, x_rows, adjT, a_t, eye, eps_half):
    w_sb = s.sb("w_sb", [P, KT, D], FP32)
    o_sb = s.sb("o_sb", [P, 2, D], FP32)
    oT_sb = s.sb("oT_sb", [P, 2, D], FP32)
    xr_sb = s.sb("xr_sb", [P, 2, D], FP32)
    z_sb = s.sb("z_sb", [P, 2, D], FP32)
    xn_sb = s.sb("xn_sb", [P, 2, D], FP32)
    stats = s.sb("stats", [P, 2, 6], FP32)
    mean_var = s.sb("mean_var", [P, 2, 2], FP32)
    rstd = s.sb("rstd", [P, 2, 1], FP32)
    t_ps = [s.ps(f"t_ps{i}", [P, D]) for i in range(2)]
    y_ps = [s.ps(f"y_ps{i}", [P, D]) for i in range(2)]
    w_loaded = s.sem("w_loaded")
    o_loaded = [s.sem(f"o_loaded{i}") for i in range(2)]
    x_loaded = [s.sem(f"x_loaded{i}") for i in range(2)]
    a_loaded = s.sem("a_loaded")
    turned = s.sem("turned")
    copied = s.sem("copied")
    multiplied = s.sem("multiplied")
    added = s.sem("added")
    normed = s.sem("normed")
    stored = [s.sem(f"stored{i}") for i in range(2)]
    block = s.block()

    @block.gpsimd
    def _(pool):
        for j in range(NT):
            pool.dma_start(a_t[:, j, :], adjT[j * P:(j + 1) * P, :]).then_inc(a_loaded, 16)

        def step(t, slot):
            inv_std(pool, mean_var[:, slot, :], rstd[:, slot, :], eps_half, normed, t * NORM_STEPS)

        pairs_of(pool, NT, step)
        pool.wait_ge(a_loaded, 16 * NT)

    @block.sync
    def _(sp):
        sp.dma_start(w_sb[:, :, :], wo.rearrange("(k p) n -> p k n", p=P)).then_inc(w_loaded, 16)

        def load(t, slot):
            sp.dma_start(o_sb[:, slot, :], o_rows[bass.ds(t * P + BR, P), :]).then_inc(o_loaded[slot], 16)
            sp.dma_start(xr_sb[:, slot, :], x_in[bass.ds(t * P, P), :]).then_inc(x_loaded[slot], 16)

        def step(t, slot, last=False):
            sp.wait_ge(normed, t * NORM_STEPS + NORM_STEPS)
            sp.dma_start(x_rows[bass.ds(t * P, P), :], xn_sb[:, slot, :]).then_inc(stored[slot], 16)
            if not last:
                load(t + 2, slot)

        load(0, 0)
        load(1, 1)
        pairs_of(sp, NT - 2, step)
        step(NT - 2, 0, last=True)
        step(NT - 1, 1, last=True)
        for i in range(2):
            sp.wait_ge(stored[i], 16 * NT // 2)

    @block.scalar
    def _(act):
        act.sem_inc(copied, 2)

        def step(t, slot):
            act.wait_ge(turned, t + 3)
            act.wait_ge(multiplied, t + 1)
            act.activation(oT_sb[:, slot, :], t_ps[slot][:, :], ACT.Copy).then_inc(copied, 1)

        pairs_of(act, NT, step)

    @block.tensor
    def _(pe):
        pe.sem_inc(turned, 2)
        pe.sem_inc(multiplied, 2)
        pe.wait_ge(w_loaded, 16)

        def turn(t, slot):
            pe.wait_ge(o_loaded[slot], (t - slot) * 8 + 16)
            pe.wait_ge(copied, t + 1)
            for k in range(KT):
                mm = pe.transpose(t_ps[slot][:, k * P:(k + 1) * P], o_sb[:, slot, k * P:(k + 1) * P], eye)
            mm.then_inc(turned, 1)

        def step(t, slot, last=False):
            if not last:
                turn(t + 1, 1 - slot)
            pe.wait_ge(copied, t + 3)
            pe.wait_ge(added, t + 1)
            for k in range(KT):
                mm = pe.matmul(y_ps[slot][:, :], oT_sb[:, slot, k * P:(k + 1) * P], w_sb[:, k, :],
                               start=(k == 0), stop=(k == KT - 1))
            mm.then_inc(multiplied, 1)

        turn(0, 0)
        pairs_of(pe, NT - 2, step)
        step(NT - 2, 0)
        step(NT - 1, 1, last=True)

    @block.vector
    def _(dve):
        dve.sem_inc(added, 2)

        def step(t, slot):
            dve.wait_ge(multiplied, t + 3)
            dve.wait_ge(x_loaded[slot], (t - slot) * 8 + 16)
            dve.tensor_tensor(z_sb[:, slot, :], y_ps[slot][:, :], xr_sb[:, slot, :], ALU.add).then_inc(added, 1)
            dve.wait_ge(added, t + 3)
            dve.wait_ge(stored[slot], (t - slot) * 8)
            layer_norm(dve, z_sb[:, slot, :], stats[:, slot, :], mean_var[:, slot, :], rstd[:, slot, :],
                       xn_sb[:, slot, :], normed, t * NORM_STEPS)

        pairs_of(dve, NT, step)


def degrees(nc, s, a_t, eye_bf, r, r_out, eps_half):
    ones = s.sb("ones", [P, 1], BF16)
    deg = s.sb("deg", [P, NT], FP32)
    pos = s.sb("pos", [P, NT], FP32)
    inv = s.sb("inv", [P, NT], FP32)
    deg_ps = s.ps("deg_ps", [P, D])
    eyed = s.sem("eyed")
    summed = s.sem("summed")
    done = s.sem("done")
    block = s.block()

    @block.vector
    def _(dve):
        dve.memset(ones[:, :], 1.0).then_inc(eyed, 1)
        for j in range(NT):
            diag = a_t[:, j, j * P:(j + 1) * P]
            dve.tensor_tensor(diag, diag, eye_bf, ALU.add).then_inc(eyed, 1)
        dve.wait_ge(summed, NT)
        dve.tensor_scalar(pos[:, :], deg_ps[:, 0:NT], 0.0, None, ALU.is_gt).then_inc(done, 1)
        dve.tensor_scalar(deg[:, :], deg_ps[:, 0:NT], 1e-30, None, ALU.max).then_inc(done, 1)
        dve.wait_ge(done, 3)
        dve.tensor_tensor(r, inv[:, :], pos[:, :], ALU.mult).then_inc(done, 1)
        dve.wait_ge(done, 4)
        dve.tensor_scalar(r_out, r, 1.0 / X_TOP, None, ALU.mult)

    @block.gpsimd
    def _(pool):
        pool.wait_ge(done, 2)
        pool.tensor_tensor(inv[:, :], deg[:, :], eps_half[:, 1:2].broadcast_to([P, NT]), ALU.pow).then_inc(done, 1)

    @block.tensor
    def _(pe):
        pe.wait_ge(eyed, NT + 1)
        with pe.Fori(0, NT, 1) as t:
            for j in range(NT):
                mm = pe.matmul(deg_ps[:, bass.ds(t, 1)], a_t[:, j, bass.ds(t * P, P)], ones[:, :],
                               start=(j == 0), stop=(j == NT - 1))
            mm.then_inc(summed, 1)


def hidden_rows(nc, s, x_rows, w1T, b1, r, g_parts, r_parts, eye):
    HID = w1T.shape[1]
    w_sb = s.sb("w_sb", [P, KT, HID], FP32)
    b1_all = s.sb("b1_all", [P, HID], FP32)
    x_sb = s.sb("x_sb", [P, 2, D], FP32)
    xT_sb = s.sb("xT_sb", [P, 2, D], FP32)
    h_sb = s.sb("h_sb", [P, 2, HID], FP32)
    g_sb = s.sb("g_sb", [P, 2, HID], FP32)
    rest = s.sb("rest", [P, 2, HID], FP32)
    r_rest = s.sb("r_rest", [P, NT], FP32)
    t_ps = [s.ps(f"t_ps{i}", [P, D]) for i in range(2)]
    h_ps = [s.ps(f"h_ps{i}", [P, D]) for i in range(2)]
    w_loaded = s.sem("w_loaded")
    x_loaded = [s.sem(f"x_loaded{i}") for i in range(2)]
    turned = s.sem("turned")
    copied = s.sem("copied")
    multiplied = s.sem("multiplied")
    biased = s.sem("biased")
    chain = s.sem("chain")
    high = s.sem("high")
    middle = s.sem("middle")
    r_chain = s.sem("r_chain")
    block = s.block()

    @block.sync
    def _(sp):
        sp.dma_start(w_sb[:, :, :], w1T.rearrange("(k p) n -> p k n", p=P)).then_inc(w_loaded, 16)
        sp.dma_start(b1_all[:, :], b1.partition_broadcast(P)).then_inc(w_loaded, 16)

        def step(t, slot):
            sp.wait_ge(turned, t + 1)
            sp.dma_start(x_sb[:, slot, :], x_rows[bass.ds(t * P, P), :]).then_inc(x_loaded[slot], 16)

        pairs_of(sp, NT, step)

    @block.tensor
    def _(pe):
        pe.sem_inc(turned, 2)
        pe.sem_inc(multiplied, 2)
        pe.wait_ge(w_loaded, 32)

        def turn(t, slot):
            pe.wait_ge(x_loaded[slot], (t - slot) * 8 + 16)
            pe.wait_ge(copied, t + 1)
            for k in range(KT):
                mm = pe.transpose(t_ps[slot][:, k * P:(k + 1) * P], x_sb[:, slot, k * P:(k + 1) * P], eye)
            mm.then_inc(turned, 1)

        def step(t, slot, last=False):
            if not last:
                turn(t + 1, 1 - slot)
            pe.wait_ge(copied, t + 3)
            pe.wait_ge(biased, t + 1)
            for k in range(KT):
                mm = pe.matmul(h_ps[slot][:, 0:HID], xT_sb[:, slot, k * P:(k + 1) * P], w_sb[:, k, :],
                               start=(k == 0), stop=(k == KT - 1))
            mm.then_inc(multiplied, 1)

        turn(0, 0)
        pairs_of(pe, NT - 2, step)
        step(NT - 2, 0)
        step(NT - 1, 1, last=True)

    @block.scalar
    def _(act):
        act.sem_inc(copied, 2)

        def copy(t, slot):
            act.wait_ge(turned, t + 3)
            act.wait_ge(multiplied, t + 1)
            act.activation(xT_sb[:, slot, :], t_ps[slot][:, :], ACT.Copy).then_inc(copied, 1)

        def step(t, slot, last=False):
            if not last:
                copy(t + 1, 1 - slot)
            act.wait_ge(chain, t * 3 + 1)
            act.activation(g_parts[:, bass.ds(t, 1), 0, :], g_sb[:, slot, :], ACT.Copy).then_inc(high, 1)
            act.wait_ge(chain, t * 3 + 2)
            act.activation(g_parts[:, bass.ds(t, 1), 1, :], rest[:, slot, :], ACT.Copy).then_inc(middle, 1)

        copy(0, 0)
        pairs_of(act, NT - 2, step)
        step(NT - 2, 0)
        step(NT - 1, 1, last=True)

    @block.vector
    def _(dve):
        dve.sem_inc(biased, 2)
        dve.tensor_copy(r_parts[:, :, 0], r).then_inc(r_chain, 1)
        dve.wait_ge(r_chain, 1)
        dve.tensor_tensor(r_rest[:, :], r, r_parts[:, :, 0], ALU.subtract).then_inc(r_chain, 1)
        dve.wait_ge(r_chain, 2)
        dve.tensor_copy(r_parts[:, :, 1], r_rest[:, :]).then_inc(r_chain, 1)
        dve.wait_ge(r_chain, 3)
        dve.tensor_tensor(r_parts[:, :, 2], r_rest[:, :], r_parts[:, :, 1], ALU.subtract).then_inc(r_chain, 1)

        def step(t, slot):
            dve.wait_ge(multiplied, t + 3)
            dve.tensor_tensor(h_sb[:, slot, :], h_ps[slot][:, 0:HID], b1_all[:, :], ALU.add).then_inc(biased, 1)
            dve.wait_ge(biased, t + 3)
            dve.tensor_scalar(g_sb[:, slot, :], h_sb[:, slot, :], r[:, bass.ds(t, 1)], None, ALU.mult)\
               .then_inc(chain, 1)
            dve.wait_ge(high, t + 1)
            dve.tensor_tensor(rest[:, slot, :], g_sb[:, slot, :], g_parts[:, bass.ds(t, 1), 0, :].squeeze(1),
                              ALU.subtract).then_inc(chain, 1)
            dve.wait_ge(middle, t + 1)
            dve.tensor_tensor(g_parts[:, bass.ds(t, 1), 2, :].squeeze(1), rest[:, slot, :],
                              g_parts[:, bass.ds(t, 1), 1, :].squeeze(1), ALU.subtract).then_inc(chain, 1)

        pairs_of(dve, NT, step)


def aggregate(nc, s, kind, a_t, parts, w_in, b_in, x_rows, out_rows, r, r_parts, eps_half):
    n_parts, width = parts.shape[2], parts.shape[3]
    KC = width // P
    BANKS = KC // 2
    linear = kind == "linear"
    w_sb = s.sb("w_sb", [P, KC, D], FP32)
    agg_sb = s.sb("agg_sb", [P, 2, KC, BR], FP32)
    x_sb = s.sb("x_sb", [P, 2, D], FP32)
    z_sb = s.sb("z_sb", [P, 2, D], FP32)
    y_sb = s.sb("y_sb", [P, 2, D], FP32)
    xn_sb = s.sb("xn_sb", [P, 2, D], FP32)
    stats = s.sb("stats", [P, 2, 6], FP32)
    mean_var = s.sb("mean_var", [P, 2, 2], FP32)
    rstd = s.sb("rstd", [P, 2, 1], FP32)
    agg_ps = [[s.ps(f"agg_ps{i}{j}", [P, D]) for j in range(BANKS)] for i in range(2)]
    y_ps = [s.ps(f"y_ps{i}", [P, D]) for i in range(2)]
    w_loaded = s.sem("w_loaded")
    x_loaded = [s.sem(f"x_loaded{i}") for i in range(2)]
    gathered = s.sem("gathered")
    copied = s.sem("copied")
    multiplied = s.sem("multiplied")
    taken = s.sem("taken")
    added = s.sem("added")
    normed = s.sem("normed")
    stored = [s.sem(f"stored{i}") for i in range(2)]
    if linear:
        b_all = s.sb("b_all", [P, D], FP32)
        rho3 = s.sb("rho3", [P, NT, 3], FP32)
        rho = s.sb("rho", [P, NT], FP32)
        rho_ps = s.ps("rho_ps", [P, D])
        rho_done = s.sem("rho_done")
        rho_chain = s.sem("rho_chain")
    block = s.block()

    @block.sync
    def _(sp):
        sp.dma_start(w_sb[:, :, :], w_in.rearrange("(k p) n -> p k n", p=P)).then_inc(w_loaded, 16)
        if linear:
            sp.dma_start(b_all[:, :], b_in.partition_broadcast(P)).then_inc(w_loaded, 16)

        def load(b, t):
            sp.dma_start(x_sb[:, t, :], x_rows[bass.ds(b * BR + t * P, P), :]).then_inc(x_loaded[t], 16)

        def step(b, last=False):
            for t in range(2):
                sp.wait_ge(normed, b * (2 * NORM_STEPS) + (t + 1) * NORM_STEPS)
                sp.dma_start(out_rows[bass.ds(b * BR + t * P, P), :], xn_sb[:, t, :]).then_inc(stored[t], 16)
                if not last:
                    load(b + 1, t)

        for t in range(2):
            load(0, t)
        with sp.Fori(0, NB - 1, 1) as b:
            step(b)
        step(NB - 1, last=True)
        for t in range(2):
            sp.wait_ge(stored[t], 16 * NB)

    @block.gpsimd
    def _(pool):
        with pool.Fori(0, NB, 1) as b:
            for t in range(2):
                inv_std(pool, mean_var[:, t, :], rstd[:, t, :], eps_half, normed, b * (2 * NORM_STEPS) + t * NORM_STEPS)

    @block.tensor
    def _(pe):
        pe.sem_inc(multiplied, 2)
        if linear:
            with pe.Fori(0, NT, 1) as t:
                for j in range(NT):
                    mm = pe.matmul(rho_ps[:, bass.ds(t * 3, 3)], a_t[:, j, bass.ds(t * P, P)], r_parts[:, j, :],
                                   start=(j == 0), stop=(j == NT - 1))
                mm.then_inc(rho_done, 1)
        pe.wait_ge(w_loaded, 32 if linear else 16)

        def gather(b, slot):
            for c in range(KC):
                if c % 2 == 0:
                    pe.wait_ge(copied, b * BANKS + (c // 2 + 1))
                for j in range(NT):
                    for i in range(n_parts):
                        mm = pe.matmul(agg_ps[slot][c // 2][:, (c % 2) * BR:(c % 2 + 1) * BR],
                                       parts[:, j, i, c * P:(c + 1) * P], a_t[:, j, bass.ds(b * BR, BR)],
                                       start=(j == 0 and i == 0), stop=(j == NT - 1 and i == n_parts - 1))
                if c % 2 == 1:
                    mm.then_inc(gathered, 1)

        def step(b, slot, last=False):
            if not last:
                gather(b + 1, 1 - slot)
            pe.wait_ge(copied, b * BANKS + 3 * BANKS)
            for t in range(2):
                pe.wait_ge(taken, b * 2 + (t + 1))
                for k in range(KC):
                    mm = pe.matmul(y_ps[t][:, :], agg_sb[:, slot, k, t * P:(t + 1) * P], w_sb[:, k, :],
                                   start=(k == 0), stop=(k == KC - 1))
                mm.then_inc(multiplied, 1)

        gather(0, 0)
        pairs_of(pe, NB - 1, step)
        step(NB - 1, 0, last=True)

    @block.scalar
    def _(act):
        act.sem_inc(copied, 2 * BANKS)
        if not linear:
            act.sem_inc(taken, 2)

        def copy(b, slot):
            for i in range(BANKS):
                act.wait_ge(gathered, b * BANKS + (i + 1))
                act.wait_ge(multiplied, b * 2)
                act.activation(agg_sb[:, slot, 2 * i:2 * i + 2, :].rearrange("p k n -> p (k n)"),
                               agg_ps[slot][i][:, :], ACT.Copy).then_inc(copied, 1)

        def step(b, slot, last=False):
            if not last:
                copy(b + 1, 1 - slot)
            if not linear:
                for t in range(2):
                    act.wait_ge(multiplied, b * 2 + (t + 3))
                    act.wait_ge(added, b * 2 + (t + 1))
                    act.activation(y_sb[:, t, :], y_ps[t][:, :], ACT.Relu,
                                   scale=r[:, bass.ds(b * 2 + t, 1)]).then_inc(taken, 1)

        copy(0, 0)
        pairs_of(act, NB - 1, step)
        step(NB - 1, 0, last=True)

    @block.vector
    def _(dve):
        dve.sem_inc(added, 2)
        if linear:
            dve.sem_inc(taken, 2)
            dve.wait_ge(rho_done, NT)
            dve.tensor_copy(rho3[:, :, :].rearrange("p t i -> p (t i)"), rho_ps[:, 0:3 * NT]).then_inc(rho_chain, 1)
            dve.wait_ge(rho_chain, 1)
            dve.tensor_reduce(rho[:, :], rho3[:, :, :], AXX, ALU.add).then_inc(rho_chain, 1)
            dve.wait_ge(rho_chain, 2)
            dve.tensor_tensor(rho[:, :], rho[:, :], r, ALU.mult).then_inc(rho_chain, 1)
            dve.wait_ge(rho_chain, 3)

        with dve.Fori(0, NB, 1) as b:
            for t in range(2):
                dve.wait_ge(x_loaded[t], b * 16 + 16)
                if linear:
                    dve.wait_ge(multiplied, b * 2 + (t + 3))
                    dve.scalar_tensor_tensor(y_sb[:, t, :], y_ps[t][:, :], r[:, bass.ds(b * 2 + t, 1)], x_sb[:, t, :],
                                             ALU.mult, ALU.add).then_inc(taken, 1)
                    dve.wait_ge(taken, b * 2 + (t + 3))
                    dve.scalar_tensor_tensor(z_sb[:, t, :], b_all[:, :], rho[:, bass.ds(b * 2 + t, 1)], y_sb[:, t, :],
                                             ALU.mult, ALU.add).then_inc(added, 1)
                else:
                    dve.wait_ge(taken, b * 2 + (t + 3))
                    dve.tensor_tensor(z_sb[:, t, :], y_sb[:, t, :], x_sb[:, t, :], ALU.add).then_inc(added, 1)
                dve.wait_ge(added, b * 2 + (t + 3))
                dve.wait_ge(stored[t], b * 16)
                layer_norm(dve, z_sb[:, t, :], stats[:, t, :], mean_var[:, t, :], rstd[:, t, :], xn_sb[:, t, :],
                           normed, b * (2 * NORM_STEPS) + t * NORM_STEPS)


def split_rows(nc, s, x_rows, x_parts, r=None, u_all=None, dots=None, a_t=None, eye_bf=None):
    product = s.sb("product", [P, 2, 2, D], FP32)
    x_sb = s.sb("x_sb", [P, 2, D], FP32)
    x_scaled = s.sb("x_scaled", [P, 2, D], FP32)
    x_loaded = [s.sem(f"x_loaded{i}") for i in range(2)]
    scaled = s.sem("scaled")
    high = s.sem("high")
    low = s.sem("low")
    block = s.block()

    @block.sync
    def _(sp):
        def step(t, slot):
            sp.wait_ge(low, t + 1)
            sp.dma_start(x_sb[:, slot, :], x_rows[bass.ds(t * P, P), :]).then_inc(x_loaded[slot], 16)

        pairs_of(sp, NT, step)

    @block.scalar
    def _(act):
        def step(t, slot):
            act.wait_ge(scaled, t + 1)
            act.activation(x_parts[:, bass.ds(t, 1), 0, :], x_scaled[:, slot, :], ACT.Copy).then_inc(high, 1)

        pairs_of(act, NT, step)

    @block.vector
    def _(dve):
        dve.sem_inc(low, 2)

        def step(t, slot):
            dve.wait_ge(x_loaded[slot], (t - slot) * 8 + 16)
            if dots is not None:
                for i in range(2):
                    dve.scalar_tensor_tensor(product[:, slot, i, :], x_sb[:, slot, :], 1.0, u_all[:, i, :], ALU.mult, ALU.mult,
                                             accum_out=dots[:, i, bass.ds(t, 1)])
            if r is None:
                dve.tensor_scalar(x_scaled[:, slot, :], x_sb[:, slot, :], X_TOP, None, ALU.mult).then_inc(scaled, 1)
            else:
                dve.tensor_scalar(x_scaled[:, slot, :], x_sb[:, slot, :], r[:, bass.ds(t, 1)], X_TOP,
                                  ALU.mult, ALU.mult).then_inc(scaled, 1)
            dve.wait_ge(high, t + 1)
            dve.tensor_tensor(x_parts[:, bass.ds(t, 1), 1, :].squeeze(1), x_scaled[:, slot, :],
                              x_parts[:, bass.ds(t, 1), 0, :].squeeze(1), ALU.subtract).then_inc(low, 1)

        pairs_of(dve, NT, step)

    if a_t is not None:
        @block.gpsimd
        def _(pool):
            for j in range(NT):
                diag = a_t[:, j, j * P:(j + 1) * P]
                pool.tensor_tensor(diag, diag, eye_bf, ALU.add)


LEAK = 0.2
NO_EDGE = -9e15


def edge_vectors(nc, s, w_cat, a_w, u_scratch, u_all, eye):
    w_sb = s.sb("w_sb", [P, 2 * KT, D], FP32)
    a_all = s.sb("a_all", [P, D], FP32)
    product = s.sb("product", [P, D], FP32)
    u_col = s.sb("u_col", [P, 2 * KT], FP32)
    u_row = s.sb("u_row", [2 * KT, P], FP32)
    turn_ps = s.ps("turn_ps", [2 * KT, P])
    loaded = s.sem("loaded")
    dotted = s.sem("dotted")
    turned = s.sem("turned")
    turned_out = s.sem("turned_out")
    moved = s.sem("moved")
    block = s.block()

    @block.sync
    def _(sp):
        sp.dma_start(a_all[:, :], a_w.partition_broadcast(P)).then_inc(loaded, 16)
        sp.dma_start(w_sb[:, :, :], w_cat.rearrange("(k p) n -> p k n", p=P)).then_inc(loaded, 16)
        sp.wait_ge(turned_out, 1)
        sp.dma_start(u_scratch.rearrange("(k p) -> k p", p=P), u_row[:, :]).then_inc(moved, 16)
        sp.wait_ge(moved, 16)
        sp.dma_start(u_all.rearrange("p i n -> p (i n)"), u_scratch.partition_broadcast(P)).then_inc(moved, 16)
        sp.wait_ge(moved, 32)

    @block.vector
    def _(dve):
        dve.wait_ge(loaded, 32)
        for k in range(2 * KT):
            if k:
                dve.wait_ge(dotted, k)
            dve.tensor_tensor_reduce(out=product[:, :], in0=w_sb[:, k, :], in1=a_all[:, :], scale=1.0, scalar=0.0,
                                     op0=ALU.mult, op1=ALU.add, accum_out=u_col[:, k:k + 1]).then_inc(dotted, 1)
        dve.wait_ge(turned, 1)
        dve.tensor_copy(u_row[:, :], turn_ps[:, :]).then_inc(turned_out, 1)

    @block.tensor
    def _(pe):
        pe.wait_ge(dotted, 2 * KT)
        pe.transpose(turn_ps[:, :], u_col[:, :], eye).then_inc(turned, 1)


def row_shifts(nc, s, a_t, eye, eye_bf, dots, a_b, s_cols, shift_scratch):
    bias = s.sb("bias", [P, 2, NP], BF16)
    most = s.sb("most", [P, NP], FP32)
    ab_all = s.sb("ab_all", [P, 1], FP32)
    best = s.sb("best", [P, NT], FP32)
    s1b = s.sb("s1b", [P, NT], FP32)
    s1b_leak = s.sb("s1b_leak", [P, NT], FP32)
    z = s.sb("z", [P, NT], FP32)
    m = s.sb("m", [P, NT], FP32)
    shifts = s.sb("shifts", [P, 2 * NT], FP32)
    shifts_T = s.sb("shifts_T", [2 * NT, P], FP32)
    t_ps = [s.ps(f"t_ps{i}", [P, D]) for i in range(2)]
    st_ps = s.ps("st_ps", [2 * NT, P])
    ab_loaded = s.sem("ab_loaded")
    uneyed = s.sem("uneyed")
    biased = s.sem("biased")
    maxed = s.sem("maxed")
    turned = s.sem("turned")
    reduced = s.sem("reduced")
    chain = s.sem("chain")
    st_done = s.sem("st_done")
    st_copied = s.sem("st_copied")
    stored = s.sem("stored")
    block = s.block()
    BANKS = [(c, min(c + 4, NT)) for c in range(0, NT, 4)]

    @block.sync
    def _(sp):
        sp.dma_start(ab_all[:, :], a_b.partition_broadcast(P)).then_inc(ab_loaded, 16)
        sp.wait_ge(st_copied, 1)
        sp.dma_start(shift_scratch.rearrange("(t p) -> t p", p=P), shifts_T[:, :]).then_inc(stored, 16)
        sp.wait_ge(stored, 16)

    @block.scalar
    def _(act):
        act.wait_ge(uneyed, NT)

        def step(j, slot):
            act.wait_ge(maxed, j + 1)
            act.activation(bias[:, slot, :], a_t[:, bass.ds(j, 1), :].squeeze(1), ACT.Copy, scale=-NO_EDGE,
                           bias=NO_EDGE).then_inc(biased, 1)

        pairs_of(act, NT, step)
        act.wait_ge(st_done, 1)
        act.activation(shifts_T[:, :], st_ps[:, :], ACT.Copy).then_inc(st_copied, 1)

    @block.vector
    def _(dve):
        dve.memset(most[:, :], -3e38).then_inc(maxed, 2)
        for j in range(NT):
            diag = a_t[:, j, j * P:(j + 1) * P]
            dve.tensor_tensor(diag, diag, eye_bf, ALU.subtract).then_inc(uneyed, 1)

        def step(j, slot):
            dve.wait_ge(biased, j + 1)
            dve.wait_ge(maxed, j + 2)
            dve.scalar_tensor_tensor(most[:, :], bias[:, slot, :], dots[:, 1, bass.ds(j, 1)], most[:, :], ALU.add,
                                     ALU.max).then_inc(maxed, 1)

        pairs_of(dve, NT, step)
        for i, (a, z_) in enumerate(BANKS):
            dve.wait_ge(turned, i + 1)
            dve.tensor_reduce(best[:, a:z_], t_ps[i % 2][:, 0:(z_ - a) * P].rearrange("p (t c) -> p t c", c=P), AXX,
                              ALU.max).then_inc(reduced, 1)
        dve.wait_ge(reduced, len(BANKS))
        dve.wait_ge(ab_loaded, 16)
        dve.tensor_scalar(s1b[:, :], dots[:, 0, :], ab_all[:, :], None, ALU.add).then_inc(chain, 1)
        dve.wait_ge(chain, 1)
        dve.tensor_tensor(z[:, :], s1b[:, :], best[:, :], ALU.add).then_inc(chain, 1)
        dve.tensor_scalar(s1b_leak[:, :], s1b[:, :], LEAK, None, ALU.mult).then_inc(chain, 1)
        dve.wait_ge(chain, 2)
        dve.scalar_tensor_tensor(m[:, :], z[:, :], LEAK, z[:, :], ALU.mult, ALU.max).then_inc(chain, 1)
        dve.wait_ge(chain, 4)
        dve.tensor_tensor(shifts[:, 0:NT], s1b[:, :], m[:, :], ALU.subtract)
        dve.tensor_tensor(shifts[:, NT:2 * NT], s1b_leak[:, :], m[:, :], ALU.subtract).then_inc(chain, 1)
        dve.tensor_copy(s_cols[:, 0, :], dots[:, 1, :])
        dve.tensor_scalar(s_cols[:, 1, :], dots[:, 1, :], LEAK, None, ALU.mult)

    @block.tensor
    def _(pe):
        pe.wait_ge(maxed, NT + 2)
        for i, (a, z_) in enumerate(BANKS):
            if i >= 2:
                pe.wait_ge(reduced, i - 1)
            for t in range(a, z_):
                mm = pe.transpose(t_ps[i % 2][:, (t - a) * P:(t - a + 1) * P], most[:, t * P:(t + 1) * P], eye)
            mm.then_inc(turned, 1)
        pe.wait_ge(chain, 5)
        pe.transpose(st_ps[:, :], shifts[:, :], eye).then_inc(st_done, 1)


def attend(nc, s, a_t, x_parts, s_cols, shift_scratch, fc_w, fc_b, x_rows, out_rows, eps_half):
    w_sb = s.sb("w_sb", [P, KT, D], FP32)
    fcb_all = s.sb("fcb_all", [P, D], FP32)
    shift = s.sb("shift", [P, 2, 2, BR], FP32)
    e_hi = s.sb("e_hi", [P, 2, 2, BR], FP32)
    e_leak = s.sb("e_leak", [P, 2, 2, BR], FP32)
    p_hi = s.sb("p_hi", [P, 2, 2, BR], FP16)
    p_lo = s.sb("p_lo", [P, 2, 2, BR], FP16)
    row_sum = s.sb("row_sum", [P, 2, 2, BR], FP32)
    ones = s.sb("ones", [P, 1], FP32)
    s_scaled = s.sb("s_scaled", [P, 2], FP32)
    s_inv = s.sb("s_inv", [P, 2], FP32)
    agg_sb = s.sb("agg_sb", [P, KT, BR], FP32)
    x_sb = s.sb("x_sb", [P, D], FP32)
    z_sb = s.sb("z_sb", [P, D], FP32)
    xn_sb = s.sb("xn_sb", [P, D], FP32)
    stats = s.sb("stats", [P, 6], FP32)
    mean_var = s.sb("mean_var", [P, 2], FP32)
    rstd = s.sb("rstd", [P, 1], FP32)
    agg_ps = [[s.ps(f"agg_ps{i}{j}", [P, D]) for j in range(2)] for i in range(2)]
    y_ps = [s.ps(f"y_ps{i}", [P, D]) for i in range(2)]
    sum_ps = s.ps("sum_ps", [P, 2])
    w_loaded = s.sem("w_loaded")
    shift_loaded = [s.sem(f"shift_loaded{i}") for i in range(2)]
    x_loaded = s.sem("x_loaded")
    exped = s.sem("exped")
    maxed = s.sem("maxed")
    weighed = s.sem("weighed")
    high = s.sem("high")
    split = s.sem("split")
    summed = s.sem("summed")
    used = s.sem("used")
    sums_done = s.sem("sums_done")
    copied = s.sem("copied")
    multiplied = s.sem("multiplied")
    taken = s.sem("taken")
    added = s.sem("added")
    inverse = s.sem("inverse")
    ones_set = s.sem("ones_set")
    normed = s.sem("normed")
    stored = s.sem("stored")
    block = s.block()
    GP = NT // 2

    def peeled(e, first, step):
        first()
        pairs_of(e, NB - 1, step)
        step(NB - 1, 0, last=True)

    @block.sync
    def _(sp):
        sp.dma_start(w_sb[:, :, :], fc_w.rearrange("(k p) n -> p k n", p=P)).then_inc(w_loaded, 16)
        sp.dma_start(fcb_all[:, :], fc_b.partition_broadcast(P)).then_inc(w_loaded, 16)

        def load_shift(b, slot):
            for i in range(2):
                sp.dma_start(shift[:, slot, i, :], shift_scratch[bass.ds(b * BR + i * NP, BR)].partition_broadcast(P))\
                  .then_inc(shift_loaded[slot], 16)

        def step(b, slot, last=False):
            if not last:
                sp.wait_ge(exped, b * GP + GP)
                load_shift(next_block(b + 2), slot)
            for t in range(2):
                sp.wait_ge(added, b * 2 + t)
                sp.dma_start(x_sb[:, :], x_rows[bass.ds(b * BR + t * P, P), :]).then_inc(x_loaded, 16)
                sp.wait_ge(normed, b * (2 * NORM_STEPS) + (t + 1) * NORM_STEPS)
                sp.dma_start(out_rows[bass.ds(b * BR + t * P, P), :], xn_sb[:, :]).then_inc(stored, 16)

        load_shift(0, 0)
        load_shift(1, 1)
        pairs_of(sp, NB - 1, step)
        step(NB - 1, 0, last=True)
        sp.wait_ge(stored, 32 * NB)
        for i in range(2):
            sp.wait_ge(shift_loaded[i], 32 * (NB // 2 + 1))

    @block.scalar
    def _(act):
        act.sem_inc(copied, 4)

        def exps(b, slot, between=None):
            act.wait_ge(shift_loaded[slot], (b - slot) * 16 + 32)
            for g in range(GP):
                ring = (slot + g) % 2
                act.wait_ge(split, b * GP + (g + 1))
                act.wait_ge(summed, b * GP + (g + 1))
                for j in range(2):
                    for i, e in enumerate((e_hi, e_leak)):
                        done = act.activation(e[:, ring, j, :], shift[:, slot, i, :], ACT.Exp,
                                              bias=s_cols[:, i, 2 * g + j:2 * g + j + 1])
                done.then_inc(exped, 1)
                if g == 1 and between:
                    between()

        def copy(b, slot):
            act.wait_ge(used, b * GP + (GP + 2))
            act.wait_ge(multiplied, b * 2)
            for i in range(2):
                act.activation(agg_sb[:, 2 * i:2 * i + 2, :].rearrange("p k n -> p (k n)"), agg_ps[slot][i][:, :],
                               ACT.Copy).then_inc(copied, 1)

        def step(b, slot, last=False):
            if last:
                copy(b, slot)
            else:
                exps(b + 1, 1 - slot, between=lambda: copy(b, slot))

        peeled(act, lambda: exps(0, 0), step)

    @block.gpsimd
    def _(pool):
        pool.sem_inc(summed, 2)

        def step(b, slot):
            flat = row_sum[:, slot]
            for g in range(GP):
                ring = (slot + g) % 2
                pool.wait_ge(weighed, b * GP + (g + 1))
                if g == 0:
                    if slot == 1 or not isinstance(b, int):
                        pool.wait_ge(sums_done, b - 1)
                    pool.nop(nofuse=True)
                    pool.tensor_copy(flat, e_hi[:, ring, :, :]).then_inc(summed, 1)
                else:
                    pool.wait_ge(summed, b * GP + (g + 2))
                    pool.tensor_tensor(flat, flat, e_hi[:, ring, :, :], ALU.add).then_inc(summed, 1)

        def norms(b):
            for t in range(2):
                inv_std(pool, mean_var[:, :], rstd[:, :], eps_half, normed, b * (2 * NORM_STEPS) + t * NORM_STEPS)

        def both(b, slot, last=False):
            if not last:
                step(b + 1, 1 - slot)
            norms(b)

        peeled(pool, lambda: step(0, 0), both)

    @block.vector
    def _(dve):
        dve.sem_inc(split, 2)
        dve.sem_inc(taken, 2)
        dve.memset(ones[:, :], 1.0).then_inc(ones_set, 1)

        def weigh(b, slot, g):
            ring = (slot + g) % 2
            dve.wait_ge(exped, b * GP + (g + 1))
            dve.tensor_tensor(e_hi[:, ring, :, :], e_hi[:, ring, :, :], e_leak[:, ring, :, :], ALU.max)\
               .then_inc(maxed, 1)
            dve.wait_ge(maxed, b * GP + (g + 1))
            dve.scalar_tensor_tensor(e_hi[:, ring, :, :], e_hi[:, ring, :, :], 1.0,
                                     a_t[:, 2 * g:2 * g + 2, bass.ds(b * BR, BR)], ALU.min, ALU.mult)\
               .then_inc(weighed, 1)

        def split_weights(b, slot, g):
            ring = (slot + g) % 2
            dve.wait_ge(weighed, b * GP + (g + 1))
            dve.wait_ge(used, b * GP + (g + 1))
            dve.tensor_scalar(p_hi[:, ring, :, :], e_hi[:, ring, :, :], P_TOP, None, ALU.mult).then_inc(high, 1)
            dve.wait_ge(high, b * GP + (g + 1))
            dve.scalar_tensor_tensor(p_lo[:, ring, :, :], e_hi[:, ring, :, :], P_TOP, p_hi[:, ring, :, :], ALU.mult,
                                     ALU.subtract).then_inc(split, 1)

        def weights(b, slot):
            for g in range(GP):
                weigh(b, slot, g)
                split_weights(b, slot, g)

        def inverse_sums(b):
            dve.wait_ge(sums_done, b + 1)
            dve.tensor_scalar(s_scaled[:, :], sum_ps[:, :], P_TOP * X_TOP, None, ALU.mult).then_inc(inverse, 1)
            dve.wait_ge(inverse, b * 2 + 1)
            dve.reciprocal(s_inv[:, :], s_scaled[:, :]).then_inc(inverse, 1)
            dve.wait_ge(inverse, b * 2 + 2)

        def finish(b):
            for t in range(2):
                dve.wait_ge(multiplied, b * 2 + (t + 1))
                dve.wait_ge(x_loaded, b * 32 + (t + 1) * 16)
                dve.scalar_tensor_tensor(z_sb[:, :], y_ps[t][:, :], s_inv[:, t:t + 1], x_sb[:, :], ALU.mult, ALU.add)\
                   .then_inc(taken, 1)
                dve.wait_ge(taken, b * 2 + (t + 3))
                dve.tensor_tensor(z_sb[:, :], z_sb[:, :], fcb_all[:, :], ALU.add).then_inc(added, 1)
                dve.wait_ge(added, b * 2 + (t + 1))
                dve.wait_ge(stored, b * 32 + t * 16)
                layer_norm(dve, z_sb[:, :], stats[:, :], mean_var[:, :], rstd[:, :], xn_sb[:, :], normed,
                           b * (2 * NORM_STEPS) + t * NORM_STEPS)

        def step(b, slot, last=False):
            if not last:
                weights(b + 1, 1 - slot)
            inverse_sums(b)
            finish(b)

        dve.wait_ge(w_loaded, 32)
        peeled(dve, lambda: weights(0, 0), step)

    @block.tensor
    def _(pe):
        pe.sem_inc(used, 2)
        pe.wait_ge(w_loaded, 32)
        pe.wait_ge(ones_set, 1)

        def gather(b, slot):
            pe.wait_ge(copied, b * 2 + 2)
            for g in range(GP):
                ring = (slot + g) % 2
                pe.wait_ge(split, b * GP + (g + 3))
                for c in range(KT):
                    for j in range(2):
                        for n, (x_part, p) in enumerate(((0, p_hi), (1, p_hi), (0, p_lo))):
                            first, last = (g == 0 and j == 0 and n == 0), (g == GP - 1 and j == 1 and n == 2)
                            mm = pe.matmul(agg_ps[slot][c // 2][:, (c % 2) * BR:(c % 2 + 1) * BR],
                                           x_parts[:, 2 * g + j, x_part, c * P:(c + 1) * P], p[:, ring, j, :],
                                           start=first and c % 2 == 0, stop=last, skip_group_check=True)
                mm.then_inc(used, 1)
            pe.wait_ge(inverse, b * 2)
            pe.wait_ge(summed, b * GP + (GP + 2))
            for t in range(2):
                for j in range(2):
                    mm = pe.matmul(sum_ps[:, t:t + 1], row_sum[:, slot, j, t * P:(t + 1) * P], ones[:, :],
                                   start=(j == 0), stop=(j == 1))
            mm.then_inc(sums_done, 1)

        def step(b, slot, last=False):
            if not last:
                gather(b + 1, 1 - slot)
            pe.wait_ge(copied, b * 2 + 6)
            for t in range(2):
                pe.wait_ge(taken, b * 2 + (t + 1))
                for k in range(KT):
                    mm = pe.matmul(y_ps[t][:, :], agg_sb[:, k, t * P:(t + 1) * P], w_sb[:, k, :],
                                   start=(k == 0), stop=(k == KT - 1))
                mm.then_inc(multiplied, 1)

        peeled(pe, lambda: gather(0, 0), step)


def constants(nc, s, eye_in, fold_in, eye, eye_bf, fold, eps_half):
    loaded = s.sem("loaded")
    block = s.block()

    @block.sync
    def _(sp):
        sp.dma_start(eye, eye_in).then_inc(loaded, 16)
        sp.dma_start(fold, fold_in).then_inc(loaded, 16)

    @block.vector
    def _(dve):
        dve.memset(eps_half[:, 0:1], EPS)
        dve.memset(eps_half[:, 1:2], -0.5)
        dve.wait_ge(loaded, 32)
        dve.tensor_copy(eye_bf, eye)


def four_layers(nc, x, xT, adj, adjT, wqkv, wo, w1T, b1, w2T, b2, w_cat, a_w, a_b, fc_w, fc_b, w3, eye_in, fold_in,
                out):
    def scratch(name, shape, dt):
        return nc.dram_tensor(name, shape, dt, kind="Internal").ap()

    qk_parts = scratch("qk_parts", [2, 2, D, NP], FP32)
    v_parts = scratch("v_parts", [H, P, NT * P], FP16)
    o_rows = scratch("o_rows", [NP + BR, D], FP32)
    x1, x2, x3 = (scratch(f"x{i}_rows", [NP, D], FP32) for i in (1, 2, 3))
    u_scratch = scratch("u_scratch", [2 * D], FP32)
    shift_scratch = scratch("shift_scratch", [2 * NP], FP32)

    with Scope(nc, "kept") as kept:
        eye = kept.sb("eye", [P, P], FP32)[:, :]
        eye_bf = kept.sb("eye_bf", [P, P], BF16)[:, :]
        fold = kept.sb("fold", [P, HD], FP32)[:, :]
        eps_half = kept.sb("eps_half", [P, 2], FP32)
        v_inv = kept.sb("v_inv", [P, 1], FP32)[:, :]
        r = kept.sb("r", [P, NT], FP32)[:, :]
        r_out = kept.sb("r_out", [P, NT], FP32)[:, :]
        dots = kept.sb("dots", [P, 2, NT], FP32)
        s_cols = kept.sb("s_cols", [P, 2, NT], FP32)
        with Scope(nc, "constants") as s:
            constants(nc, s, eye_in, fold_in, eye, eye_bf, fold, eps_half)

        with Scope(nc, "values") as values:
            v_all = values.sb("v_all", [P, NT * D], FP32)[:, :]
            with Scope(nc, "project") as s:
                project_qkv(nc, s, xT, wqkv, qk_parts, v_all)
            with Scope(nc, "split_v") as s:
                split_values(nc, s, v_all, v_parts, eye, v_inv)
        with Scope(nc, "attention") as s:
            attention(nc, s, adj, qk_parts, v_parts, o_rows, eye, fold, v_inv)
        a_t = kept.sb("a_t", [P, NT, NP], BF16)
        with Scope(nc, "project_out") as s:
            project_out(nc, s, x, o_rows, wo, x1, adjT, a_t, eye, eps_half)

        with Scope(nc, "degrees") as s:
            degrees(nc, s, a_t, eye_bf, r, r_out, eps_half)
        with Scope(nc, "hidden") as hidden:
            g_parts = hidden.sb("g_parts", [P, NT, 3, w1T.shape[1]], BF16)
            r_parts = hidden.sb("r_parts", [P, NT, 3], BF16)
            with Scope(nc, "hidden_rows") as s:
                hidden_rows(nc, s, x1, w1T, b1, r, g_parts, r_parts, eye)
            with Scope(nc, "linear") as s:
                aggregate(nc, s, "linear", a_t, g_parts, w2T, b2, x1, x2, r, r_parts, eps_half)

        with Scope(nc, "rows") as rows:
            x_parts = rows.sb("x_parts", [P, NT, 2, D], FP16)
            with Scope(nc, "vectors") as vectors:
                u_all = vectors.sb("u_all", [P, 2, D], FP32)
                with Scope(nc, "edge_vectors") as s:
                    edge_vectors(nc, s, w_cat, a_w, u_scratch, u_all[:, :, :], eye)
                with Scope(nc, "split2") as s:
                    split_rows(nc, s, x2, x_parts, u_all=u_all, dots=dots)
            with Scope(nc, "row_shifts") as s:
                row_shifts(nc, s, a_t, eye, eye_bf, dots, a_b, s_cols, shift_scratch)
            with Scope(nc, "attend") as s:
                attend(nc, s, a_t, x_parts, s_cols, shift_scratch, fc_w, fc_b, x2, x3, eps_half)

            with Scope(nc, "split3") as s:
                split_rows(nc, s, x3, x_parts, r=r, a_t=a_t, eye_bf=eye_bf)
            with Scope(nc, "relu") as s:
                aggregate(nc, s, "relu", a_t, x_parts, w3, None, x3, out, r_out, None, eps_half)


def kernel(**inputs):
    import numpy as _np
    import concourse.bacc as _bacc
    from concourse import mybir as _mybir
    from concourse.bass_utils import run_bass_kernel_spmd as _run

    a = {name: _np.asarray(value) for name, value in inputs.items()}
    f32 = _np.float32

    def rows_padded(m, columns):
        out = _np.zeros((NP, columns), f32)
        out[:m.shape[0], :m.shape[1]] = m
        return out

    adjT = rows_padded(a["adj"].T, NP)
    adjT[N:, N:] = _np.eye(NP - N, dtype=f32)
    x = rows_padded(a["x"], D)
    arrays = {
        "x": x,
        "xT": x.T,
        "adj": rows_padded(a["adj"], NP),
        "adjT": adjT,
        "wqkv": _np.stack([a[f"L0_gnn_{w}"].transpose(1, 0, 2).reshape(D, D) for w in ("Wqs", "Wks", "Wvs")]),
        "wo": a["L0_gnn_Wo"].reshape(D, D),
        "w1T": a["L1_gnn_W1"].T,
        "b1": a["L1_gnn_b1"],
        "w2T": a["L1_gnn_W2"].T,
        "b2": a["L1_gnn_b2"],
        "w_cat": a["L2_gnn_W"],
        "a_w": a["L2_gnn_a_w"],
        "a_b": a["L2_gnn_a_b"].reshape(1),
        "fc_w": a["L2_gnn_fc_w"],
        "fc_b": a["L2_gnn_fc_b"],
        "w3": a["L3_gnn_W"],
        "eye_in": _np.eye(P, dtype=f32),
        "fold_in": _np.vstack([_np.eye(HD, dtype=f32)] * 2),
    }
    arrays = {name: _np.ascontiguousarray(value) for name, value in arrays.items()}

    nc = _bacc.Bacc("TRN2", target_bir_lowering=False, num_devices=1)
    args = {name: nc.dram_tensor(name, v.shape, _mybir.dt.from_np(v.dtype), kind="ExternalInput").ap()
            for name, v in arrays.items()}
    out = nc.dram_tensor("out", (NP, D), _mybir.dt.float32, kind="ExternalOutput").ap()
    four_layers(nc, out=out, **args)
    result = _run(nc, [arrays], core_ids=[0])
    return result.results[0]["out"][:N]
```

```python
import concourse.bass as bass
from concourse import mybir
from contextlib import ExitStack

FP32 = mybir.dt.float32
FP32R = mybir.dt.float32r
FP16 = mybir.dt.float16
BF16 = mybir.dt.bfloat16
ALU = mybir.AluOpType
ACT = mybir.ActivationFunctionType
AXX = mybir.AxisListType.X

P = 128
N = 2708
D = 512
KT = D // P
NT = -(-N // P)
NP = NT * P
BR = 2 * P
NB = NP // BR
H = 8
HD = D // H
PASSES3 = ((0, 0), (0, 1), (1, 0))

V_TOP = 8192.0
P_TOP = 4096.0
MASKED = -1e16


class Scope:

    def __init__(self, nc, stage):
        self.nc, self.stage = nc, stage
        self.stack = ExitStack()

    def __enter__(self):
        return self

    def __exit__(self, *a):
        self.stack.close()

    def sb(self, name, shape, dt):
        return self.stack.enter_context(self.nc.sbuf_tensor(f"{self.stage}_{name}", shape, dt))

    def ps(self, name, shape, dt=FP32):
        return self.stack.enter_context(self.nc.psum_tensor(f"{self.stage}_{name}", shape, dt))

    def sem(self, name):
        return self.stack.enter_context(self.nc.semaphore(f"{self.stage}_{name}"))

    def block(self):
        return self.stack.enter_context(self.nc.Block())



def pairs_of(e, count, step):
    with e.Fori(0, count // 2, 1) as n:
        step(n * 2, 0)
        step(n * 2 + 1, 1)
    if count % 2:
        step(count - 1, 0)


def next_block(v):
    span = NB.bit_length()
    past = (v + ((1 << span) - NB)) >> span
    return v - past * NB if isinstance(v, int) else (v - past * NB).with_bounds(min_val=0, max_val=NB - 1)


def project_qkv(nc, s, xT, wqkv, qk_parts, v_all):
    RING = 4
    M = 2 * KT
    NEXT_AT = 4
    w_raw = s.sb("w_raw", [P, 3, KT, D], FP32)
    w_hi = s.sb("w_hi", [P, 3, KT, D], FP32R)
    w_lo = s.sb("w_lo", [P, 3, KT, D], FP32R)
    x_raw = s.sb("x_raw", [P, 2, KT, BR], FP32)
    x_hi = s.sb("x_hi", [P, 2, KT, BR], FP32R)
    x_lo = s.sb("x_lo", [P, 2, KT, BR], FP32R)
    out_hi = s.sb("out_hi", [P, RING, BR], FP32R)
    out_lo = s.sb("out_lo", [P, RING, BR], FP32R)
    qk_ps = [s.ps(f"qk_ps{i}", [P, D]) for i in range(RING)]
    v_ps = [s.ps(f"v_ps{i}", [P, D]) for i in range(2)]

    w_loaded = s.sem("w_loaded")
    w_hi_ready = s.sem("w_hi_ready")
    w_ready = s.sem("w_ready")
    x_loaded = [s.sem(f"x_loaded{i}") for i in range(2)]
    x_hi_ready = s.sem("x_hi_ready")
    x_ready = s.sem("x_ready")
    qk_done = s.sem("qk_done")
    v_done = s.sem("v_done")
    v_free = s.sem("v_free")
    hi_ready = s.sem("hi_ready")
    lo_ready = s.sem("lo_ready")
    stored = [s.sem(f"stored{i}") for i in range(RING)]
    xT_v = xT.rearrange("(k p) n -> p k n", p=P)
    block = s.block()

    @block.gpsimd
    def _(pool):
        for i in range(3):
            pool.dma_start(w_raw[:, i], wqkv[i].rearrange("(k p) n -> p k n", p=P)).then_inc(w_loaded, 16)

        def step(b, slot):
            pool.wait_ge(x_ready, b + 1)
            pool.dma_start(x_raw[:, slot], xT_v[:, :, bass.ds(b * BR, BR)]).then_inc(x_loaded[slot], 16)

        pairs_of(pool, NB, step)

    @block.sync
    def _(sp):
        for r in range(RING):
            sp.sem_inc(stored[r], 16)

        def step(b, slot):
            for m in range(M):
                sp.wait_ge(lo_ready, b * M + (m + 1 + RING))
                for part, src in enumerate((out_hi, out_lo)):
                    dst = qk_parts[m // KT, part, (m % KT) * P:(m % KT + 1) * P, bass.ds(b * BR, BR)]
                    sp.dma_start(dst, src[:, m % RING, :].bitcast(FP32)).then_inc(stored[m % RING], 16)

        pairs_of(sp, NB, step)
        for r in range(RING):
            sp.wait_ge(stored[r], 32 * NB * M // RING + 16)

    @block.scalar
    def _(act):
        act.sem_inc(v_free, 2)
        act.wait_ge(w_loaded, 48)
        for i in range(3):
            act.activation(w_hi[:, i], w_raw[:, i], ACT.Copy).then_inc(w_hi_ready, 1)

        def split_x(b, slot):
            act.wait_ge(x_loaded[slot], (b - slot) * 8 + 16)
            act.wait_ge(v_done, b * 2 + 1)
            act.activation(x_hi[:, slot], x_raw[:, slot], ACT.Copy).then_inc(x_hi_ready, 1)

        def step(b, slot, last=False):
            for m in range(M):
                if m == NEXT_AT and not last:
                    split_x(b + 1, 1 - slot)
                r = m % RING
                act.wait_ge(qk_done, b * M + (m + 1))
                act.wait_ge(stored[r], b * (32 * M // RING) + 32 * (m // RING) + 16)
                act.activation(out_hi[:, r, :], qk_ps[r][:, 0:BR], ACT.Copy).then_inc(hi_ready, 1)
            for t in range(2):
                act.wait_ge(v_done, b * 2 + (t + 4))
                act.activation(v_all[:, bass.ds((b * 2 + t) * D, D)], v_ps[t][:, :], ACT.Copy).then_inc(v_free, 1)

        split_x(0, 0)
        pairs_of(act, NB - 1, step)
        step(NB - 1, 0, last=True)

    @block.vector
    def _(dve):
        dve.sem_inc(x_ready, 2)
        dve.sem_inc(lo_ready, RING)
        for i in range(3):
            dve.wait_ge(w_hi_ready, i + 1)
            dve.tensor_tensor(w_lo[:, i], w_raw[:, i], w_hi[:, i], ALU.subtract).then_inc(w_ready, 1)

        def split_x(b, slot):
            dve.wait_ge(x_hi_ready, b + 1)
            dve.tensor_tensor(x_lo[:, slot], x_raw[:, slot], x_hi[:, slot], ALU.subtract).then_inc(x_ready, 1)

        def step(b, slot, last=False):
            for m in range(M):
                if m == NEXT_AT and not last:
                    split_x(b + 1, 1 - slot)
                r = m % RING
                dve.wait_ge(hi_ready, b * M + (m + 1))
                dve.tensor_tensor(out_lo[:, r, :], qk_ps[r][:, 0:BR], out_hi[:, r, :],
                                  ALU.subtract).then_inc(lo_ready, 1)

        split_x(0, 0)
        pairs_of(dve, NB - 1, step)
        step(NB - 1, 0, last=True)

    @block.tensor
    def _(pe):
        pe.sem_inc(v_done, 3)
        pe.wait_ge(w_ready, 3)
        xs, ws = (x_hi, x_lo), (w_hi, w_lo)

        def step(b, slot):
            pe.wait_ge(x_ready, b + 3)
            for m in range(M):
                pe.wait_ge(lo_ready, b * M + (m + 1))
                for n, (i, j) in enumerate(PASSES3):
                    for k in range(KT):
                        mm = pe.matmul(qk_ps[m % RING][:, 0:BR],
                                       ws[i][:, m // KT, k, (m % KT) * P:(m % KT + 1) * P],
                                       xs[j][:, slot, k, :], start=(n == 0 and k == 0),
                                       stop=(n == 2 and k == KT - 1))
                mm.then_inc(qk_done, 1)
            for t in range(2):
                pe.wait_ge(v_free, b * 2 + (t + 1))
                for n, (i, j) in enumerate(PASSES3):
                    for k in range(KT):
                        mm = pe.matmul(v_ps[t][:, :], xs[j][:, slot, k, t * P:(t + 1) * P],
                                       ws[i][:, 2, k, :], start=(n == 0 and k == 0),
                                       stop=(n == 2 and k == KT - 1))
                mm.then_inc(v_done, 1)

        pairs_of(pe, NB, step)


def split_values(nc, s, v_all, v_parts, eye, v_inv):
    v_split = s.sb("v_split", [P, NT, H, 2, HD], FP16)
    top = s.sb("top", [P, 1], FP32)
    row = s.sb("row", [1, P], FP32)
    ones = s.sb("ones", [1, P], FP32)
    unit = s.sb("unit", [P, 1], FP32)
    scale = s.sb("scale", [P, 1], FP32)
    t_ps = s.ps("t_ps", [1, P])
    b_ps = s.ps("b_ps", [P, 1])
    step_done = s.sem("step_done")
    t_done = s.sem("t_done")
    b_done = s.sem("b_done")
    hi_ready = s.sem("hi_ready")
    lo_ready = s.sem("lo_ready")
    stored = s.sem("stored")
    v_view = v_all.rearrange("p (t h c) -> p t h c", t=NT, h=H)
    block = s.block()

    @block.vector
    def _(dve):
        dve.memset(ones[:, :], 1.0)
        dve.tensor_reduce(top[:, :], v_all, AXX, ALU.max, apply_absolute_value=True).then_inc(step_done, 1)
        dve.wait_ge(t_done, 1)
        dve.tensor_reduce(row[:, 0:1], t_ps[:, :], AXX, ALU.max).then_inc(step_done, 1)
        dve.wait_ge(b_done, 1)
        dve.tensor_scalar(unit[:, :], b_ps[:, :], 1e-30, 1.0 / V_TOP, ALU.max, ALU.mult).then_inc(step_done, 1)
        dve.wait_ge(step_done, 3)
        dve.tensor_scalar(v_inv, unit[:, :], 1.0 / P_TOP, None, ALU.mult)
        dve.reciprocal(scale[:, :], unit[:, :]).then_inc(step_done, 1)
        dve.wait_ge(step_done, 4)
        for h in range(H):
            dve.wait_ge(hi_ready, h + 1)
            dve.scalar_tensor_tensor(v_split[:, :, h, 1, :], v_view[:, :, h, :], scale[:, :],
                                     v_split[:, :, h, 0, :], ALU.mult, ALU.subtract).then_inc(lo_ready, 1)

    @block.tensor
    def _(pe):
        pe.wait_ge(step_done, 1)
        pe.transpose(t_ps[:, :], top[:, :], eye[:, :]).then_inc(t_done, 1)
        pe.wait_ge(step_done, 2)
        pe.matmul(b_ps[:, :], ones[:, :], row[:, 0:1], start=True, stop=True).then_inc(b_done, 1)

    @block.scalar
    def _(act):
        act.wait_ge(step_done, 4)
        for h in range(H):
            act.activation(v_split[:, :, h, 0, :], v_view[:, :, h, :], ACT.Copy,
                           scale=scale[:, :]).then_inc(hi_ready, 1)

    @block.sync
    def _(sp):
        for h in range(H):
            sp.wait_ge(lo_ready, h + 1)
            sp.dma_start(v_parts[h].rearrange("p (t c) -> p t c", t=NT),
                         v_split[:, :, h].rearrange("p t a c -> p t (a c)")).then_inc(stored, 16)
        sp.wait_ge(stored, 16 * H)


PAIR = 1024
PIECES = [(c, min(PAIR, N - c)) for c in range(0, N, PAIR)]
EXPS = [(0, 5 * BR + 74), (5 * BR + 74, N - 5 * BR - 74)]
GROUPS = NT // 2
PE_ORDER = ["S0", "T0", "T1", "S1", "O", "V0", "S2", "T2", "T3", "V1", "T4", "S3", "V2", "T5", "T6", "S4", "V3",
            "S5", "V4", "T7", "T8", "V5", "V6", "T9", "V7", "T10", "V8", "V9", "V10"]
DVE_ORDER = ["S0", "T0", "T1", "S1", "O", "S2", "T2", "T3", "T4", "S3", "T5", "S4", "T6", "S5", "T7", "T8", "T9",
             "T10"]
ACT_ORDER = ["H0", "H1", "C", "H2", "H3", "H4", "E0", "H5", "H6", "E1", "H7", "H8", "E2", "H9", "H10", "E3"]
SUMS_AFTER = (1, 3)


def attention(nc, s, adj, qk_parts, v_parts, o_rows, eye, fold, v_inv, deg, adjT, adjT_bf):
    S_RING, T_RING, W_RING = 2, 3, 4
    keys = s.sb("keys", [P, H, N], FP32R)
    mask = [s.sb(f"mask{t}", [P, N], BF16) for t in range(2)]
    adj_rows = [s.sb(f"adj_rows{t}", [P, NP], FP32) for t in range(2)]
    probs = [[s.sb(f"probs{i}{t}", [P, NP], FP32) for t in range(2)] for i in range(2)]
    vals = s.sb("vals", [P, 2, NT, P], FP16)
    q_st = s.sb("q_st", [P, 2, 2, BR], FP32R)
    pt_hi = s.sb("pt_hi", [P, W_RING, 2 * BR], FP16)
    pt_lo = s.sb("pt_lo", [P, W_RING, 2 * BR], FP16)
    top = s.sb("top", [P, 2, 2, 3], FP32)
    sums = s.sb("sums", [P, 2, 2, 2], FP32)
    r_sum = s.sb("r_sum", [P, 2, 2], FP32)
    r_inv = s.sb("r_inv", [P, 2, 2], FP32)
    acc_sb = s.sb("acc_sb", [P, 2, BR], FP32)
    o_sb = s.sb("o_sb", [P, 2, D], FP32)
    s_ps = [s.ps(f"s_ps{i}", [P, PAIR]) for i in range(S_RING)]
    t_ps = [s.ps(f"t_ps{i}", [P, 2 * BR]) for i in range(T_RING)]
    acc_ps = s.ps("acc_ps", [P, D])

    keys_loaded = [s.sem(f"keys_loaded{h}") for h in range(H)]
    adj_loaded = [s.sem(f"adj_loaded{t}") for t in range(2)]
    adj_summed = s.sem("adj_summed")
    adj_fixed = s.sem("adj_fixed")
    adjT_stored = s.sem("adjT_stored")
    mask_ready = s.sem("mask_ready")
    q_loaded = [s.sem(f"q_loaded{i}") for i in range(2)]
    v_loaded = [s.sem(f"v_loaded{i}") for i in range(2)]
    scored = s.sem("scored")
    masked = s.sem("masked")
    weighed = s.sem("weighed")
    turned = s.sem("turned")
    hi_ready = s.sem("hi_ready")
    drained = s.sem("drained")
    used = s.sem("used")
    acc_copied = s.sem("acc_copied")
    folded = s.sem("folded")
    r_done = s.sem("r_done")
    o_stored = s.sem("o_stored")
    padded = s.sem("padded")
    block = s.block()
    SP_, GP = 2 * len(PIECES), GROUPS
    TP = GROUPS + 1

    def stages(e, stage):
        with e.Fori(0, NB, 1) as b:
            for h in range(H):
                stage(b, h)

    @block.sync
    def _(sp):
        def load_q(row0, h, slot):
            for a in range(2):
                for part in range(2):
                    half = part ^ a
                    sp.dma_start(q_st[half * HD:(half + 1) * HD, slot, a, :].bitcast(FP32),
                                 qk_parts[0, part, h * HD:(h + 1) * HD, bass.ds(row0, BR)])\
                      .then_inc(q_loaded[slot], 16)

        def load_keys(h):
            for part in range(2):
                sp.dma_start(keys[part * HD:(part + 1) * HD, h, :].bitcast(FP32),
                             qk_parts[1, part, h * HD:(h + 1) * HD, 0:N]).then_inc(keys_loaded[h], 16)

        def load_v(h, slot):
            sp.dma_start(vals[:, slot], v_parts[h].rearrange("p (t c) -> p t c", t=NT)).then_inc(v_loaded[slot], 16)

        load_q(0, 0, 0)
        load_keys(0)
        load_q(0, 1, 1)
        load_keys(1)
        load_v(0, 0)
        load_v(1, 1)
        for h in range(2, H):
            load_keys(h)

        def stage(b, h):
            sp.wait_ge(scored, b * (H * SP_) + (h + 1) * SP_)
            nxt = b * BR if h + 2 < H else next_block(b + 1) * BR
            load_q(nxt, (h + 2) % H, h % 2)
            if h == 0:
                sp.wait_ge(drained, b * (H * TP) + 3 + T_RING)
                sp.dma_start(o_rows[bass.ds(b * BR, BR), :].rearrange("(t p) c -> p t c", p=P),
                             o_sb[:, :, :]).then_inc(o_stored, 16)
            sp.wait_ge(used, b * (H * GP) + (h + 1) * GP + T_RING)
            load_v((h + 2) % H, h % 2)

        stages(sp, stage)
        sp.wait_ge(drained, NB * H * TP + 1 + T_RING)
        sp.dma_start(o_rows[NB * BR:(NB + 1) * BR, :].rearrange("(t p) c -> p t c", p=P),
                     o_sb[:, :, :]).then_inc(o_stored, 16)
        sp.wait_ge(o_stored, 16 * (NB + 1))
        for i in range(2):
            sp.wait_ge(q_loaded[i], 64 * (1 + NB * H // 2))
            sp.wait_ge(v_loaded[i], 16 * (1 + NB * H // 2))

    @block.gpsimd
    def _(pool):
        def load_adj(row0, t):
            pool.dma_start(adj_rows[t][:, 0:N], adj[bass.ds(row0 + t * P, P), 0:N]).then_inc(adj_loaded[t], 16)

        def make_mask(b, t, first=False):
            pool.wait_ge(adj_fixed, b * 2 + (t + 1))
            if not first:
                pool.wait_ge(masked, b * (H * SP_) - (1 - t) * len(PIECES) + S_RING)
            pool.nop(nofuse=True)
            pool.tensor_scalar(mask[t][:, :], adj_rows[t][:, 0:N], -MASKED, MASKED, ALU.mult, ALU.add)\
                .then_inc(mask_ready, 1)

        for t in range(2):
            pool.memset(adj_rows[t][:, N:NP], 0.0).then_inc(padded, 1)
            for i in range(2):
                pool.memset(probs[i][t][:, N:NP], 0.0).then_inc(padded, 1)
        pool.memset(sums[:, 1], 1.0).then_inc(padded, 1)
        pool.memset(o_sb[:, :, :], 0.0).then_inc(padded, 1)
        pool.wait_ge(padded, 9)
        for t in range(2):
            load_adj(0, t)
        for t in range(2):
            make_mask(0, t, first=True)
        for j in range(NT):
            pool.dma_start(adjT_bf[j * P:(j + 1) * P, :], adjT[j * P:(j + 1) * P, :]).then_inc(adjT_stored, 16)
        with pool.Fori(0, NB, 1) as b:
            nxt = next_block(b + 1) * BR
            for t in range(2):
                pool.wait_ge(mask_ready, b * 2 + (t + 1))
                load_adj(nxt, t)
            for t in range(2):
                make_mask(b + 1, t)
        pool.wait_ge(adjT_stored, 16 * NT)

    @block.tensor
    def _(pe):
        pe.sem_inc(used, T_RING)

        def scores(base, n_in_block, h, slot, i):
            t, (c0, width) = i // len(PIECES), PIECES[i % len(PIECES)]
            pe.wait_ge(masked, base * (H * SP_) + n_in_block * SP_ + (i + 1))
            for c in range(c0, c0 + width, 512):
                w = min(512, c0 + width - c)
                for a in range(2):
                    mm = pe.matmul(s_ps[i % S_RING][:, c - c0:c - c0 + w], q_st[:, slot, a, t * P:(t + 1) * P],
                                   keys[:, h, c:c + w], start=(a == 0), stop=(a == 1))
            mm.then_inc(scored, 1)

        def fold_heads(b, n_in_block):
            pe.wait_ge(acc_copied, b * H + n_in_block + 1)
            pe.wait_ge(drained, b * (H * TP) + n_in_block * TP + 3)
            for t in range(2):
                mm = pe.matmul(t_ps[2][:, t * HD:(t + 1) * HD], acc_sb[:, (n_in_block + 1) % 2, t * P:(t + 1) * P],
                               fold, start=True, stop=True)
            mm.then_inc(folded, 1)

        pe.wait_ge(q_loaded[0], 64)
        pe.wait_ge(keys_loaded[0], 32)
        for i in range(SP_):
            scores(0, 0, 0, 0, i)

        def stage(b, h):
            cur, nxt = h % 2, (h + 1) % 2
            for what in PE_ORDER:
                kind, i = what[0], int(what[1:] or 0)
                ring = i if i < 2 else i + 1
                if kind == "S":
                    if i == 0:
                        pe.wait_ge(q_loaded[nxt], b * (64 * H // 2) + 64 * ((h + 1) // 2 + 1))
                        pe.wait_ge(keys_loaded[(h + 1) % H], 32)
                    scores(b, h + 1, (h + 1) % H, nxt, i)
                elif kind == "T":
                    late = (i + 1) * BR > EXPS[0][1]
                    pe.wait_ge(weighed, b * (4 * H) + 4 * h + (4 if late else 3))
                    pe.wait_ge(drained, b * (H * TP) + h * TP + (ring + 1))
                    for j in range(2):
                        for t in range(2):
                            mm = pe.transpose(t_ps[ring % T_RING][:, j * BR + t * P:j * BR + (t + 1) * P],
                                              probs[cur][t][:, (2 * i + j) * P:(2 * i + j + 1) * P], eye)
                    mm.then_inc(turned, 1)
                elif kind == "V":
                    if i == 0:
                        pe.wait_ge(v_loaded[cur], b * (16 * H // 2) + 16 * (h // 2 + 1))
                        pe.wait_ge(acc_copied, b * H + h + 1)
                    pe.wait_ge(drained, b * (H * TP) + h * TP + (ring + 1) + T_RING)
                    for j in range(2):
                        for part in (pt_hi, pt_lo):
                            mm = pe.matmul(acc_ps[:, 0:BR], vals[:, cur, 2 * i + j, :],
                                           part[:, i % W_RING, j * BR:(j + 1) * BR],
                                           start=(i == 0 and j == 0 and part is pt_hi),
                                           stop=(i == GROUPS - 1 and j == 1 and part is pt_lo))
                    mm.then_inc(used, 1)
                else:
                    fold_heads(b, h)

        stages(pe, stage)
        fold_heads(NB, 0)

    @block.scalar
    def _(act):

        def exps(b, n_in_block, i):
            cur, t, e = n_in_block % 2, i // 2, i % 2
            act.wait_ge(masked, b * (H * SP_) + n_in_block * SP_ + (t + 1) * len(PIECES) + S_RING)
            c, w = EXPS[e]
            cols = probs[cur][t][:, c:c + w]
            act.activation(cols, cols, ACT.Exp, bias=top[:, cur, t, 2:3], scale=-1.0,
                           accum_out=sums[:, cur, t, e:e + 1]).then_inc(weighed, 1)

        def high_part(b, h, i):
            ring = i if i < 2 else i + 1
            act.wait_ge(turned, b * (H * GP) + h * GP + (i + 1))
            act.wait_ge(used, b * (H * GP) + h * GP + (i + 1 if i < 3 else i))
            act.activation(pt_hi[:, i % W_RING, :], t_ps[ring % T_RING][:, :], ACT.Copy, scale=P_TOP)\
                .then_inc(hi_ready, 1)

        def copy_acc(b, n_in_block):
            act.wait_ge(used, b * (H * GP) + n_in_block * GP + T_RING)
            act.activation(acc_sb[:, (n_in_block + 1) % 2, :], acc_ps[:, 0:BR], ACT.Copy).then_inc(acc_copied, 1)

        def sum_adj(b, tile0, t):
            act.wait_ge(adj_loaded[t], b * 16 + 16)
            rows = adj_rows[t][:, 0:N]
            act.activation(rows, rows, ACT.Copy, accum_out=deg[:, bass.ds(tile0 + t, 1)]).then_inc(adj_summed, 1)

        act.wait_ge(padded, 9)
        sum_adj(0, 0, 0)
        sum_adj(0, 0, 1)
        for i in range(4):
            exps(0, 0, i)

        def stage(b, h):
            for what in ACT_ORDER:
                kind, i = what[0], int(what[1:] or 0)
                if kind == "H":
                    high_part(b, h, i)
                elif kind == "E":
                    exps(b, h + 1, i)
                else:
                    copy_acc(b, h)
            if h in SUMS_AFTER:
                sum_adj(b + 1, next_block(b + 1) * 2, SUMS_AFTER.index(h))

        stages(act, stage)
        copy_acc(NB, 0)

    @block.vector
    def _(dve):
        dve.memset(acc_ps[:, 0:BR], 0.0).then_inc(padded, 1)
        dve.wait_ge(padded, 9)
        dve.sem_inc(masked, S_RING)
        dve.sem_inc(drained, T_RING)

        def set_diagonal(b, row0):
            for t in range(2):
                dve.wait_ge(adj_summed, b * 2 + (t + 1))
                diag = adj_rows[t][:, bass.ds(row0 + t * P, P)]
                dve.tensor_tensor(diag, diag, eye, ALU.max).then_inc(adj_fixed, 1)

        def mask_scores(b, n_in_block, i):
            cur, t, k = n_in_block % 2, i // len(PIECES), i % len(PIECES)
            c, w = PIECES[k]
            dve.wait_ge(scored, b * (H * SP_) + n_in_block * SP_ + (i + 1))
            if n_in_block in (0, H) and k == 0:
                at_block = b if n_in_block == 0 else b + 1
                dve.wait_ge(mask_ready, at_block * 2 + (t + 1))
            if k > 0:
                dve.wait_ge(masked, b * (H * SP_) + n_in_block * SP_ + i + S_RING)
            dve.nop(nofuse=True)
            dve.tensor_tensor_reduce(out=probs[cur][t][:, c:c + w], in0=s_ps[i % S_RING][:, 0:w],
                                     in1=mask[t][:, c:c + w], scale=-(HD ** -0.5),
                                     scalar=3e38 if k == 0 else top[:, cur, t, k - 1:k],
                                     op0=ALU.add, op1=ALU.min, accum_out=top[:, cur, t, k:k + 1])\
                .then_inc(masked, 1)

        def low_part(b, h, i):
            ring = i if i < 2 else i + 1
            dve.wait_ge(hi_ready, b * (H * GP) + h * GP + (i + 1))
            dve.scalar_tensor_tensor(pt_lo[:, i % W_RING, :], t_ps[ring % T_RING][:, :], P_TOP,
                                     pt_hi[:, i % W_RING, :], ALU.mult, ALU.subtract).then_inc(drained, 1)

        def norm(b, n_in_block):
            h, slot = (n_in_block + H - 1) % H, (n_in_block + 1) % 2
            dve.tensor_tensor(r_sum[:, slot, :], sums[:, slot, :, 0], sums[:, slot, :, 1], ALU.add).then_inc(r_done, 1)
            dve.wait_ge(r_done, b * (2 * H) + n_in_block * 2 + 1)
            dve.reciprocal(r_inv[:, slot, :], r_sum[:, slot, :]).then_inc(r_done, 1)
            dve.wait_ge(r_done, b * (2 * H) + n_in_block * 2 + 2)
            dve.wait_ge(folded, b * H + (n_in_block + 1))
            if h == 0:
                dve.wait_ge(o_stored, b * 16 + 16)
            dve.scalar_tensor_tensor(o_sb[:, :, h * HD:(h + 1) * HD],
                                     t_ps[2][:, 0:2 * HD].rearrange("p (t c) -> p t c", t=2), v_inv,
                                     r_inv[:, slot, :].unsqueeze(2).broadcast_to([P, 2, HD]), ALU.mult, ALU.mult)\
                .then_inc(drained, 1)

        set_diagonal(0, 0)
        for i in range(SP_):
            mask_scores(0, 0, i)

        def stage(b, h):
            for what in DVE_ORDER:
                kind, i = what[0], int(what[1:] or 0)
                if kind == "S":
                    mask_scores(b, h + 1, i)
                elif kind == "T":
                    low_part(b, h, i)
                elif kind == "O":
                    norm(b, h)
            if h == H // 2:
                set_diagonal(b + 1, next_block(b + 1) * BR)

        stages(dve, stage)
        norm(NB, 0)


EPS = 1e-5
X_TOP = 256.0
NORM_STEPS = 5


def layer_norm(dve, z, stats, mean_var, rstd, out, chain, at):
    dve.bn_stats(stats, z).then_inc(chain, 1)
    dve.wait_ge(chain, at + 1)
    dve.nop(nofuse=True)
    dve.bn_aggr(mean_var, stats).then_inc(chain, 1)
    dve.wait_ge(chain, at + 4)
    dve.tensor_scalar(out, z, mean_var[:, 0:1], rstd, ALU.subtract, ALU.mult).then_inc(chain, 1)


def inv_std(pool, mean_var, rstd, eps_half, chain, at):
    pool.wait_ge(chain, at + 2)
    pool.tensor_tensor(mean_var[:, 1:2], mean_var[:, 1:2], eps_half[:, 0:1], ALU.add).then_inc(chain, 1)
    pool.wait_ge(chain, at + 3)
    pool.tensor_tensor(rstd, mean_var[:, 1:2], eps_half[:, 1:2], ALU.pow).then_inc(chain, 1)


def project_out(nc, s, x_in, o_rows, wo, x_rows, adjT_bf, a_t, eye, eps_half):
    w_sb = s.sb("w_sb", [P, KT, D], FP32)
    o_sb = s.sb("o_sb", [P, 2, D], FP32)
    oT_sb = s.sb("oT_sb", [P, 2, D], FP32)
    xr_sb = s.sb("xr_sb", [P, 2, D], FP32)
    z_sb = s.sb("z_sb", [P, 2, D], FP32)
    xn_sb = s.sb("xn_sb", [P, 2, D], FP32)
    stats = s.sb("stats", [P, 2, 6], FP32)
    mean_var = s.sb("mean_var", [P, 2, 2], FP32)
    rstd = s.sb("rstd", [P, 2, 1], FP32)
    t_ps = [s.ps(f"t_ps{i}", [P, D]) for i in range(2)]
    y_ps = [s.ps(f"y_ps{i}", [P, D]) for i in range(2)]
    w_loaded = s.sem("w_loaded")
    o_loaded = [s.sem(f"o_loaded{i}") for i in range(2)]
    x_loaded = [s.sem(f"x_loaded{i}") for i in range(2)]
    a_loaded = s.sem("a_loaded")
    turned = s.sem("turned")
    copied = s.sem("copied")
    multiplied = s.sem("multiplied")
    added = s.sem("added")
    normed = s.sem("normed")
    stored = [s.sem(f"stored{i}") for i in range(2)]
    block = s.block()

    @block.gpsimd
    def _(pool):
        def step(t, slot):
            pool.dma_start(a_t[:, bass.ds(t, 1), :].squeeze(1), adjT_bf[bass.ds(t * P, P), :]).then_inc(a_loaded, 16)
            inv_std(pool, mean_var[:, slot, :], rstd[:, slot, :], eps_half, normed, t * NORM_STEPS)

        pairs_of(pool, NT, step)
        pool.wait_ge(a_loaded, 16 * NT)

    @block.sync
    def _(sp):
        for i in range(2):
            sp.sem_inc(stored[i], 16)
        sp.dma_start(w_sb[:, :, :], wo.rearrange("(k p) n -> p k n", p=P)).then_inc(w_loaded, 16)

        def load_o(t, slot):
            sp.dma_start(o_sb[:, slot, :], o_rows[bass.ds(t * P + BR, P), :]).then_inc(o_loaded[slot], 16)

        def load_x(t, slot):
            sp.dma_start(xr_sb[:, slot, :], x_in[bass.ds(t * P, P), :]).then_inc(x_loaded[slot], 16)

        def step(t, slot):
            if not isinstance(t, int) or t + 3 < NT:
                sp.wait_ge(turned, t + 4)
                load_o(t + 3, 1 - slot)
            if not isinstance(t, int) or t + 2 < NT:
                sp.wait_ge(added, t + 3)
                load_x(t + 2, slot)
            sp.wait_ge(normed, t * NORM_STEPS + NORM_STEPS)
            sp.dma_start(x_rows[bass.ds(t * P, P), :], xn_sb[:, slot, :]).then_inc(stored[slot], 16)

        for t in range(2):
            load_o(t, t)
            load_x(t, t)
        sp.wait_ge(turned, 3)
        load_o(2, 0)
        pairs_of(sp, NT - 4, step)
        for t in range(NT - 4, NT):
            step(t, t % 2)
        for i in range(2):
            sp.wait_ge(stored[i], 16 * NT // 2 + 16)

    @block.scalar
    def _(act):
        act.sem_inc(copied, 2)

        def step(t, slot):
            act.wait_ge(turned, t + 3)
            act.wait_ge(multiplied, t + 1)
            act.activation(oT_sb[:, slot, :], t_ps[slot][:, :], ACT.Copy).then_inc(copied, 1)

        pairs_of(act, NT, step)

    @block.tensor
    def _(pe):
        pe.sem_inc(turned, 2)
        pe.sem_inc(multiplied, 2)
        pe.wait_ge(w_loaded, 16)

        def turn(t, slot):
            pe.wait_ge(o_loaded[slot], (t - slot) * 8 + 16)
            pe.wait_ge(copied, t + 1)
            for k in range(KT):
                mm = pe.transpose(t_ps[slot][:, k * P:(k + 1) * P], o_sb[:, slot, k * P:(k + 1) * P], eye)
            mm.then_inc(turned, 1)

        def step(t, slot, last=False):
            if not last:
                turn(t + 1, 1 - slot)
            pe.wait_ge(copied, t + 3)
            pe.wait_ge(added, t + 1)
            for k in range(KT):
                mm = pe.matmul(y_ps[slot][:, :], oT_sb[:, slot, k * P:(k + 1) * P], w_sb[:, k, :],
                               start=(k == 0), stop=(k == KT - 1))
            mm.then_inc(multiplied, 1)

        turn(0, 0)
        pairs_of(pe, NT - 2, step)
        step(NT - 2, 0)
        step(NT - 1, 1, last=True)

    @block.vector
    def _(dve):
        dve.sem_inc(added, 2)

        def step(t, slot):
            dve.wait_ge(multiplied, t + 3)
            dve.wait_ge(x_loaded[slot], (t - slot) * 8 + 16)
            dve.tensor_tensor(z_sb[:, slot, :], y_ps[slot][:, :], xr_sb[:, slot, :], ALU.add).then_inc(added, 1)
            dve.wait_ge(added, t + 3)
            dve.wait_ge(stored[slot], (t - slot) * 8 + 16)
            layer_norm(dve, z_sb[:, slot, :], stats[:, slot, :], mean_var[:, slot, :], rstd[:, slot, :],
                       xn_sb[:, slot, :], normed, t * NORM_STEPS)

        pairs_of(dve, NT, step)


def degrees(nc, s, a_t, eye_bf, deg, r, r_in, r_out, eps_half):
    whole = s.sb("whole", [P, NT], FP32)
    pos = s.sb("pos", [P, NT], FP32)
    safe = s.sb("safe", [P, NT], FP32)
    inv = s.sb("inv", [P, NT], FP32)
    done = s.sem("done")
    block = s.block()

    @block.vector
    def _(dve):
        dve.tensor_scalar(whole[:, :], deg, 1.0, None, ALU.add).then_inc(done, 1)
        dve.wait_ge(done, 1)
        dve.tensor_scalar(pos[:, :], whole[:, :], 0.0, None, ALU.is_gt).then_inc(done, 1)
        dve.tensor_scalar(safe[:, :], whole[:, :], 1e-30, None, ALU.max).then_inc(done, 1)
        for j in range(NT):
            diag = a_t[:, j, j * P:(j + 1) * P]
            dve.tensor_tensor(diag, diag, eye_bf, ALU.add)
        dve.wait_ge(done, 4)
        dve.tensor_tensor(r, inv[:, :], pos[:, :], ALU.mult).then_inc(done, 1)
        dve.wait_ge(done, 5)
        dve.tensor_scalar(r_in, r, X_TOP, None, ALU.mult)
        dve.tensor_scalar(r_out, r, 1.0 / X_TOP, None, ALU.mult)

    @block.gpsimd
    def _(pool):
        pool.wait_ge(done, 3)
        pool.tensor_tensor(inv[:, :], safe[:, :], eps_half[:, 1:2].broadcast_to([P, NT]), ALU.pow).then_inc(done, 1)


def hidden_rows(nc, s, x_rows, w1T, b1, r, g_parts, r_parts, eye):
    HID = w1T.shape[1]
    w_sb = s.sb("w_sb", [P, KT, HID], FP32)
    b1_all = s.sb("b1_all", [P, HID], FP32)
    x_sb = s.sb("x_sb", [P, 2, D], FP32)
    xT_sb = s.sb("xT_sb", [P, 2, D], FP32)
    h_sb = s.sb("h_sb", [P, 2, HID], FP32)
    g_sb = s.sb("g_sb", [P, 2, HID], FP32)
    rest = s.sb("rest", [P, 2, HID], FP32)
    r_rest = s.sb("r_rest", [P, NT], FP32)
    t_ps = [s.ps(f"t_ps{i}", [P, D]) for i in range(2)]
    h_ps = [s.ps(f"h_ps{i}", [P, D]) for i in range(2)]
    w_loaded = s.sem("w_loaded")
    x_loaded = [s.sem(f"x_loaded{i}") for i in range(2)]
    turned = s.sem("turned")
    copied = s.sem("copied")
    multiplied = s.sem("multiplied")
    biased = s.sem("biased")
    chain = s.sem("chain")
    high = s.sem("high")
    middle = s.sem("middle")
    r_chain = s.sem("r_chain")
    block = s.block()

    @block.sync
    def _(sp):
        sp.dma_start(w_sb[:, :, :], w1T.rearrange("(k p) n -> p k n", p=P)).then_inc(w_loaded, 16)
        sp.dma_start(b1_all[:, :], b1.partition_broadcast(P)).then_inc(w_loaded, 16)

        def step(t, slot):
            sp.wait_ge(turned, t + 1)
            sp.dma_start(x_sb[:, slot, :], x_rows[bass.ds(t * P, P), :]).then_inc(x_loaded[slot], 16)

        pairs_of(sp, NT, step)

    @block.tensor
    def _(pe):
        pe.sem_inc(turned, 2)
        pe.sem_inc(multiplied, 2)
        pe.wait_ge(w_loaded, 32)

        def turn(t, slot):
            pe.wait_ge(x_loaded[slot], (t - slot) * 8 + 16)
            pe.wait_ge(copied, t + 1)
            for k in range(KT):
                mm = pe.transpose(t_ps[slot][:, k * P:(k + 1) * P], x_sb[:, slot, k * P:(k + 1) * P], eye)
            mm.then_inc(turned, 1)

        def step(t, slot, last=False):
            if not last:
                turn(t + 1, 1 - slot)
            pe.wait_ge(copied, t + 3)
            pe.wait_ge(biased, t + 1)
            for k in range(KT):
                mm = pe.matmul(h_ps[slot][:, 0:HID], xT_sb[:, slot, k * P:(k + 1) * P], w_sb[:, k, :],
                               start=(k == 0), stop=(k == KT - 1))
            mm.then_inc(multiplied, 1)

        turn(0, 0)
        pairs_of(pe, NT - 2, step)
        step(NT - 2, 0)
        step(NT - 1, 1, last=True)

    @block.scalar
    def _(act):
        act.sem_inc(copied, 2)

        def copy(t, slot):
            act.wait_ge(turned, t + 3)
            act.wait_ge(multiplied, t + 1)
            act.activation(xT_sb[:, slot, :], t_ps[slot][:, :], ACT.Copy).then_inc(copied, 1)

        def step(t, slot, last=False):
            if not last:
                copy(t + 1, 1 - slot)
            act.wait_ge(chain, t * 3 + 1)
            act.activation(g_parts[:, bass.ds(t, 1), 0, :], g_sb[:, slot, :], ACT.Copy).then_inc(high, 1)
            act.wait_ge(chain, t * 3 + 2)
            act.activation(g_parts[:, bass.ds(t, 1), 1, :], rest[:, slot, :], ACT.Copy).then_inc(middle, 1)

        copy(0, 0)
        pairs_of(act, NT - 2, step)
        step(NT - 2, 0)
        step(NT - 1, 1, last=True)

    @block.vector
    def _(dve):
        dve.sem_inc(biased, 2)
        dve.tensor_copy(r_parts[:, :, 0], r).then_inc(r_chain, 1)
        dve.wait_ge(r_chain, 1)
        dve.tensor_tensor(r_rest[:, :], r, r_parts[:, :, 0], ALU.subtract).then_inc(r_chain, 1)
        dve.wait_ge(r_chain, 2)
        dve.tensor_copy(r_parts[:, :, 1], r_rest[:, :]).then_inc(r_chain, 1)
        dve.wait_ge(r_chain, 3)
        dve.tensor_tensor(r_parts[:, :, 2], r_rest[:, :], r_parts[:, :, 1], ALU.subtract).then_inc(r_chain, 1)

        def step(t, slot):
            dve.wait_ge(multiplied, t + 3)
            dve.tensor_tensor(h_sb[:, slot, :], h_ps[slot][:, 0:HID], b1_all[:, :], ALU.add).then_inc(biased, 1)
            dve.wait_ge(biased, t + 3)
            dve.tensor_scalar(g_sb[:, slot, :], h_sb[:, slot, :], r[:, bass.ds(t, 1)], None, ALU.mult)\
               .then_inc(chain, 1)
            dve.wait_ge(high, t + 1)
            dve.tensor_tensor(rest[:, slot, :], g_sb[:, slot, :], g_parts[:, bass.ds(t, 1), 0, :].squeeze(1),
                              ALU.subtract).then_inc(chain, 1)
            dve.wait_ge(middle, t + 1)
            dve.tensor_tensor(g_parts[:, bass.ds(t, 1), 2, :].squeeze(1), rest[:, slot, :],
                              g_parts[:, bass.ds(t, 1), 1, :].squeeze(1), ALU.subtract).then_inc(chain, 1)

        pairs_of(dve, NT, step)


def aggregate(nc, s, kind, a_t, parts, w_in, b_in, x_rows, out_rows, r, r_parts, eps_half, u_all=None, dots=None,
              r_in=None, eye_bf=None):
    n_parts, width = parts.shape[2], parts.shape[3]
    KC = width // P
    BANKS = KC // 2
    linear = kind == "linear"
    w_sb = s.sb("w_sb", [P, KC, D], FP32)
    agg_sb = s.sb("agg_sb", [P, 2, KC, BR], FP32)
    x_sb = s.sb("x_sb", [P, 2, D], FP32)
    z_sb = s.sb("z_sb", [P, 2, D], FP32)
    y_sb = s.sb("y_sb", [P, 2, D], FP32)
    xn_sb = s.sb("xn_sb", [P, 2, D], FP32)
    stats = s.sb("stats", [P, 2, 6], FP32)
    mean_var = s.sb("mean_var", [P, 2, 2], FP32)
    rstd = s.sb("rstd", [P, 2, 1], FP32)
    agg_ps = [[s.ps(f"agg_ps{i}{j}", [P, D]) for j in range(BANKS)] for i in range(2)]
    y_ps = [s.ps(f"y_ps{i}", [P, D]) for i in range(2)]
    w_loaded = s.sem("w_loaded")
    x_loaded = [s.sem(f"x_loaded{i}") for i in range(2)]
    gathered = s.sem("gathered")
    copied = s.sem("copied")
    multiplied = s.sem("multiplied")
    taken = s.sem("taken")
    added = s.sem("added")
    normed = s.sem("normed")
    stored = [s.sem(f"stored{i}") for i in range(2)]
    if linear:
        b_all = s.sb("b_all", [P, D], FP32)
        rho3 = s.sb("rho3", [P, NT, 3], FP32)
        rho = s.sb("rho", [P, NT], FP32)
        rho_ps = s.ps("rho_ps", [P, D])
        rho_done = s.sem("rho_done")
        rho_chain = s.sem("rho_chain")
        dotted = s.sem("dotted")
    else:
        rows_loaded = [s.sem(f"rows_loaded{i}") for i in range(2)]
        high = s.sem("high")
        low = s.sem("low")
        eyed = s.sem("eyed")
    block = s.block()

    @block.sync
    def _(sp):
        for t in range(2):
            sp.sem_inc(stored[t], 16)
        sp.dma_start(w_sb[:, :, :], w_in.rearrange("(k p) n -> p k n", p=P)).then_inc(w_loaded, 16)
        if linear:
            sp.dma_start(b_all[:, :], b_in.partition_broadcast(P)).then_inc(w_loaded, 16)

        def load(b, t):
            sp.dma_start(x_sb[:, t, :], x_rows[bass.ds(b * BR + t * P, P), :]).then_inc(x_loaded[t], 16)

        def step(b, last=False):
            for t in range(2):
                sp.wait_ge(normed, b * (2 * NORM_STEPS) + (t + 1) * NORM_STEPS)
                sp.dma_start(out_rows[bass.ds(b * BR + t * P, P), :], xn_sb[:, t, :]).then_inc(stored[t], 16)
                if not last:
                    load(b + 1, t)

        def load_rows(t, slot):
            sp.wait_ge(low, t + 1)
            sp.dma_start(x_sb[:, slot, :], x_rows[bass.ds(t * P, P), :]).then_inc(rows_loaded[slot], 16)

        if not linear:
            pairs_of(sp, NT, load_rows)
            sp.wait_ge(low, NT + 2)
        for t in range(2):
            load(0, t)
        with sp.Fori(0, NB - 1, 1) as b:
            step(b)
        step(NB - 1, last=True)
        for t in range(2):
            sp.wait_ge(stored[t], 16 * NB + 16)

    @block.gpsimd
    def _(pool):
        if not linear:
            for j in range(NT):
                diag = a_t[:, j, j * P:(j + 1) * P]
                pool.tensor_tensor(diag, diag, eye_bf, ALU.add).then_inc(eyed, 1)
        with pool.Fori(0, NB, 1) as b:
            for t in range(2):
                inv_std(pool, mean_var[:, t, :], rstd[:, t, :], eps_half, normed, b * (2 * NORM_STEPS) + t * NORM_STEPS)

    @block.tensor
    def _(pe):
        pe.sem_inc(multiplied, 2)
        if linear:
            with pe.Fori(0, NT, 1) as t:
                for j in range(NT):
                    mm = pe.matmul(rho_ps[:, bass.ds(t * 3, 3)], a_t[:, j, bass.ds(t * P, P)], r_parts[:, j, :],
                                   start=(j == 0), stop=(j == NT - 1))
                mm.then_inc(rho_done, 1)
        pe.wait_ge(w_loaded, 32 if linear else 16)

        def gather(b, slot, splitting=False):
            for c in range(KC):
                if c % 2 == 0:
                    pe.wait_ge(copied, b * BANKS + (c // 2 + 1))
                for j in range(NT):
                    if splitting and c == 0:
                        pe.wait_ge(low, j + 3)
                    for i in range(n_parts):
                        mm = pe.matmul(agg_ps[slot][c // 2][:, (c % 2) * BR:(c % 2 + 1) * BR],
                                       parts[:, j, i, c * P:(c + 1) * P], a_t[:, j, bass.ds(b * BR, BR)],
                                       start=(j == 0 and i == 0), stop=(j == NT - 1 and i == n_parts - 1))
                if c % 2 == 1:
                    mm.then_inc(gathered, 1)

        def step(b, slot, last=False):
            if not last:
                gather(b + 1, 1 - slot)
            pe.wait_ge(copied, b * BANKS + 3 * BANKS)
            for t in range(2):
                pe.wait_ge(taken, b * 2 + (t + 1))
                for k in range(KC):
                    mm = pe.matmul(y_ps[t][:, :], agg_sb[:, slot, k, t * P:(t + 1) * P], w_sb[:, k, :],
                                   start=(k == 0), stop=(k == KC - 1))
                mm.then_inc(multiplied, 1)

        if not linear:
            pe.wait_ge(eyed, NT)
        gather(0, 0, splitting=not linear)
        pairs_of(pe, NB - 1, step)
        step(NB - 1, 0, last=True)

    @block.scalar
    def _(act):
        act.sem_inc(copied, 2 * BANKS)

        def high_part(t, slot):
            act.wait_ge(rows_loaded[slot], (t - slot) * 8 + 16)
            act.activation(parts[:, bass.ds(t, 1), 0, :].squeeze(1), x_sb[:, slot, :], ACT.Copy,
                           scale=r_in[:, bass.ds(t, 1)]).then_inc(high, 1)

        if not linear:
            act.sem_inc(taken, 2)
            pairs_of(act, NT, high_part)

        def copy(b, slot):
            for i in range(BANKS):
                act.wait_ge(gathered, b * BANKS + (i + 1))
                act.wait_ge(multiplied, b * 2)
                act.activation(agg_sb[:, slot, 2 * i:2 * i + 2, :].rearrange("p k n -> p (k n)"),
                               agg_ps[slot][i][:, :], ACT.Copy).then_inc(copied, 1)

        def step(b, slot, last=False):
            if not last:
                copy(b + 1, 1 - slot)
            if not linear:
                for t in range(2):
                    act.wait_ge(multiplied, b * 2 + (t + 3))
                    act.wait_ge(added, b * 2 + (t + 1))
                    act.activation(y_sb[:, t, :], y_ps[t][:, :], ACT.Relu,
                                   scale=r[:, bass.ds(b * 2 + t, 1)]).then_inc(taken, 1)

        copy(0, 0)
        pairs_of(act, NB - 1, step)
        step(NB - 1, 0, last=True)

    @block.vector
    def _(dve):
        dve.sem_inc(added, 2)
        if linear:
            dve.sem_inc(taken, 2)
            dve.wait_ge(rho_done, NT)
            dve.tensor_copy(rho3[:, :, :].rearrange("p t i -> p (t i)"), rho_ps[:, 0:3 * NT]).then_inc(rho_chain, 1)
            dve.wait_ge(rho_chain, 1)
            dve.tensor_reduce(rho[:, :], rho3[:, :, :], AXX, ALU.add).then_inc(rho_chain, 1)
            dve.wait_ge(rho_chain, 2)
            dve.tensor_tensor(rho[:, :], rho[:, :], r, ALU.mult).then_inc(rho_chain, 1)
            dve.wait_ge(rho_chain, 3)
            dve.sem_inc(dotted, 2)
        else:
            dve.sem_inc(low, 2)

        def low_part(t, slot):
            dve.wait_ge(high, t + 1)
            dve.scalar_tensor_tensor(parts[:, bass.ds(t, 1), 1, :].squeeze(1), x_sb[:, slot, :],
                                     r_in[:, bass.ds(t, 1)], parts[:, bass.ds(t, 1), 0, :].squeeze(1), ALU.mult,
                                     ALU.subtract).then_inc(low, 1)

        if not linear:
            pairs_of(dve, NT, low_part)

        with dve.Fori(0, NB, 1) as b:
            for t in range(2):
                dve.wait_ge(x_loaded[t], b * 16 + 16)
                if linear:
                    dve.wait_ge(dotted, b * 2 + (t + 1))
                    dve.wait_ge(multiplied, b * 2 + (t + 3))
                    dve.scalar_tensor_tensor(y_sb[:, t, :], y_ps[t][:, :], r[:, bass.ds(b * 2 + t, 1)], x_sb[:, t, :],
                                             ALU.mult, ALU.add).then_inc(taken, 1)
                    dve.wait_ge(taken, b * 2 + (t + 3))
                    dve.scalar_tensor_tensor(z_sb[:, t, :], b_all[:, :], rho[:, bass.ds(b * 2 + t, 1)], y_sb[:, t, :],
                                             ALU.mult, ALU.add).then_inc(added, 1)
                else:
                    dve.wait_ge(taken, b * 2 + (t + 3))
                    dve.tensor_tensor(z_sb[:, t, :], y_sb[:, t, :], x_sb[:, t, :], ALU.add).then_inc(added, 1)
                dve.wait_ge(added, b * 2 + (t + 3))
                dve.wait_ge(stored[t], b * 16 + 16)
                layer_norm(dve, z_sb[:, t, :], stats[:, t, :], mean_var[:, t, :], rstd[:, t, :], xn_sb[:, t, :],
                           normed, b * (2 * NORM_STEPS) + t * NORM_STEPS)
                if linear:
                    dve.wait_ge(normed, b * (2 * NORM_STEPS) + (t + 1) * NORM_STEPS)
                    for i, products in enumerate((y_sb, z_sb)):
                        dot = dve.scalar_tensor_tensor(products[:, t, :], xn_sb[:, t, :], 1.0, u_all[:, i, :],
                                                       ALU.mult, ALU.mult,
                                                       accum_out=dots[:, i, bass.ds(b * 2 + t, 1)])
                    dot.then_inc(dotted, 1)


LEAK = 0.2
NO_EDGE = -9e15


def edge_vectors(nc, s, w_cat, a_w, u_scratch, u_all, eye):
    w_sb = s.sb("w_sb", [P, 2 * KT, D], FP32)
    a_all = s.sb("a_all", [P, D], FP32)
    product = s.sb("product", [P, D], FP32)
    u_col = s.sb("u_col", [P, 2 * KT], FP32)
    u_row = s.sb("u_row", [2 * KT, P], FP32)
    turn_ps = s.ps("turn_ps", [2 * KT, P])
    loaded = s.sem("loaded")
    dotted = s.sem("dotted")
    turned = s.sem("turned")
    turned_out = s.sem("turned_out")
    moved = s.sem("moved")
    block = s.block()

    @block.sync
    def _(sp):
        sp.dma_start(a_all[:, :], a_w.partition_broadcast(P)).then_inc(loaded, 16)
        sp.dma_start(w_sb[:, :, :], w_cat.rearrange("(k p) n -> p k n", p=P)).then_inc(loaded, 16)
        sp.wait_ge(turned_out, 1)
        sp.dma_start(u_scratch.rearrange("(k p) -> k p", p=P), u_row[:, :]).then_inc(moved, 16)
        sp.wait_ge(moved, 16)
        sp.dma_start(u_all.rearrange("p i n -> p (i n)"), u_scratch.partition_broadcast(P)).then_inc(moved, 16)
        sp.wait_ge(moved, 32)

    @block.vector
    def _(dve):
        dve.wait_ge(loaded, 32)
        for k in range(2 * KT):
            if k:
                dve.wait_ge(dotted, k)
            dve.tensor_tensor_reduce(out=product[:, :], in0=w_sb[:, k, :], in1=a_all[:, :], scale=1.0, scalar=0.0,
                                     op0=ALU.mult, op1=ALU.add, accum_out=u_col[:, k:k + 1]).then_inc(dotted, 1)
        dve.wait_ge(turned, 1)
        dve.tensor_copy(u_row[:, :], turn_ps[:, :]).then_inc(turned_out, 1)

    @block.tensor
    def _(pe):
        pe.wait_ge(dotted, 2 * KT)
        pe.transpose(turn_ps[:, :], u_col[:, :], eye).then_inc(turned, 1)


def row_shifts(nc, s, x_rows, x_parts, a_t, eye, eye_bf, dots, a_b, s_cols, shift_scratch):
    x_sb = s.sb("x_sb", [P, 2, D], FP32)
    x_loaded = [s.sem(f"x_loaded{i}") for i in range(2)]
    high = s.sem("high")
    low = s.sem("low")
    bias = s.sb("bias", [P, 2, NP], BF16)
    most = s.sb("most", [P, NP], FP32)
    ab_all = s.sb("ab_all", [P, 1], FP32)
    best = s.sb("best", [P, NT], FP32)
    s1b = s.sb("s1b", [P, NT], FP32)
    s1b_leak = s.sb("s1b_leak", [P, NT], FP32)
    z = s.sb("z", [P, NT], FP32)
    m = s.sb("m", [P, NT], FP32)
    shifts = s.sb("shifts", [P, 2 * NT], FP32)
    shifts_T = s.sb("shifts_T", [2 * NT, P], FP32)
    t_ps = [s.ps(f"t_ps{i}", [P, D]) for i in range(2)]
    st_ps = s.ps("st_ps", [2 * NT, P])
    ab_loaded = s.sem("ab_loaded")
    uneyed = s.sem("uneyed")
    biased = s.sem("biased")
    maxed = s.sem("maxed")
    turned = s.sem("turned")
    reduced = s.sem("reduced")
    chain = s.sem("chain")
    st_done = s.sem("st_done")
    st_copied = s.sem("st_copied")
    stored = s.sem("stored")
    block = s.block()
    BANKS = [(c, min(c + 4, NT)) for c in range(0, NT, 4)]

    @block.sync
    def _(sp):
        sp.dma_start(ab_all[:, :], a_b.partition_broadcast(P)).then_inc(ab_loaded, 16)

        def load_rows(t, slot):
            sp.wait_ge(low, t + 1)
            sp.dma_start(x_sb[:, slot, :], x_rows[bass.ds(t * P, P), :]).then_inc(x_loaded[slot], 16)

        pairs_of(sp, NT, load_rows)
        sp.wait_ge(st_copied, 1)
        sp.dma_start(shift_scratch.rearrange("(t p) -> t p", p=P), shifts_T[:, :]).then_inc(stored, 16)
        sp.wait_ge(stored, 16)

    @block.scalar
    def _(act):
        act.wait_ge(uneyed, NT)

        def step(j, slot):
            act.wait_ge(maxed, j + 1)
            act.activation(bias[:, slot, :], a_t[:, bass.ds(j, 1), :].squeeze(1), ACT.Copy, scale=-NO_EDGE,
                           bias=NO_EDGE).then_inc(biased, 1)
            act.wait_ge(x_loaded[slot], (j - slot) * 8 + 16)
            act.activation(x_parts[:, bass.ds(j, 1), 0, :].squeeze(1), x_sb[:, slot, :], ACT.Copy, scale=X_TOP)\
               .then_inc(high, 1)

        pairs_of(act, NT, step)
        act.wait_ge(st_done, 1)
        act.activation(shifts_T[:, :], st_ps[:, :], ACT.Copy).then_inc(st_copied, 1)

    @block.vector
    def _(dve):
        dve.memset(most[:, :], -3e38).then_inc(maxed, 2)
        for j in range(NT):
            diag = a_t[:, j, j * P:(j + 1) * P]
            dve.tensor_tensor(diag, diag, eye_bf, ALU.subtract).then_inc(uneyed, 1)

        def step(j, slot):
            dve.wait_ge(biased, j + 1)
            dve.wait_ge(maxed, j + 2)
            dve.scalar_tensor_tensor(most[:, :], bias[:, slot, :], dots[:, 1, bass.ds(j, 1)], most[:, :], ALU.add,
                                     ALU.max).then_inc(maxed, 1)
            dve.wait_ge(high, j + 1)
            dve.scalar_tensor_tensor(x_parts[:, bass.ds(j, 1), 1, :].squeeze(1), x_sb[:, slot, :], X_TOP,
                                     x_parts[:, bass.ds(j, 1), 0, :].squeeze(1), ALU.mult, ALU.subtract)\
               .then_inc(low, 1)

        dve.sem_inc(low, 2)
        pairs_of(dve, NT, step)
        for i, (a, z_) in enumerate(BANKS):
            dve.wait_ge(turned, i + 1)
            dve.tensor_reduce(best[:, a:z_], t_ps[i % 2][:, 0:(z_ - a) * P].rearrange("p (t c) -> p t c", c=P), AXX,
                              ALU.max).then_inc(reduced, 1)
        dve.wait_ge(reduced, len(BANKS))
        dve.wait_ge(ab_loaded, 16)
        dve.tensor_scalar(s1b[:, :], dots[:, 0, :], ab_all[:, :], None, ALU.add).then_inc(chain, 1)
        dve.wait_ge(chain, 1)
        dve.tensor_tensor(z[:, :], s1b[:, :], best[:, :], ALU.add).then_inc(chain, 1)
        dve.tensor_scalar(s1b_leak[:, :], s1b[:, :], LEAK, None, ALU.mult).then_inc(chain, 1)
        dve.wait_ge(chain, 2)
        dve.scalar_tensor_tensor(m[:, :], z[:, :], LEAK, z[:, :], ALU.mult, ALU.max).then_inc(chain, 1)
        dve.wait_ge(chain, 4)
        dve.tensor_tensor(shifts[:, 0:NT], s1b[:, :], m[:, :], ALU.subtract)
        dve.tensor_tensor(shifts[:, NT:2 * NT], s1b_leak[:, :], m[:, :], ALU.subtract).then_inc(chain, 1)
        dve.tensor_copy(s_cols[:, 0, :], dots[:, 1, :])
        dve.tensor_scalar(s_cols[:, 1, :], dots[:, 1, :], LEAK, None, ALU.mult)

    @block.tensor
    def _(pe):
        pe.wait_ge(maxed, NT + 2)
        for i, (a, z_) in enumerate(BANKS):
            if i >= 2:
                pe.wait_ge(reduced, i - 1)
            for t in range(a, z_):
                mm = pe.transpose(t_ps[i % 2][:, (t - a) * P:(t - a + 1) * P], most[:, t * P:(t + 1) * P], eye)
            mm.then_inc(turned, 1)
        pe.wait_ge(chain, 5)
        pe.transpose(st_ps[:, :], shifts[:, :], eye).then_inc(st_done, 1)


PRODUCT_AT = (3, 6)
SUMS_AT = 3
FINISH_AT = (6, 9)


def attend(nc, s, a_t, x_parts, s_cols, shift_scratch, fc_w, fc_b, x_rows, out_rows, eps_half):
    RING = 3
    w_sb = s.sb("w_sb", [P, KT, D], FP32)
    fcb_all = s.sb("fcb_all", [P, D], FP32)
    shift = s.sb("shift", [P, 2, 2, BR], FP32)
    e_hi = s.sb("e_hi", [P, RING, 2, BR], FP32)
    e_leak = s.sb("e_leak", [P, 2, 2, BR], FP32)
    p_hi = s.sb("p_hi", [P, 2, 2, BR], FP16)
    p_lo = s.sb("p_lo", [P, 2, 2, BR], FP16)
    row_sum = s.sb("row_sum", [P, 2, 2, BR], FP32)
    ones = s.sb("ones", [P, 1], FP32)
    s_scaled = s.sb("s_scaled", [P, 2], FP32)
    s_inv = s.sb("s_inv", [P, 2], FP32)
    agg_sb = s.sb("agg_sb", [P, KT, BR], FP32)
    x_sb = s.sb("x_sb", [P, D], FP32)
    xn_sb = s.sb("xn_sb", [P, D], FP32)
    stats = s.sb("stats", [P, 6], FP32)
    mean_var = s.sb("mean_var", [P, 2], FP32)
    rstd = s.sb("rstd", [P, 1], FP32)
    agg_ps = [[s.ps(f"agg_ps{i}{j}", [P, D]) for j in range(2)] for i in range(2)]
    y_ps = [s.ps(f"y_ps{i}", [P, D]) for i in range(2)]
    sum_ps = s.ps("sum_ps", [P, 2])
    w_loaded = s.sem("w_loaded")
    shift_loaded = [s.sem(f"shift_loaded{i}") for i in range(2)]
    x_loaded = s.sem("x_loaded")
    exped = s.sem("exped")
    maxed = s.sem("maxed")
    weighed = s.sem("weighed")
    high = s.sem("high")
    split = s.sem("split")
    summed = s.sem("summed")
    used = s.sem("used")
    sums_done = s.sem("sums_done")
    copied = s.sem("copied")
    multiplied = s.sem("multiplied")
    taken = s.sem("taken")
    added = s.sem("added")
    inverse = s.sem("inverse")
    ones_set = s.sem("ones_set")
    normed = s.sem("normed")
    stored = s.sem("stored")
    block = s.block()
    GP = NT // 2

    def freed(g):
        return g + 1 if g < 2 else g

    def peeled(e, first, step):
        first()
        pairs_of(e, NB - 1, step)
        step(NB - 1, 0, last=True)

    @block.sync
    def _(sp):
        sp.sem_inc(stored, 16)
        sp.dma_start(w_sb[:, :, :], fc_w.rearrange("(k p) n -> p k n", p=P)).then_inc(w_loaded, 16)
        sp.dma_start(fcb_all[:, :], fc_b.partition_broadcast(P)).then_inc(w_loaded, 16)

        def load_shift(b, slot):
            for i in range(2):
                sp.dma_start(shift[:, slot, i, :], shift_scratch[bass.ds(b * BR + i * NP, BR)].partition_broadcast(P))\
                  .then_inc(shift_loaded[slot], 16)

        def step(b, slot, last=False):
            if not last:
                sp.wait_ge(exped, b * GP + GP)
                load_shift(next_block(b + 2), slot)
            for t in range(2):
                sp.dma_start(x_sb[:, :], x_rows[bass.ds(b * BR + t * P, P), :]).then_inc(x_loaded, 16)
                sp.wait_ge(normed, b * (2 * NORM_STEPS) + (t + 1) * NORM_STEPS)
                sp.dma_start(out_rows[bass.ds(b * BR + t * P, P), :], xn_sb[:, :]).then_inc(stored, 16)

        load_shift(0, 0)
        load_shift(1, 1)
        pairs_of(sp, NB - 1, step)
        step(NB - 1, 0, last=True)
        sp.wait_ge(stored, 32 * NB + 16)
        for i in range(2):
            sp.wait_ge(shift_loaded[i], 32 * (NB // 2 + 1))

    @block.scalar
    def _(act):
        act.sem_inc(copied, 4)

        def high_part(b, slot, g):
            ring = (slot + g) % 2
            act.wait_ge(weighed, b * GP + (g + 1))
            act.wait_ge(used, b * GP + (g + 1))
            act.activation(p_hi[:, ring, :, :], e_hi[:, g % RING, :, :], ACT.Copy, scale=P_TOP).then_inc(high, 1)

        def exps(b, slot, between=None):
            for g in range(GP):
                ring = (slot + g) % 2
                if g == 0:
                    act.wait_ge(shift_loaded[slot], (b - slot) * 16 + 32)
                act.wait_ge(split, b * GP + freed(g))
                act.wait_ge(summed, b * GP + freed(g))
                act.wait_ge(maxed, b * GP + (g + 1))
                for j in range(2):
                    for i, e in enumerate((e_hi[:, g % RING], e_leak[:, ring])):
                        done = act.activation(e[:, j, :], shift[:, slot, i, :], ACT.Exp,
                                              bias=s_cols[:, i, 2 * g + j:2 * g + j + 1])
                done.then_inc(exped, 1)
                if g > 0:
                    high_part(b, slot, g - 1)
                if g == 2 and between:
                    between()
            high_part(b, slot, GP - 1)

        def copy(b, slot):
            act.wait_ge(used, b * GP + (GP + 2))
            act.wait_ge(multiplied, b * 2 + 1)
            for i in range(2):
                act.activation(agg_sb[:, 2 * i:2 * i + 2, :].rearrange("p k n -> p (k n)"), agg_ps[slot][i][:, :],
                               ACT.Copy).then_inc(copied, 1)

        def step(b, slot, last=False):
            if last:
                copy(b, slot)
            else:
                exps(b + 1, 1 - slot, between=lambda: copy(b, slot))

        peeled(act, lambda: exps(0, 0), step)

    @block.gpsimd
    def _(pool):
        pool.sem_inc(summed, 2)

        def step(b, slot, between=None):
            flat = row_sum[:, slot]
            for g in range(GP):
                ring = (slot + g) % 2
                pool.wait_ge(weighed, b * GP + (g + 1))
                if g == 0:
                    if slot == 1 or not isinstance(b, int):
                        pool.wait_ge(sums_done, b)
                    pool.nop(nofuse=True)
                    pool.tensor_copy(flat, e_hi[:, g % RING, :, :]).then_inc(summed, 1)
                else:
                    pool.wait_ge(summed, b * GP + (g + 2))
                    pool.tensor_tensor(flat, flat, e_hi[:, g % RING, :, :], ALU.add).then_inc(summed, 1)
                if between:
                    between(g)

        def norm(b, t):
            inv_std(pool, mean_var[:, :], rstd[:, :], eps_half, normed, b * (2 * NORM_STEPS) + t * NORM_STEPS)

        def both(b, slot, last=False):
            if last:
                norm(b, 0)
                norm(b, 1)
            else:
                step(b + 1, 1 - slot, lambda g: norm(b, FINISH_AT.index(g)) if g in FINISH_AT else None)

        peeled(pool, lambda: step(0, 0), both)

    @block.vector
    def _(dve):
        dve.sem_inc(added, 1)
        dve.sem_inc(inverse, 1)
        dve.sem_inc(split, 2)
        dve.sem_inc(maxed, 2)
        dve.sem_inc(taken, 2)
        dve.memset(ones[:, :], 1.0).then_inc(ones_set, 1)

        def weigh(b, slot, g):
            ring = (slot + g) % 2
            dve.wait_ge(exped, b * GP + (g + 1))
            dve.tensor_tensor(e_hi[:, g % RING, :, :], e_hi[:, g % RING, :, :], e_leak[:, ring, :, :], ALU.max)\
               .then_inc(maxed, 1)
            dve.wait_ge(maxed, b * GP + (g + 3))
            dve.scalar_tensor_tensor(e_hi[:, g % RING, :, :], e_hi[:, g % RING, :, :], 1.0,
                                     a_t[:, 2 * g:2 * g + 2, bass.ds(b * BR, BR)], ALU.min, ALU.mult)\
               .then_inc(weighed, 1)

        def low_part(b, slot, g):
            ring = (slot + g) % 2
            dve.wait_ge(high, b * GP + (g + 1))
            dve.scalar_tensor_tensor(p_lo[:, ring, :, :], e_hi[:, g % RING, :, :], P_TOP, p_hi[:, ring, :, :], ALU.mult,
                                     ALU.subtract).then_inc(split, 1)

        def weights(b, slot, between=None):
            for g in range(GP):
                weigh(b, slot, g)
                if g > 0:
                    low_part(b, slot, g - 1)
                if between:
                    between(g)
            low_part(b, slot, GP - 1)

        def inverse_sums(b):
            dve.wait_ge(sums_done, b + 2)
            dve.tensor_scalar(s_scaled[:, :], sum_ps[:, :], P_TOP * X_TOP, None, ALU.mult).then_inc(inverse, 1)
            dve.wait_ge(inverse, b * 2 + 2)
            dve.reciprocal(s_inv[:, :], s_scaled[:, :]).then_inc(inverse, 1)
            dve.wait_ge(inverse, b * 2 + 3)

        def finish(b, t):
            dve.wait_ge(multiplied, b * 2 + (t + 2))
            dve.wait_ge(x_loaded, b * 32 + (t + 1) * 16)
            dve.scalar_tensor_tensor(x_sb[:, :], y_ps[t][:, :], s_inv[:, t:t + 1], x_sb[:, :], ALU.mult, ALU.add)\
               .then_inc(taken, 1)
            dve.wait_ge(taken, b * 2 + (t + 3))
            dve.tensor_tensor(x_sb[:, :], x_sb[:, :], fcb_all[:, :], ALU.add).then_inc(added, 1)
            dve.wait_ge(added, b * 2 + (t + 2))
            dve.wait_ge(stored, b * 32 + (t + 1) * 16)
            layer_norm(dve, x_sb[:, :], stats[:, :], mean_var[:, :], rstd[:, :], xn_sb[:, :], normed,
                       b * (2 * NORM_STEPS) + t * NORM_STEPS)

        def step(b, slot, last=False):
            def between(g):
                if g == SUMS_AT:
                    inverse_sums(b)
                if g in FINISH_AT:
                    finish(b, FINISH_AT.index(g))

            if last:
                inverse_sums(b)
                finish(b, 0)
                finish(b, 1)
            else:
                weights(b + 1, 1 - slot, between)

        dve.wait_ge(w_loaded, 32)
        peeled(dve, lambda: weights(0, 0), step)

    @block.tensor
    def _(pe):
        pe.sem_inc(sums_done, 1)
        pe.sem_inc(multiplied, 1)
        pe.sem_inc(used, 2)
        pe.wait_ge(w_loaded, 32)
        pe.wait_ge(ones_set, 1)

        def gather(b, slot, between=None):
            pe.wait_ge(copied, b * 2 + 2)
            for g in range(GP):
                ring = (slot + g) % 2
                pe.wait_ge(split, b * GP + (g + 3))
                for c in range(KT):
                    for j in range(2):
                        for n, (x_part, p) in enumerate(((0, p_hi), (1, p_hi), (0, p_lo))):
                            first, last = (g == 0 and j == 0 and n == 0), (g == GP - 1 and j == 1 and n == 2)
                            mm = pe.matmul(agg_ps[slot][c // 2][:, (c % 2) * BR:(c % 2 + 1) * BR],
                                           x_parts[:, 2 * g + j, x_part, c * P:(c + 1) * P], p[:, ring, j, :],
                                           start=first and c % 2 == 0, stop=last, skip_group_check=True)
                mm.then_inc(used, 1)
                if between:
                    between(g)
            pe.wait_ge(inverse, b * 2 + 1)
            pe.wait_ge(summed, b * GP + (GP + 2))
            for t in range(2):
                for j in range(2):
                    mm = pe.matmul(sum_ps[:, t:t + 1], row_sum[:, slot, j, t * P:(t + 1) * P], ones[:, :],
                                   start=(j == 0), stop=(j == 1))
            mm.then_inc(sums_done, 1)

        def product(b, t):
            pe.wait_ge(copied, b * 2 + 6)
            pe.wait_ge(taken, b * 2 + (t + 1))
            for k in range(KT):
                mm = pe.matmul(y_ps[t][:, :], agg_sb[:, k, t * P:(t + 1) * P], w_sb[:, k, :],
                               start=(k == 0), stop=(k == KT - 1))
            mm.then_inc(multiplied, 1)

        def step(b, slot, last=False):
            if last:
                product(b, 0)
                product(b, 1)
            else:
                gather(b + 1, 1 - slot, lambda g: product(b, PRODUCT_AT.index(g)) if g in PRODUCT_AT else None)

        peeled(pe, lambda: gather(0, 0), step)


def constants(nc, s, eye_in, fold_in, eye, eye_bf, fold, eps_half):
    loaded = s.sem("loaded")
    block = s.block()

    @block.sync
    def _(sp):
        sp.dma_start(eye, eye_in).then_inc(loaded, 16)
        sp.dma_start(fold, fold_in).then_inc(loaded, 16)

    @block.vector
    def _(dve):
        dve.memset(eps_half[:, 0:1], EPS)
        dve.memset(eps_half[:, 1:2], -0.5)
        dve.wait_ge(loaded, 32)
        dve.tensor_copy(eye_bf, eye)


def four_layers(nc, x, xT, adj, adjT, wqkv, wo, w1T, b1, w2T, b2, w_cat, a_w, a_b, fc_w, fc_b, w3, eye_in, fold_in,
                out):
    def scratch(name, shape, dt):
        return nc.dram_tensor(name, shape, dt, kind="Internal").ap()

    qk_parts = scratch("qk_parts", [2, 2, D, NP], FP32)
    v_parts = scratch("v_parts", [H, P, NT * P], FP16)
    o_rows = scratch("o_rows", [NP + BR, D], FP32)
    adjT_bf = scratch("adjT_bf", [NP, NP], BF16)
    x1, x2, x3 = (scratch(f"x{i}_rows", [NP, D], FP32) for i in (1, 2, 3))
    u_scratch = scratch("u_scratch", [2 * D], FP32)
    shift_scratch = scratch("shift_scratch", [2 * NP], FP32)

    with Scope(nc, "kept") as kept:
        eye = kept.sb("eye", [P, P], FP32)[:, :]
        eye_bf = kept.sb("eye_bf", [P, P], BF16)[:, :]
        fold = kept.sb("fold", [P, HD], FP32)[:, :]
        eps_half = kept.sb("eps_half", [P, 2], FP32)
        v_inv = kept.sb("v_inv", [P, 1], FP32)[:, :]
        deg = kept.sb("deg", [P, NT], FP32)[:, :]
        r = kept.sb("r", [P, NT], FP32)[:, :]
        r_in = kept.sb("r_in", [P, NT], FP32)[:, :]
        r_out = kept.sb("r_out", [P, NT], FP32)[:, :]
        dots = kept.sb("dots", [P, 2, NT], FP32)
        s_cols = kept.sb("s_cols", [P, 2, NT], FP32)
        with Scope(nc, "constants") as s:
            constants(nc, s, eye_in, fold_in, eye, eye_bf, fold, eps_half)

        with Scope(nc, "values") as values:
            v_all = values.sb("v_all", [P, NT * D], FP32)[:, :]
            with Scope(nc, "project") as s:
                project_qkv(nc, s, xT, wqkv, qk_parts, v_all)
            with Scope(nc, "split_v") as s:
                split_values(nc, s, v_all, v_parts, eye, v_inv)
        with Scope(nc, "attention") as s:
            attention(nc, s, adj, qk_parts, v_parts, o_rows, eye, fold, v_inv, deg, adjT, adjT_bf)
        a_t = kept.sb("a_t", [P, NT, NP], BF16)
        with Scope(nc, "project_out") as s:
            project_out(nc, s, x, o_rows, wo, x1, adjT_bf, a_t, eye, eps_half)

        with Scope(nc, "degrees") as s:
            degrees(nc, s, a_t, eye_bf, deg, r, r_in, r_out, eps_half)
        with Scope(nc, "vectors") as vectors:
            u_all = vectors.sb("u_all", [P, 2, D], FP32)
            g_parts = vectors.sb("g_parts", [P, NT, 3, w1T.shape[1]], BF16)
            r_parts = vectors.sb("r_parts", [P, NT, 3], BF16)
            with Scope(nc, "edge_vectors") as s:
                edge_vectors(nc, s, w_cat, a_w, u_scratch, u_all[:, :, :], eye)
            with Scope(nc, "hidden_rows") as s:
                hidden_rows(nc, s, x1, w1T, b1, r, g_parts, r_parts, eye)
            with Scope(nc, "linear") as s:
                aggregate(nc, s, "linear", a_t, g_parts, w2T, b2, x1, x2, r, r_parts, eps_half, u_all=u_all,
                          dots=dots)

        with Scope(nc, "rows") as rows:
            x_parts = rows.sb("x_parts", [P, NT, 2, D], FP16)
            with Scope(nc, "row_shifts") as s:
                row_shifts(nc, s, x2, x_parts, a_t, eye, eye_bf, dots, a_b, s_cols, shift_scratch)
            with Scope(nc, "attend") as s:
                attend(nc, s, a_t, x_parts, s_cols, shift_scratch, fc_w, fc_b, x2, x3, eps_half)

            with Scope(nc, "relu") as s:
                aggregate(nc, s, "relu", a_t, x_parts, w3, None, x3, out, r_out, None, eps_half, r_in=r_in,
                          eye_bf=eye_bf)


def kernel(**inputs):
    import numpy as _np
    import concourse.bacc as _bacc
    from concourse import mybir as _mybir
    from concourse.bass_utils import run_bass_kernel_spmd as _run

    a = {name: _np.asarray(value) for name, value in inputs.items()}
    f32 = _np.float32

    def rows_padded(m, columns):
        out = _np.zeros((NP, columns), f32)
        out[:m.shape[0], :m.shape[1]] = m
        return out

    adjT = rows_padded(a["adj"].T, NP)
    adjT[N:, N:] = _np.eye(NP - N, dtype=f32)
    x = rows_padded(a["x"], D)
    arrays = {
        "x": x,
        "xT": x.T,
        "adj": rows_padded(a["adj"], NP),
        "adjT": adjT,
        "wqkv": _np.stack([a[f"L0_gnn_{w}"].transpose(1, 0, 2).reshape(D, D) for w in ("Wqs", "Wks", "Wvs")]),
        "wo": a["L0_gnn_Wo"].reshape(D, D),
        "w1T": a["L1_gnn_W1"].T,
        "b1": a["L1_gnn_b1"],
        "w2T": a["L1_gnn_W2"].T,
        "b2": a["L1_gnn_b2"],
        "w_cat": a["L2_gnn_W"],
        "a_w": a["L2_gnn_a_w"],
        "a_b": a["L2_gnn_a_b"].reshape(1),
        "fc_w": a["L2_gnn_fc_w"],
        "fc_b": a["L2_gnn_fc_b"],
        "w3": a["L3_gnn_W"],
        "eye_in": _np.eye(P, dtype=f32),
        "fold_in": _np.vstack([_np.eye(HD, dtype=f32)] * 2),
    }
    arrays = {name: _np.ascontiguousarray(value) for name, value in arrays.items()}

    nc = _bacc.Bacc("TRN2", target_bir_lowering=False, num_devices=1)
    args = {name: nc.dram_tensor(name, v.shape, _mybir.dt.from_np(v.dtype), kind="ExternalInput").ap()
            for name, v in arrays.items()}
    out = nc.dram_tensor("out", (NP, D), _mybir.dt.float32, kind="ExternalOutput").ap()
    four_layers(nc, out=out, **args)
    result = _run(nc, [arrays], core_ids=[0])
    return result.results[0]["out"][:N]
```

```python
import concourse.bass as bass
from concourse import mybir
from contextlib import ExitStack

FP32 = mybir.dt.float32
FP32R = mybir.dt.float32r
FP16 = mybir.dt.float16
BF16 = mybir.dt.bfloat16
ALU = mybir.AluOpType
ACT = mybir.ActivationFunctionType
AXX = mybir.AxisListType.X

P = 128
N = 2708
D = 512
KT = D // P
NT = -(-N // P)
NP = NT * P
BR = 2 * P
NB = NP // BR
H = 8
HD = D // H
PASSES3 = ((0, 0), (0, 1), (1, 0))

V_TOP = 8192.0
P_TOP = 4096.0
MASKED = -1e16


class Scope:

    def __init__(self, nc, stage):
        self.nc, self.stage = nc, stage
        self.stack = ExitStack()

    def __enter__(self):
        return self

    def __exit__(self, *a):
        self.stack.close()

    def sb(self, name, shape, dt):
        return self.stack.enter_context(self.nc.sbuf_tensor(f"{self.stage}_{name}", shape, dt))

    def ps(self, name, shape, dt=FP32):
        return self.stack.enter_context(self.nc.psum_tensor(f"{self.stage}_{name}", shape, dt))

    def sem(self, name):
        return self.stack.enter_context(self.nc.semaphore(f"{self.stage}_{name}"))

    def block(self):
        return self.stack.enter_context(self.nc.Block())



def pairs_of(e, count, step):
    with e.Fori(0, count // 2, 1) as n:
        step(n * 2, 0)
        step(n * 2 + 1, 1)
    if count % 2:
        step(count - 1, 0)


def rings_of(e, count, ring, step):
    with e.Fori(0, count // ring, 1) as n:
        for i in range(ring):
            step(n * ring + i, i)
    for b in range(count // ring * ring, count):
        step(b, b % ring)


class RowSplit:

    def __init__(self, s, slots, x_rows, parts, scale_of):
        self.slots, self.x_rows, self.parts, self.scale_of = slots, x_rows, parts, scale_of
        self.ring = len(slots)
        self.rows_loaded = [s.sem(f"rows_loaded{i}") for i in range(self.ring)]
        self.high = s.sem("high")
        self.low = s.sem("low")

    def load(self, sp, b, slot):
        sp.wait_ge(self.low, b * 2 + 2)
        sp.dma_start(self.slots[slot], self.x_rows[bass.ds(b * BR, BR), :].rearrange("(t p) c -> p t c", p=P))\
            .then_inc(self.rows_loaded[slot], 16)

    def high_parts(self, act, b, slot):
        act.wait_ge(self.rows_loaded[slot], (b - slot) * (16 // self.ring) + 16)
        for t in range(2):
            tile = bass.ds(b * 2 + t, 1)
            act.activation(self.parts[:, tile, 0, :].squeeze(1), self.slots[slot][:, t, :], ACT.Copy,
                           scale=self.scale_of(tile)).then_inc(self.high, 1)

    def low_parts(self, dve, b, slot):
        for t in range(2):
            tile = bass.ds(b * 2 + t, 1)
            dve.wait_ge(self.high, b * 2 + (t + 1))
            dve.scalar_tensor_tensor(self.parts[:, tile, 1, :].squeeze(1), self.slots[slot][:, t, :],
                                     self.scale_of(tile), self.parts[:, tile, 0, :].squeeze(1), ALU.mult,
                                     ALU.subtract).then_inc(self.low, 1)


def next_block(v):
    span = NB.bit_length()
    past = (v + ((1 << span) - NB)) >> span
    return v - past * NB if isinstance(v, int) else (v - past * NB).with_bounds(min_val=0, max_val=NB - 1)


def project_qkv(nc, s, xT, wqkv, qk_parts, v_all, v_tops, w_cat, a_w, u_scratch, eye):
    RING = 4
    M = 2 * KT
    NEXT_AT = 4
    w_raw = s.sb("w_raw", [P, 3, KT, D], FP32)
    w_hi = s.sb("w_hi", [P, 3, KT, D], FP32R)
    w_lo = s.sb("w_lo", [P, 3, KT, D], FP32R)
    x_raw = s.sb("x_raw", [P, 2, KT, BR], FP32)
    x_hi = s.sb("x_hi", [P, 2, KT, BR], FP32R)
    x_lo = s.sb("x_lo", [P, 2, KT, BR], FP32R)
    out_hi = s.sb("out_hi", [P, RING, BR], FP32R)
    out_lo = s.sb("out_lo", [P, RING, BR], FP32R)
    w_cat_sb = s.sb("w_cat_sb", [P, 2 * KT, D], FP32)
    a_all = s.sb("a_all", [P, D], FP32)
    product = s.sb("product", [P, D], FP32)
    u_col = s.sb("u_col", [P, 2 * KT], FP32)
    u_row = s.sb("u_row", [2 * KT, P], FP32)
    u_ps = s.ps("u_ps", [2 * KT, P])
    cat_loaded = s.sem("cat_loaded")
    dotted = s.sem("dotted")
    u_turned = s.sem("u_turned")
    u_copied = s.sem("u_copied")
    u_stored = s.sem("u_stored")
    qk_ps = [s.ps(f"qk_ps{i}", [P, D]) for i in range(RING)]
    v_ps = [s.ps(f"v_ps{i}", [P, D]) for i in range(2)]

    w_loaded = [s.sem(f"w_loaded{i}") for i in range(3)]
    w_hi_ready = s.sem("w_hi_ready")
    w_ready = s.sem("w_ready")
    x_loaded = [s.sem(f"x_loaded{i}") for i in range(2)]
    x_hi_ready = s.sem("x_hi_ready")
    x_ready = s.sem("x_ready")
    qk_done = s.sem("qk_done")
    v_done = s.sem("v_done")
    v_free = s.sem("v_free")
    hi_ready = s.sem("hi_ready")
    lo_ready = s.sem("lo_ready")
    stored = [s.sem(f"stored{i}") for i in range(RING)]
    xT_v = xT.rearrange("(k p) n -> p k n", p=P)
    block = s.block()

    @block.gpsimd
    def _(pool):
        def load_w(i):
            pool.dma_start(w_raw[:, i], wqkv[i].rearrange("(k p) n -> p k n", p=P)).then_inc(w_loaded[i], 16)

        def load_x(b, slot):
            pool.wait_ge(x_ready, b + 1)
            pool.dma_start(x_raw[:, slot], xT_v[:, :, bass.ds(b * BR, BR)]).then_inc(x_loaded[slot], 16)

        load_w(0)
        load_x(0, 0)
        load_w(1)
        load_w(2)
        pool.dma_start(w_cat_sb[:, :, :], w_cat.rearrange("(k p) n -> p k n", p=P)).then_inc(cat_loaded, 16)
        pool.dma_start(a_all[:, :], a_w.partition_broadcast(P)).then_inc(cat_loaded, 16)
        with pool.Fori(0, NB // 2, 1) as n:
            load_x(n * 2 + 1, 1)
            load_x(n * 2 + 2, 0)

    @block.sync
    def _(sp):
        for r in range(RING):
            sp.sem_inc(stored[r], 16)

        def step(b, slot):
            for m in range(M):
                sp.wait_ge(lo_ready, b * M + (m + 1 + RING))
                for part, src in enumerate((out_hi, out_lo)):
                    dst = qk_parts[m // KT, part, (m % KT) * P:(m % KT + 1) * P, bass.ds(b * BR, BR)]
                    sp.dma_start(dst, src[:, m % RING, :].bitcast(FP32)).then_inc(stored[m % RING], 16)

        pairs_of(sp, NB, step)
        sp.wait_ge(u_copied, 1)
        sp.dma_start(u_scratch.rearrange("(k p) -> k p", p=P), u_row[:, :]).then_inc(u_stored, 16)
        for r in range(RING):
            sp.wait_ge(stored[r], 32 * NB * M // RING + 16)
        sp.wait_ge(u_stored, 16)

    @block.scalar
    def _(act):
        act.sem_inc(v_free, 2)

        def split_w(i):
            act.wait_ge(w_loaded[i], 16)
            act.activation(w_hi[:, i], w_raw[:, i], ACT.Copy).then_inc(w_hi_ready, 1)

        def split_x(b, slot):
            act.wait_ge(x_loaded[slot], (b - slot) * 8 + 16)
            act.wait_ge(v_done, b * 2 + 1)
            act.activation(x_hi[:, slot], x_raw[:, slot], ACT.Copy).then_inc(x_hi_ready, 1)

        def step(b, slot, last=False):
            for m in range(M):
                if m == NEXT_AT and not last:
                    split_x(b + 1, 1 - slot)
                r = m % RING
                act.wait_ge(qk_done, b * M + (m + 1))
                act.wait_ge(stored[r], b * (32 * M // RING) + 32 * (m // RING) + 16)
                act.activation(out_hi[:, r, :], qk_ps[r][:, 0:BR], ACT.Copy).then_inc(hi_ready, 1)
            for t in range(2):
                act.wait_ge(v_done, b * 2 + (t + 4))
                act.activation(v_all[:, bass.ds((b * 2 + t) * D, D)], v_ps[t][:, :], ACT.Copy).then_inc(v_free, 1)

        split_w(0)
        split_x(0, 0)
        split_w(1)
        split_w(2)
        pairs_of(act, NB - 1, step)
        step(NB - 1, 0, last=True)

    @block.vector
    def _(dve):
        dve.sem_inc(x_ready, 2)
        dve.sem_inc(lo_ready, RING)

        def split_w(i):
            dve.wait_ge(w_hi_ready, i + 1)
            dve.tensor_tensor(w_lo[:, i], w_raw[:, i], w_hi[:, i], ALU.subtract).then_inc(w_ready, 1)

        def top(b):
            dve.wait_ge(v_free, b * 2 + 4)
            dve.tensor_reduce(v_tops[:, bass.ds(b, 1)], v_all[:, bass.ds(b * 2 * D, 2 * D)], AXX, ALU.max,
                              apply_absolute_value=True)

        def split_x(b, slot):
            dve.wait_ge(x_hi_ready, b + 1)
            dve.tensor_tensor(x_lo[:, slot], x_raw[:, slot], x_hi[:, slot], ALU.subtract).then_inc(x_ready, 1)

        def step(b, slot, edge_tile=False, last=False):
            for m in range(M):
                if m == NEXT_AT and not last:
                    split_x(b + 1, 1 - slot)
                r = m % RING
                dve.wait_ge(hi_ready, b * M + (m + 1))
                dve.tensor_tensor(out_lo[:, r, :], qk_ps[r][:, 0:BR], out_hi[:, r, :],
                                  ALU.subtract).then_inc(lo_ready, 1)
            if not last:
                top(b)
            if edge_tile:
                dve.wait_ge(dotted, b + 1)
                dve.scalar_tensor_tensor(product[:, :], w_cat_sb[:, bass.ds(b, 1), :].squeeze(1), 1.0, a_all[:, :],
                                         ALU.mult, ALU.mult, accum_out=u_col[:, bass.ds(b, 1)]).then_inc(dotted, 1)

        split_w(0)
        split_x(0, 0)
        split_w(1)
        split_w(2)
        dve.sem_inc(dotted, 1)
        dve.wait_ge(cat_loaded, 32)
        pairs_of(dve, 2 * KT, lambda b, slot: step(b, slot, edge_tile=True))
        for b in range(2 * KT, NB):
            step(b, b % 2, last=(b == NB - 1))
        top(NB - 1)
        dve.wait_ge(u_turned, 1)
        dve.tensor_copy(u_row[:, :], u_ps[:, :]).then_inc(u_copied, 1)

    @block.tensor
    def _(pe):
        pe.sem_inc(v_done, 3)
        xs, ws = (x_hi, x_lo), (w_hi, w_lo)

        def step(b, slot):
            pe.wait_ge(x_ready, b + 3)
            for m in range(M):
                if m % KT == 0:
                    pe.wait_ge(w_ready, m // KT + 1)
                pe.wait_ge(lo_ready, b * M + (m + 1))
                for n, (i, j) in enumerate(PASSES3):
                    for k in range(KT):
                        mm = pe.matmul(qk_ps[m % RING][:, 0:BR],
                                       ws[i][:, m // KT, k, (m % KT) * P:(m % KT + 1) * P],
                                       xs[j][:, slot, k, :], start=(n == 0 and k == 0),
                                       stop=(n == 2 and k == KT - 1))
                mm.then_inc(qk_done, 1)
            pe.wait_ge(w_ready, 3)
            for t in range(2):
                pe.wait_ge(v_free, b * 2 + (t + 1))
                for n, (i, j) in enumerate(PASSES3):
                    for k in range(KT):
                        mm = pe.matmul(v_ps[t][:, :], xs[j][:, slot, k, t * P:(t + 1) * P],
                                       ws[i][:, 2, k, :], start=(n == 0 and k == 0),
                                       stop=(n == 2 and k == KT - 1))
                mm.then_inc(v_done, 1)

        pairs_of(pe, NB, step)
        pe.wait_ge(dotted, 2 * KT + 1)
        pe.transpose(u_ps[:, :], u_col[:, :], eye).then_inc(u_turned, 1)


class AttentionInputs:

    def __init__(self, s, adj, qk_parts):
        self.adj, self.qk_parts = adj, qk_parts
        self.keys = s.sb("keys", [P, H, N], FP32R)
        self.q_st = s.sb("q_st", [P, 2, 2, BR], FP32R)
        self.adj_rows = [s.sb(f"adj_rows{t}", [P, NP], FP32) for t in range(2)]
        self.keys_loaded = [s.sem(f"keys_loaded{h}") for h in range(H)]
        self.q_loaded = [s.sem(f"q_loaded{i}") for i in range(2)]
        self.adj_loaded = [s.sem(f"adj_loaded{t}") for t in range(2)]

    def load_q(self, sp, row0, h, slot):
        for a in range(2):
            for part in range(2):
                half = part ^ a
                sp.dma_start(self.q_st[half * HD:(half + 1) * HD, slot, a, :].bitcast(FP32),
                             self.qk_parts[0, part, h * HD:(h + 1) * HD, bass.ds(row0, BR)])\
                    .then_inc(self.q_loaded[slot], 16)

    def load_keys(self, sp, h):
        for part in range(2):
            sp.dma_start(self.keys[part * HD:(part + 1) * HD, h, :].bitcast(FP32),
                         self.qk_parts[1, part, h * HD:(h + 1) * HD, 0:N]).then_inc(self.keys_loaded[h], 16)

    def load_adj(self, pool, row0, t):
        pool.dma_start(self.adj_rows[t][:, 0:N], self.adj[bass.ds(row0 + t * P, P), 0:N])\
            .then_inc(self.adj_loaded[t], 16)


def split_values(nc, s, v_all, v_tops, v_parts, eye, v_inv, inputs):
    v_split = s.sb("v_split", [P, H, NT, 2, HD], FP16)
    top = s.sb("top", [P, 1], FP32)
    row = s.sb("row", [1, P], FP32)
    ones = s.sb("ones", [1, P], FP32)
    unit = s.sb("unit", [P, 1], FP32)
    scale = s.sb("scale", [P, 1], FP32)
    t_ps = s.ps("t_ps", [1, P])
    b_ps = s.ps("b_ps", [P, 1])
    step_done = s.sem("step_done")
    t_done = s.sem("t_done")
    b_done = s.sem("b_done")
    hi_ready = s.sem("hi_ready")
    lo_ready = s.sem("lo_ready")
    stored = s.sem("stored")
    v_view = v_all.rearrange("p (t h c) -> p t h c", t=NT, h=H)
    block = s.block()

    @block.vector
    def _(dve):
        dve.memset(ones[:, :], 1.0)
        dve.tensor_reduce(top[:, :], v_tops, AXX, ALU.max).then_inc(step_done, 1)
        dve.wait_ge(t_done, 1)
        dve.tensor_reduce(row[:, 0:1], t_ps[:, :], AXX, ALU.max).then_inc(step_done, 1)
        dve.wait_ge(b_done, 1)
        dve.tensor_scalar(unit[:, :], b_ps[:, :], 1e-30, 1.0 / V_TOP, ALU.max, ALU.mult).then_inc(step_done, 1)
        dve.wait_ge(step_done, 3)
        dve.tensor_scalar(v_inv, unit[:, :], 1.0 / P_TOP, None, ALU.mult)
        dve.reciprocal(scale[:, :], unit[:, :]).then_inc(step_done, 1)
        dve.wait_ge(step_done, 4)
        for h in range(H):
            dve.wait_ge(hi_ready, h + 1)
            dve.scalar_tensor_tensor(v_split[:, h, :, 1, :], v_view[:, :, h, :], scale[:, :],
                                     v_split[:, h, :, 0, :], ALU.mult, ALU.subtract).then_inc(lo_ready, 1)

    @block.tensor
    def _(pe):
        pe.wait_ge(step_done, 1)
        pe.transpose(t_ps[:, :], top[:, :], eye[:, :]).then_inc(t_done, 1)
        pe.wait_ge(step_done, 2)
        pe.matmul(b_ps[:, :], ones[:, :], row[:, 0:1], start=True, stop=True).then_inc(b_done, 1)

    @block.scalar
    def _(act):
        act.wait_ge(step_done, 4)
        for h in range(H):
            act.activation(v_split[:, h, :, 0, :], v_view[:, :, h, :], ACT.Copy,
                           scale=scale[:, :]).then_inc(hi_ready, 1)

    @block.gpsimd
    def _(pool):
        for t in range(2):
            inputs.load_adj(pool, 0, t)

    @block.sync
    def _(sp):
        for h in range(2):
            inputs.load_q(sp, 0, h, h)
        inputs.load_keys(sp, 0)
        for h in range(H):
            sp.wait_ge(lo_ready, h + 1)
            sp.dma_start(v_parts[h], v_split[:, h].rearrange("p t a c -> p (t a c)")).then_inc(stored, 16)
        sp.wait_ge(stored, 16 * H)


PAIR = 1024
PIECES = [(c, min(PAIR, N - c)) for c in range(0, N, PAIR)]
EXPS = [(0, 5 * BR + 74), (5 * BR + 74, N - 5 * BR - 74)]
GROUPS = NT // 2
PE_ORDER = ["S0", "T0", "S1", "T1", "T2", "S2", "T3", "S3", "T4", "V0", "V1", "O", "V2", "S4", "T5", "V3", "T6",
            "T7", "V4", "S5", "T8", "T9", "T10", "V5", "V6", "V7", "V8", "V9", "V10"]
DVE_ORDER = ["S0", "T0", "S1", "T1", "T2", "S2", "T3", "S3", "T4", "O", "S4", "T5", "T6", "T7", "S5", "T8", "T9",
             "T10"]
ACT_ORDER = ["H0", "H1", "C", "H2", "H3", "H4", "E0", "E1", "H5", "H6", "H7", "H8", "H9", "H10", "E2", "E3"]
SUMS_AFTER = (1, 3)
O_RING = 5


def attention(nc, s, inputs, probs, v_parts, o_rows, eye, fold, v_inv, deg, adjT, adjT_bf):
    S_RING, T_RING, W_RING = 2, 3, 6
    keys, q_st, adj_rows = inputs.keys, inputs.q_st, inputs.adj_rows
    keys_loaded, q_loaded, adj_loaded = inputs.keys_loaded, inputs.q_loaded, inputs.adj_loaded
    mask = [s.sb(f"mask{t}", [P, N], BF16) for t in range(2)]
    probs = [[probs[:, i, t, :] for t in range(2)] for i in range(2)]
    vals = s.sb("vals", [P, 2, NT, P], FP16)
    pt_hi = s.sb("pt_hi", [P, W_RING, 2 * BR], FP16)
    pt_lo = s.sb("pt_lo", [P, W_RING, 2 * BR], FP16)
    top = s.sb("top", [P, 2, 2, 3], FP32)
    sums = s.sb("sums", [P, 2, 2, 2], FP32)
    r_sum = s.sb("r_sum", [P, 2, 2], FP32)
    r_inv = s.sb("r_inv", [P, 2, 2], FP32)
    acc_sb = s.sb("acc_sb", [P, 2, BR], FP32)
    o_sb = s.sb("o_sb", [P, 2, D], FP32)
    s_ps = [s.ps(f"s_ps{i}", [P, PAIR]) for i in range(S_RING)]
    t_ps = [s.ps(f"t_ps{i}", [P, 2 * BR]) for i in range(T_RING)]
    acc_ps = s.ps("acc_ps", [P, D])

    adj_summed = s.sem("adj_summed")
    adj_fixed = s.sem("adj_fixed")
    adjT_stored = s.sem("adjT_stored")
    mask_ready = s.sem("mask_ready")
    v_loaded = [s.sem(f"v_loaded{i}") for i in range(2)]
    scored = s.sem("scored")
    masked = s.sem("masked")
    weighed = s.sem("weighed")
    turned = s.sem("turned")
    hi_ready = s.sem("hi_ready")
    drained = s.sem("drained")
    used = s.sem("used")
    acc_copied = s.sem("acc_copied")
    folded = s.sem("folded")
    r_done = s.sem("r_done")
    o_stored = s.sem("o_stored")
    padded = s.sem("padded")
    block = s.block()
    SP_, GP = 2 * len(PIECES), GROUPS
    TP = GROUPS + 1
    O_BANK = O_RING % T_RING

    def stages(e, stage):
        with e.Fori(0, NB, 1) as b:
            for h in range(H):
                stage(b, h)

    @block.sync
    def _(sp):
        def load_v(h, slot):
            sp.dma_start(vals[:, slot], v_parts[h].rearrange("p (t c) -> p t c", t=NT)).then_inc(v_loaded[slot], 16)

        load_v(0, 0)
        inputs.load_keys(sp, 1)
        load_v(1, 1)
        for h in range(2, H):
            inputs.load_keys(sp, h)

        def stage(b, h):
            sp.wait_ge(scored, b * (H * SP_) + (h + 1) * SP_)
            nxt = b * BR if h + 2 < H else next_block(b + 1) * BR
            inputs.load_q(sp, nxt, (h + 2) % H, h % 2)
            if h == 0:
                sp.wait_ge(drained, b * (H * TP) + (O_RING + 1) + T_RING)
                sp.dma_start(o_rows[bass.ds(b * BR, BR), :].rearrange("(t p) c -> p t c", p=P),
                             o_sb[:, :, :]).then_inc(o_stored, 16)
            sp.wait_ge(used, b * (H * GP) + (h + 1) * GP + W_RING)
            load_v((h + 2) % H, h % 2)

        stages(sp, stage)
        sp.wait_ge(drained, NB * H * TP + 1 + T_RING)
        sp.dma_start(o_rows[NB * BR:(NB + 1) * BR, :].rearrange("(t p) c -> p t c", p=P),
                     o_sb[:, :, :]).then_inc(o_stored, 16)
        sp.wait_ge(o_stored, 16 * (NB + 1))
        for i in range(2):
            sp.wait_ge(q_loaded[i], 64 * (1 + NB * H // 2))
            sp.wait_ge(v_loaded[i], 16 * (1 + NB * H // 2))

    @block.gpsimd
    def _(pool):
        def make_mask(b, t, first=False):
            pool.wait_ge(adj_fixed, b * 2 + (t + 1))
            if not first:
                pool.wait_ge(masked, b * (H * SP_) - (1 - t) * len(PIECES) + S_RING)
            pool.nop(nofuse=True)
            pool.tensor_scalar(mask[t][:, :], adj_rows[t][:, 0:N], -MASKED, MASKED, ALU.mult, ALU.add)\
                .then_inc(mask_ready, 1)

        for t in range(2):
            pool.memset(adj_rows[t][:, N:NP], 0.0).then_inc(padded, 1)
            for i in range(2):
                pool.memset(probs[i][t][:, N:NP], 0.0).then_inc(padded, 1)
        pool.memset(sums[:, 1], 1.0).then_inc(padded, 1)
        pool.memset(o_sb[:, :, :], 0.0).then_inc(padded, 1)
        pool.wait_ge(padded, 9)
        for t in range(2):
            make_mask(0, t, first=True)
        for j in range(NT):
            pool.dma_start(adjT_bf[j * P:(j + 1) * P, :], adjT[j * P:(j + 1) * P, :]).then_inc(adjT_stored, 16)
        with pool.Fori(0, NB, 1) as b:
            nxt = next_block(b + 1) * BR
            for t in range(2):
                pool.wait_ge(mask_ready, b * 2 + (t + 1))
                inputs.load_adj(pool, nxt, t)
            for t in range(2):
                make_mask(b + 1, t)
        pool.wait_ge(adjT_stored, 16 * NT)

    @block.tensor
    def _(pe):
        pe.sem_inc(used, W_RING)

        def scores(base, n_in_block, h, slot, i):
            t, (c0, width) = i // len(PIECES), PIECES[i % len(PIECES)]
            pe.wait_ge(masked, base * (H * SP_) + n_in_block * SP_ + (i + 1))
            for c in range(c0, c0 + width, 512):
                w = min(512, c0 + width - c)
                for a in range(2):
                    mm = pe.matmul(s_ps[i % S_RING][:, c - c0:c - c0 + w], q_st[:, slot, a, t * P:(t + 1) * P],
                                   keys[:, h, c:c + w], start=(a == 0), stop=(a == 1))
            mm.then_inc(scored, 1)

        def fold_heads(b, n_in_block):
            pe.wait_ge(acc_copied, b * H + n_in_block + 2)
            pe.wait_ge(drained, NB * H * TP + T_RING if isinstance(b, int) else
                       b * (H * TP) + n_in_block * TP + (O_RING + 1))
            for t in range(2):
                mm = pe.matmul(t_ps[O_BANK][:, t * HD:(t + 1) * HD], acc_sb[:, (n_in_block + 1) % 2, t * P:(t + 1) * P],
                               fold, start=True, stop=True)
            mm.then_inc(folded, 1)

        pe.wait_ge(q_loaded[0], 64)
        pe.wait_ge(keys_loaded[0], 32)
        for i in range(SP_):
            scores(0, 0, 0, 0, i)

        def stage(b, h):
            cur, nxt = h % 2, (h + 1) % 2
            for what in PE_ORDER:
                kind, i = what[0], int(what[1:] or 0)
                ring = i if i < O_RING else i + 1
                if kind == "S":
                    if i == 0:
                        pe.wait_ge(q_loaded[nxt], b * (64 * H // 2) + 64 * ((h + 1) // 2 + 1))
                        pe.wait_ge(keys_loaded[(h + 1) % H], 32)
                    scores(b, h + 1, (h + 1) % H, nxt, i)
                elif kind == "T":
                    late = (i + 1) * BR > EXPS[0][1]
                    pe.wait_ge(weighed, b * (4 * H) + 4 * h + (4 if late else 3))
                    pe.wait_ge(drained, b * (H * TP) + h * TP + (ring + 1))
                    for j in range(2):
                        for t in range(2):
                            mm = pe.transpose(t_ps[ring % T_RING][:, j * BR + t * P:j * BR + (t + 1) * P],
                                              probs[cur][t][:, (2 * i + j) * P:(2 * i + j + 1) * P], eye)
                    mm.then_inc(turned, 1)
                elif kind == "V":
                    if i == 0:
                        pe.wait_ge(v_loaded[cur], b * (16 * H // 2) + 16 * (h // 2 + 1))
                        pe.wait_ge(acc_copied, b * H + h + 2)
                    pe.wait_ge(drained, b * (H * TP) + h * TP + (ring + 1) + T_RING)
                    for j in range(2):
                        for part in (pt_hi, pt_lo):
                            mm = pe.matmul(acc_ps[:, 0:BR], vals[:, cur, 2 * i + j, :],
                                           part[:, i % W_RING, j * BR:(j + 1) * BR],
                                           start=(i == 0 and j == 0 and part is pt_hi),
                                           stop=(i == GROUPS - 1 and j == 1 and part is pt_lo))
                    mm.then_inc(used, 1)
                else:
                    fold_heads(b, h)

        stages(pe, stage)
        fold_heads(NB, 0)

    @block.scalar
    def _(act):

        def exps(b, n_in_block, i):
            cur, t, e = n_in_block % 2, i // 2, i % 2
            act.wait_ge(masked, b * (H * SP_) + n_in_block * SP_ + (t + 1) * len(PIECES) + S_RING)
            c, w = EXPS[e]
            cols = probs[cur][t][:, c:c + w]
            act.activation(cols, cols, ACT.Exp, bias=top[:, cur, t, 2:3], scale=-1.0,
                           accum_out=sums[:, cur, t, e:e + 1]).then_inc(weighed, 1)

        def high_part(b, h, i):
            ring = i if i < O_RING else i + 1
            act.wait_ge(turned, b * (H * GP) + h * GP + (i + 1))
            act.wait_ge(used, b * (H * GP) + h * GP + (i + 2 if i < W_RING - 1 else i + 1))
            act.activation(pt_hi[:, i % W_RING, :], t_ps[ring % T_RING][:, :], ACT.Copy, scale=P_TOP)\
                .then_inc(hi_ready, 1)

        def copy_acc(b, n_in_block):
            act.wait_ge(used, b * (H * GP) + n_in_block * GP + W_RING)
            slot = (n_in_block + 1) % 2
            act.activation(acc_sb[:, slot, :], acc_ps[:, 0:BR], ACT.Copy)\
               .then_inc(acc_copied, 1)

        def sum_adj(b, tile0, t):
            act.wait_ge(adj_loaded[t], b * 16 + 16)
            rows = adj_rows[t][:, 0:N]
            act.activation(rows, rows, ACT.Copy, accum_out=deg[:, bass.ds(tile0 + t, 1)]).then_inc(adj_summed, 1)

        act.sem_inc(acc_copied, 1)
        act.wait_ge(padded, 9)
        sum_adj(0, 0, 0)
        sum_adj(0, 0, 1)
        for i in range(4):
            exps(0, 0, i)

        def stage(b, h):
            for what in ACT_ORDER:
                kind, i = what[0], int(what[1:] or 0)
                if kind == "H":
                    high_part(b, h, i)
                elif kind == "E":
                    exps(b, h + 1, i)
                else:
                    copy_acc(b, h)
            if h in SUMS_AFTER:
                sum_adj(b + 1, next_block(b + 1) * 2, SUMS_AFTER.index(h))

        stages(act, stage)
        copy_acc(NB, 0)

    @block.vector
    def _(dve):
        dve.memset(acc_ps[:, 0:BR], 0.0).then_inc(padded, 1)
        dve.wait_ge(padded, 9)
        dve.sem_inc(masked, S_RING)
        dve.sem_inc(drained, T_RING)

        def set_diagonal(b, row0):
            for t in range(2):
                dve.wait_ge(adj_summed, b * 2 + (t + 1))
                diag = adj_rows[t][:, bass.ds(row0 + t * P, P)]
                dve.tensor_tensor(diag, diag, eye, ALU.max).then_inc(adj_fixed, 1)

        def mask_scores(b, n_in_block, i):
            cur, t, k = n_in_block % 2, i // len(PIECES), i % len(PIECES)
            c, w = PIECES[k]
            dve.wait_ge(scored, b * (H * SP_) + n_in_block * SP_ + (i + 1))
            if n_in_block in (0, H) and k == 0:
                at_block = b if n_in_block == 0 else b + 1
                dve.wait_ge(mask_ready, at_block * 2 + (t + 1))
            if k > 0:
                dve.wait_ge(masked, b * (H * SP_) + n_in_block * SP_ + i + S_RING)
            dve.nop(nofuse=True)
            dve.tensor_tensor_reduce(out=probs[cur][t][:, c:c + w], in0=s_ps[i % S_RING][:, 0:w],
                                     in1=mask[t][:, c:c + w], scale=-(HD ** -0.5),
                                     scalar=3e38 if k == 0 else top[:, cur, t, k - 1:k],
                                     op0=ALU.add, op1=ALU.min, accum_out=top[:, cur, t, k:k + 1])\
                .then_inc(masked, 1)

        def low_part(b, h, i):
            ring = i if i < O_RING else i + 1
            dve.wait_ge(hi_ready, b * (H * GP) + h * GP + (i + 1))
            dve.scalar_tensor_tensor(pt_lo[:, i % W_RING, :], t_ps[ring % T_RING][:, :], P_TOP,
                                     pt_hi[:, i % W_RING, :], ALU.mult, ALU.subtract).then_inc(drained, 1)

        def invert_sums(b, n_in_block):
            slot = (n_in_block + 1) % 2
            dve.tensor_tensor(r_sum[:, slot, :], sums[:, slot, :, 0], sums[:, slot, :, 1], ALU.add).then_inc(r_done, 1)
            dve.wait_ge(r_done, b * (2 * H) + n_in_block * 2 + 1)
            dve.reciprocal(r_inv[:, slot, :], r_sum[:, slot, :]).then_inc(r_done, 1)

        def norm(b, n_in_block):
            h, slot = (n_in_block + H - 1) % H, (n_in_block + 1) % 2
            dve.wait_ge(r_done, b * (2 * H) + n_in_block * 2 + 2)
            dve.wait_ge(folded, b * H + (n_in_block + 1))
            if h == 0:
                dve.wait_ge(o_stored, b * 16 + 16)
            dve.scalar_tensor_tensor(o_sb[:, :, h * HD:(h + 1) * HD],
                                     t_ps[O_BANK][:, 0:2 * HD].rearrange("p (t c) -> p t c", t=2), v_inv,
                                     r_inv[:, slot, :].unsqueeze(2).broadcast_to([P, 2, HD]), ALU.mult, ALU.mult)\
                .then_inc(drained, 1)

        set_diagonal(0, 0)
        for i in range(SP_):
            mask_scores(0, 0, i)

        def stage(b, h):
            invert_sums(b, h)
            for what in DVE_ORDER:
                kind, i = what[0], int(what[1:] or 0)
                if kind == "S":
                    mask_scores(b, h + 1, i)
                elif kind == "T":
                    low_part(b, h, i)
                elif kind == "O":
                    norm(b, h)
            if h == H // 2:
                set_diagonal(b + 1, next_block(b + 1) * BR)

        stages(dve, stage)
        invert_sums(NB, 0)
        norm(NB, 0)


EPS = 1e-5
X_TOP = 256.0
NORM_STEPS = 5


def layer_norm(dve, z, stats, mean_var, rstd, out, chain, at):
    norm_moments(dve, z, stats, mean_var, chain, at)
    norm_apply(dve, z, mean_var, rstd, out, chain, at)


def norm_moments(dve, z, stats, mean_var, chain, at):
    dve.bn_stats(stats, z).then_inc(chain, 1)
    dve.wait_ge(chain, at + 1)
    dve.nop(nofuse=True)
    dve.bn_aggr(mean_var, stats).then_inc(chain, 1)


def norm_apply(dve, z, mean_var, rstd, out, chain, at):
    dve.wait_ge(chain, at + 4)
    dve.tensor_scalar(out, z, mean_var[:, 0:1], rstd, ALU.subtract, ALU.mult).then_inc(chain, 1)


def inv_std(pool, mean_var, rstd, eps_half, chain, at):
    pool.wait_ge(chain, at + 2)
    pool.tensor_tensor(mean_var[:, 1:2], mean_var[:, 1:2], eps_half[:, 0:1], ALU.add).then_inc(chain, 1)
    pool.wait_ge(chain, at + 3)
    pool.tensor_tensor(rstd, mean_var[:, 1:2], eps_half[:, 1:2], ALU.pow).then_inc(chain, 1)


def first_rows(nc, s, x_in, o_rows, wo, w1T, b1, deg, r, r_in, r_out, u_scratch, u_all, x_rows, g_parts, r_parts,
               adjT_bf, a_t, eye, eye_bf, eps_half):
    whole = s.sb("whole", [P, NT], FP32)
    pos = s.sb("pos", [P, NT], FP32)
    safe = s.sb("safe", [P, NT], FP32)
    inv = s.sb("inv", [P, NT], FP32)
    u_loaded = s.sem("u_loaded")
    HID = w1T.shape[1]
    w_sb = s.sb("w_sb", [P, KT, D], FP32)
    w1_sb = s.sb("w1_sb", [P, KT, HID], FP32)
    b1_all = s.sb("b1_all", [P, HID], FP32)
    o_sb = s.sb("o_sb", [P, 2, D], FP32)
    oT_sb = s.sb("oT_sb", [P, 2, D], FP32)
    xr_sb = s.sb("xr_sb", [P, 2, D], FP32)
    z_sb = s.sb("z_sb", [P, 2, D], FP32)
    xn_sb = s.sb("xn_sb", [P, 2, D], FP32)
    xT_sb = s.sb("xT_sb", [P, 2, D], FP32)
    h_sb = s.sb("h_sb", [P, 2, HID], FP32)
    rest = s.sb("rest", [P, 2, HID], FP32)
    r_rest = s.sb("r_rest", [P, NT], FP32)
    stats = s.sb("stats", [P, 2, 6], FP32)
    mean_var = s.sb("mean_var", [P, 2, 2], FP32)
    rstd = s.sb("rstd", [P, 2, 1], FP32)
    oT_ps = [s.ps(f"oT_ps{i}", [P, D]) for i in range(2)]
    y_ps = [s.ps(f"y_ps{i}", [P, D]) for i in range(2)]
    xT_ps = [s.ps(f"xT_ps{i}", [P, D]) for i in range(2)]
    h_ps = [s.ps(f"h_ps{i}", [P, D]) for i in range(2)]
    w_loaded = s.sem("w_loaded")
    o_loaded = [s.sem(f"o_loaded{i}") for i in range(2)]
    x_loaded = [s.sem(f"x_loaded{i}") for i in range(2)]
    a_loaded = s.sem("a_loaded")
    o_turned = s.sem("o_turned")
    o_copied = s.sem("o_copied")
    projected = s.sem("projected")
    added = s.sem("added")
    normed = s.sem("normed")
    stored = [s.sem(f"stored{i}") for i in range(2)]
    x_turned = s.sem("x_turned")
    x_copied = s.sem("x_copied")
    multiplied = s.sem("multiplied")
    biased = s.sem("biased")
    high = s.sem("high")
    rested = s.sem("rested")
    middle = s.sem("middle")
    low = s.sem("low")
    r_chain = s.sem("r_chain")
    block = s.block()

    def steps(e, step):
        for t in range(4):
            step(t, t % 2)
        with e.Fori(2, NT // 2 - 2, 1) as n:
            step(n * 2, 0)
            step(n * 2 + 1, 1)
        for t in range(NT - 4, NT + 3):
            step(t, t % 2)

    def within(t, lag, ahead=0):
        return not isinstance(t, int) or 0 <= t - lag and t + ahead < NT + lag

    @block.gpsimd
    def _(pool):
        pool.wait_ge(r_chain, 3)
        pool.tensor_tensor(inv[:, :], safe[:, :], eps_half[:, 1:2].broadcast_to([P, NT]), ALU.pow)\
            .then_inc(r_chain, 1)

        def step(t, slot):
            if within(t, 0):
                pool.dma_start(a_t[:, bass.ds(t, 1), :].squeeze(1), adjT_bf[bass.ds(t * P, P), :])\
                    .then_inc(a_loaded, 16)
                inv_std(pool, mean_var[:, slot, :], rstd[:, slot, :], eps_half, normed, t * NORM_STEPS)

        steps(pool, step)
        pool.wait_ge(a_loaded, 16 * NT)
        for j in range(NT):
            diag = a_t[:, j, j * P:(j + 1) * P]
            pool.tensor_tensor(diag, diag, eye_bf, ALU.add)

    @block.sync
    def _(sp):
        for i in range(2):
            sp.sem_inc(stored[i], 16)

        def load_o(t, slot):
            sp.dma_start(o_sb[:, slot, :], o_rows[bass.ds(t * P + BR, P), :]).then_inc(o_loaded[slot], 16)

        def load_x(t, slot):
            sp.dma_start(xr_sb[:, slot, :], x_in[bass.ds(t * P, P), :]).then_inc(x_loaded[slot], 16)

        def step(t, slot):
            if within(t, 0, 3):
                sp.wait_ge(o_turned, t + 4)
                load_o(t + 3, 1 - slot)
            if within(t, 0, 2):
                sp.wait_ge(added, t + 3)
                load_x(t + 2, slot)
            if within(t, 0):
                sp.wait_ge(normed, t * NORM_STEPS + NORM_STEPS)
                sp.dma_start(x_rows[bass.ds(t * P, P), :], xn_sb[:, slot, :]).then_inc(stored[slot], 16)

        load_o(0, 0)
        sp.dma_start(w_sb[:, :, :], wo.rearrange("(k p) n -> p k n", p=P)).then_inc(w_loaded, 16)
        load_x(0, 0)
        load_o(1, 1)
        load_x(1, 1)
        sp.dma_start(w1_sb[:, :, :], w1T.rearrange("(k p) n -> p k n", p=P)).then_inc(w_loaded, 16)
        sp.dma_start(b1_all[:, :], b1.partition_broadcast(P)).then_inc(w_loaded, 16)
        sp.wait_ge(o_turned, 3)
        load_o(2, 0)
        sp.dma_start(u_all.rearrange("p i n -> p (i n)"), u_scratch.partition_broadcast(P)).then_inc(u_loaded, 16)
        steps(sp, step)
        sp.wait_ge(u_loaded, 16)
        for i in range(2):
            sp.wait_ge(stored[i], 16 * NT // 2 + 16)

    @block.tensor
    def _(pe):
        pe.sem_inc(o_turned, 2)
        pe.sem_inc(projected, 2)
        pe.sem_inc(x_turned, 2)
        pe.sem_inc(multiplied, 2)

        def turn(dst, src):
            for k in range(KT):
                mm = pe.transpose(dst[:, k * P:(k + 1) * P], src[:, k * P:(k + 1) * P], eye)
            return mm

        def turn_o(t, slot):
            pe.wait_ge(o_loaded[slot], (t - slot) * 8 + 16)
            pe.wait_ge(o_copied, t + 1)
            turn(oT_ps[slot], o_sb[:, slot, :]).then_inc(o_turned, 1)

        def project(t, slot):
            pe.wait_ge(o_copied, t + 3)
            pe.wait_ge(added, t + 1)
            for k in range(KT):
                mm = pe.matmul(y_ps[slot][:, :], oT_sb[:, slot, k * P:(k + 1) * P], w_sb[:, k, :],
                               start=(k == 0), stop=(k == KT - 1))
            mm.then_inc(projected, 1)

        def turn_x(t, slot):
            pe.wait_ge(normed, t * NORM_STEPS + NORM_STEPS)
            pe.wait_ge(x_copied, t + 1)
            turn(xT_ps[slot], xn_sb[:, slot, :]).then_inc(x_turned, 1)

        def multiply(t, slot):
            pe.wait_ge(x_copied, t + 3)
            pe.wait_ge(biased, t + 1)
            for k in range(KT):
                mm = pe.matmul(h_ps[slot][:, 0:HID], xT_sb[:, slot, k * P:(k + 1) * P], w1_sb[:, k, :],
                               start=(k == 0), stop=(k == KT - 1))
            mm.then_inc(multiplied, 1)

        def step(t, slot):
            if within(t, 0, 1):
                turn_o(t + 1, 1 - slot)
            if within(t, 0):
                project(t, slot)
            if within(t, 1):
                turn_x(t - 1, 1 - slot)
            if within(t, 2):
                multiply(t - 2, slot)

        turn_o(0, 0)
        pe.wait_ge(w_loaded, 48)
        steps(pe, step)

    @block.scalar
    def _(act):
        act.sem_inc(o_copied, 2)
        act.sem_inc(x_copied, 2)

        def copy_o(t, slot):
            act.wait_ge(o_turned, t + 3)
            act.wait_ge(projected, t + 1)
            act.activation(oT_sb[:, slot, :], oT_ps[slot][:, :], ACT.Copy).then_inc(o_copied, 1)

        def copy_x(t, slot):
            act.wait_ge(x_turned, t + 3)
            act.wait_ge(multiplied, t + 1)
            act.activation(xT_sb[:, slot, :], xT_ps[slot][:, :], ACT.Copy).then_inc(x_copied, 1)

        def step(t, slot):
            if within(t, 0, 1):
                copy_o(t + 1, 1 - slot)
            if within(t, 3):
                act.wait_ge(biased, t)
                act.activation(g_parts[:, bass.ds(t - 3, 1), 0, :].squeeze(1), h_sb[:, 1 - slot, :], ACT.Copy,
                               scale=r[:, bass.ds(t - 3, 1)]).then_inc(high, 1)
            if within(t, 1):
                copy_x(t - 1, 1 - slot)
            if within(t, 3):
                act.wait_ge(rested, t - 2)
                act.activation(g_parts[:, bass.ds(t - 3, 1), 1, :].squeeze(1), rest[:, 1 - slot, :], ACT.Copy)\
                   .then_inc(middle, 1)

        copy_o(0, 0)
        steps(act, step)

    @block.vector
    def _(dve):
        dve.sem_inc(added, 2)
        dve.sem_inc(biased, 2)
        dve.tensor_scalar(whole[:, :], deg, 1.0, None, ALU.add).then_inc(r_chain, 1)
        dve.wait_ge(r_chain, 1)
        dve.tensor_scalar(pos[:, :], whole[:, :], 0.0, None, ALU.is_gt).then_inc(r_chain, 1)
        dve.tensor_scalar(safe[:, :], whole[:, :], 1e-30, None, ALU.max).then_inc(r_chain, 1)
        dve.wait_ge(r_chain, 4)
        dve.tensor_tensor(r, inv[:, :], pos[:, :], ALU.mult).then_inc(r_chain, 1)
        dve.wait_ge(r_chain, 5)
        dve.tensor_scalar(r_in, r, X_TOP, None, ALU.mult)
        dve.tensor_scalar(r_out, r, 1.0 / X_TOP, None, ALU.mult)
        dve.tensor_copy(r_parts[:, :, 0], r).then_inc(r_chain, 1)
        dve.wait_ge(r_chain, 6)
        dve.tensor_tensor(r_rest[:, :], r, r_parts[:, :, 0], ALU.subtract).then_inc(r_chain, 1)
        dve.wait_ge(r_chain, 7)
        dve.tensor_copy(r_parts[:, :, 1], r_rest[:, :]).then_inc(r_chain, 1)
        dve.wait_ge(r_chain, 8)
        dve.tensor_tensor(r_parts[:, :, 2], r_rest[:, :], r_parts[:, :, 1], ALU.subtract).then_inc(r_chain, 1)

        def bias(t, slot):
            dve.wait_ge(multiplied, t + 3)
            dve.tensor_tensor(h_sb[:, slot, :], h_ps[slot][:, 0:HID], b1_all[:, :], ALU.add).then_inc(biased, 1)

        def first_rest(t, slot):
            dve.wait_ge(high, t + 1)
            dve.scalar_tensor_tensor(rest[:, slot, :], h_sb[:, slot, :], r[:, bass.ds(t, 1)],
                                     g_parts[:, bass.ds(t, 1), 0, :].squeeze(1), ALU.mult, ALU.subtract)\
                .then_inc(rested, 1)

        def low_part(t, slot):
            dve.wait_ge(middle, t + 1)
            dve.tensor_tensor(g_parts[:, bass.ds(t, 1), 2, :].squeeze(1), rest[:, slot, :],
                              g_parts[:, bass.ds(t, 1), 1, :].squeeze(1), ALU.subtract).then_inc(low, 1)

        def step(t, slot):
            if within(t, 3):
                bias(t - 3, 1 - slot)
            if within(t, 0):
                dve.wait_ge(projected, t + 3)
                dve.wait_ge(x_loaded[slot], (t - slot) * 8 + 16)
                dve.tensor_tensor(z_sb[:, slot, :], y_ps[slot][:, :], xr_sb[:, slot, :], ALU.add).then_inc(added, 1)
            if within(t, 3):
                first_rest(t - 3, 1 - slot)
            if within(t, 0):
                dve.wait_ge(added, t + 3)
                dve.wait_ge(stored[slot], (t - slot) * 8 + 16)
                dve.wait_ge(x_turned, t + 1)
                layer_norm(dve, z_sb[:, slot, :], stats[:, slot, :], mean_var[:, slot, :], rstd[:, slot, :],
                           xn_sb[:, slot, :], normed, t * NORM_STEPS)
            if within(t, 3):
                low_part(t - 3, 1 - slot)

        steps(dve, step)


def aggregate(nc, s, kind, a_t, parts, w_in, b_in, x_rows, out_rows, r, r_parts, eps_half, u_all=None, dots=None,
              best=None, r_in=None, eye=None, eye_bf=None):
    n_parts, width = parts.shape[2], parts.shape[3]
    KC = width // P
    BANKS = KC // 2
    linear = kind == "linear"
    CHUNKS = [(c, min(D, NP - c)) for c in range(0, NP, D)]
    BY_4 = [(c, min(c + 4, NT)) for c in range(0, NT, 4)]
    w_sb = s.sb("w_sb", [P, KC, D], FP32)
    agg_sb = s.sb("agg_sb", [P, 2, KC, BR], FP32)
    x_sb = s.sb("x_sb", [P, 2, D], FP32)
    y_sb = s.sb("y_sb", [P, 2, D], FP32)
    z_sb = y_sb if linear else s.sb("z_sb", [P, 2, D], FP32)
    xn_sb = s.sb("xn_sb", [P, 2, D], FP32)
    stats = s.sb("stats", [P, 2, 6], FP32)
    mean_var = s.sb("mean_var", [P, 2, 2], FP32)
    rstd = s.sb("rstd", [P, 2, 1], FP32)
    agg_ps = [[s.ps(f"agg_ps{i}{j}", [P, D]) for j in range(BANKS)] for i in range(2)]
    y_ps = [s.ps(f"y_ps{i}", [P, D]) for i in range(2)]
    w_loaded = s.sem("w_loaded")
    x_loaded = [s.sem(f"x_loaded{i}") for i in range(2)]
    gathered = s.sem("gathered")
    copied = s.sem("copied")
    multiplied = s.sem("multiplied")
    taken = s.sem("taken")
    added = s.sem("added")
    normed = s.sem("normed")
    stored = [s.sem(f"stored{i}") for i in range(2)]
    if linear:
        b_all = s.sb("b_all", [P, D], FP32)
        rho3 = s.sb("rho3", [P, NT, 3], FP32)
        rho = s.sb("rho", [P, NT], FP32)
        least_sb = s.sb("least", [P, NP], FP32)
        sums_sb = least_sb[0:3, :]
        least = least_sb[:, :]
        turned = s.sem("turned")
        reduced = s.sem("reduced")
        no_edge = s.sb("no_edge", [P, 2, NP], BF16)
        far = s.sb("far", [P, 1], FP32)
        no_edge_ready = s.sem("no_edge_ready")
        lessened = s.sem("lessened")
        turn_ps = [s.ps(f"turn_ps{i}", [P, D]) for i in range(2)]
        sums_ps = [bank[0:3, :] for bank in turn_ps]
        rho_ps = s.ps("rho_ps", [P, D])
        summed = s.sem("summed")
        sums_copied = s.sem("sums_copied")
        rho_done = s.sem("rho_done")
        rho_chain = s.sem("rho_chain")
        dotted = s.sem("dotted")
    else:
        rows_sb = s.sb("rows_sb", [P, 2, 2, D], FP32)
        split = RowSplit(s, [rows_sb[:, 0], rows_sb[:, 1], y_sb[:, :, :], z_sb[:, :, :]], x_rows, parts,
                         lambda tile: r_in[:, tile])
        eyed = s.sem("eyed")
    block = s.block()

    @block.sync
    def _(sp):
        for t in range(2):
            sp.sem_inc(stored[t], 16)

        def load(b, t):
            sp.dma_start(x_sb[:, t, :], x_rows[bass.ds(b * BR + t * P, P), :]).then_inc(x_loaded[t], 16)

        def step(b, last=False):
            for t in range(2):
                sp.wait_ge(normed, b * (2 * NORM_STEPS) + (t + 1) * NORM_STEPS)
                sp.dma_start(out_rows[bass.ds(b * BR + t * P, P), :], xn_sb[:, t, :]).then_inc(stored[t], 16)
                if not last:
                    load(b + 1, t)

        if not linear:
            rings_of(sp, NB, split.ring, lambda b, slot: split.load(sp, b, slot))
        for t in range(2):
            load(0, t)
        with sp.Fori(0, NB - 1, 1) as b:
            step(b)
        step(NB - 1, last=True)
        for t in range(2):
            sp.wait_ge(stored[t], 16 * NB + 16)

    @block.gpsimd
    def _(pool):
        pool.dma_start(w_sb[:, :, :], w_in.rearrange("(k p) n -> p k n", p=P)).then_inc(w_loaded, 16)
        if linear:
            pool.dma_start(b_all[:, :], b_in.partition_broadcast(P)).then_inc(w_loaded, 16)
        with pool.Fori(0, NB, 1) as b:
            for t in range(2):
                inv_std(pool, mean_var[:, t, :], rstd[:, t, :], eps_half, normed, b * (2 * NORM_STEPS) + t * NORM_STEPS)

    @block.tensor
    def _(pe):
        pe.sem_inc(multiplied, 2)
        if linear:
            for i, (c, w) in enumerate(CHUNKS):
                if i >= 2:
                    pe.wait_ge(sums_copied, i - 1)
                for j in range(NT):
                    mm = pe.matmul(sums_ps[i % 2][:, 0:w], r_parts[:, j, :], a_t[:, j, c:c + w], start=(j == 0),
                                   stop=(j == NT - 1))
                mm.then_inc(summed, 1)
            pe.wait_ge(sums_copied, len(CHUNKS))
            for t in range(NT):
                mm = pe.transpose(rho_ps[:, t * 3:(t + 1) * 3], sums_sb[:, t * P:(t + 1) * P], eye[0:3, 0:3])
            mm.then_inc(rho_done, 1)
        pe.wait_ge(w_loaded, 32 if linear else 16)

        def gather(b, slot, splitting=False):
            for c in range(KC):
                if c % 2 == 0:
                    pe.wait_ge(copied, b * BANKS + (c // 2 + 1))
                for j in range(NT):
                    if splitting and c == 0:
                        pe.wait_ge(split.low, j + 1 + 2 * split.ring)
                    for i in range(n_parts):
                        mm = pe.matmul(agg_ps[slot][c // 2][:, (c % 2) * BR:(c % 2 + 1) * BR],
                                       parts[:, j, i, c * P:(c + 1) * P], a_t[:, j, bass.ds(b * BR, BR)],
                                       start=(j == 0 and i == 0), stop=(j == NT - 1 and i == n_parts - 1))
                if c % 2 == 1:
                    mm.then_inc(gathered, 1)

        def step(b, slot, last=False):
            if not last:
                gather(b + 1, 1 - slot)
            pe.wait_ge(copied, b * BANKS + 3 * BANKS)
            for t in range(2):
                pe.wait_ge(taken, b * 2 + (t + 1))
                for k in range(KC):
                    mm = pe.matmul(y_ps[t][:, :], agg_sb[:, slot, k, t * P:(t + 1) * P], w_sb[:, k, :],
                                   start=(k == 0), stop=(k == KC - 1))
                mm.then_inc(multiplied, 1)

        if not linear:
            pe.wait_ge(eyed, NT)
        gather(0, 0, splitting=not linear)
        pairs_of(pe, NB - 1, step)
        step(NB - 1, 0, last=True)
        if linear:
            pe.wait_ge(lessened, NT + 2)
            for i, (first, end) in enumerate(BY_4):
                if i >= 2:
                    pe.wait_ge(reduced, i - 1)
                for t in range(first, end):
                    mm = pe.transpose(turn_ps[i % 2][:, (t - first) * P:(t - first + 1) * P],
                                      least[:, t * P:(t + 1) * P], eye)
                mm.then_inc(turned, 1)

    @block.scalar
    def _(act):
        act.sem_inc(copied, 2 * BANKS)

        if linear:
            for i, (c, w) in enumerate(CHUNKS):
                act.wait_ge(summed, i + 1)
                act.activation(sums_sb[:, c:c + w], sums_ps[i % 2][:, 0:w], ACT.Copy).then_inc(sums_copied, 1)
        else:
            act.sem_inc(taken, 2)
            rings_of(act, NB, split.ring, lambda b, slot: split.high_parts(act, b, slot))
            act.wait_ge(split.low, NT + 2 * split.ring)

        def copy(b, slot):
            for i in range(BANKS):
                act.wait_ge(gathered, b * BANKS + (i + 1))
                act.wait_ge(multiplied, b * 2)
                act.activation(agg_sb[:, slot, 2 * i:2 * i + 2, :].rearrange("p k n -> p (k n)"),
                               agg_ps[slot][i][:, :], ACT.Copy).then_inc(copied, 1)

        def step(b, slot, last=False):
            if not last:
                copy(b + 1, 1 - slot)
            if linear:
                for t in range(2):
                    act.wait_ge(lessened, b * 2 + (t + 1))
                    act.activation(no_edge[:, t, :], a_t[:, bass.ds(b * 2 + t, 1), :].squeeze(1), ACT.Relu,
                                   scale=NO_EDGE, bias=far[:, :]).then_inc(no_edge_ready, 1)
            if not linear:
                for t in range(2):
                    act.wait_ge(multiplied, b * 2 + (t + 3))
                    act.wait_ge(added, b * 2 + (t + 1))
                    act.activation(y_sb[:, t, :], y_ps[t][:, :], ACT.Relu,
                                   scale=r[:, bass.ds(b * 2 + t, 1)]).then_inc(taken, 1)

        copy(0, 0)
        pairs_of(act, NB - 1, step)
        step(NB - 1, 0, last=True)

    @block.vector
    def _(dve):
        dve.sem_inc(added, 2)
        if linear:
            dve.sem_inc(taken, 2)
            dve.wait_ge(rho_done, 1)
            dve.tensor_copy(rho3[:, :, :].rearrange("p t i -> p (t i)"), rho_ps[:, 0:3 * NT]).then_inc(rho_chain, 1)
            dve.wait_ge(rho_chain, 1)
            dve.tensor_reduce(rho[:, :], rho3[:, :, :], AXX, ALU.add).then_inc(rho_chain, 1)
            dve.wait_ge(rho_chain, 2)
            dve.tensor_tensor(rho[:, :], rho[:, :], r, ALU.mult).then_inc(rho_chain, 1)
            dve.wait_ge(rho_chain, 3)
            dve.sem_inc(dotted, 1)
            dve.memset(far[:, :], -NO_EDGE)
            dve.memset(least, 3e38).then_inc(lessened, 2)
        else:
            dve.sem_inc(split.low, 2 * split.ring)
            for j in range(NT):
                diag = a_t[:, j, j * P:(j + 1) * P]
                dve.tensor_tensor(diag, diag, eye_bf, ALU.add).then_inc(eyed, 1)
            rings_of(dve, NB, split.ring, lambda b, slot: split.low_parts(dve, b, slot))

        with dve.Fori(0, NB, 1) as b:
            for t in range(2):
                dve.wait_ge(x_loaded[t], b * 16 + 16)
                if linear:
                    dve.wait_ge(multiplied, b * 2 + (t + 3))
                    dve.scalar_tensor_tensor(y_sb[:, t, :], y_ps[t][:, :], r[:, bass.ds(b * 2 + t, 1)], x_sb[:, t, :],
                                             ALU.mult, ALU.add).then_inc(taken, 1)
                    dve.wait_ge(taken, b * 2 + (t + 3))
                    dve.scalar_tensor_tensor(z_sb[:, t, :], b_all[:, :], rho[:, bass.ds(b * 2 + t, 1)], y_sb[:, t, :],
                                             ALU.mult, ALU.add).then_inc(added, 1)
                else:
                    dve.wait_ge(taken, b * 2 + (t + 3))
                    dve.tensor_tensor(z_sb[:, t, :], y_sb[:, t, :], x_sb[:, t, :], ALU.add).then_inc(added, 1)
                dve.wait_ge(added, b * 2 + (t + 3))
                dve.wait_ge(stored[t], b * 16 + 16)
                layer_norm(dve, z_sb[:, t, :], stats[:, t, :], mean_var[:, t, :], rstd[:, t, :], xn_sb[:, t, :],
                           normed, b * (2 * NORM_STEPS) + t * NORM_STEPS)
                if linear:
                    dve.wait_ge(normed, b * (2 * NORM_STEPS) + (t + 1) * NORM_STEPS)
                    for i in range(2):
                        dve.scalar_tensor_tensor(y_sb[:, t, :], xn_sb[:, t, :], 1.0, u_all[:, i, :], ALU.mult, ALU.mult,
                                                 accum_out=dots[:, i, bass.ds(b * 2 + t, 1)]).then_inc(dotted, 1)
                        dve.wait_ge(dotted, b * 4 + (t * 2 + i + 2))
                    dve.wait_ge(no_edge_ready, b * 2 + (t + 1))
                    dve.wait_ge(lessened, b * 2 + (t + 2))
                    dve.scalar_tensor_tensor(least, no_edge[:, t, :], dots[:, 1, bass.ds(b * 2 + t, 1)], least,
                                             ALU.subtract, ALU.min).then_inc(lessened, 1)

        if linear:
            for i, (first, end) in enumerate(BY_4):
                dve.wait_ge(turned, i + 1)
                dve.tensor_reduce(best[:, first:end],
                                  turn_ps[i % 2][:, 0:(end - first) * P].rearrange("p (t c) -> p t c", c=P), AXX,
                                  ALU.min).then_inc(reduced, 1)



LEAK = 0.2
NO_EDGE = -9e15


def row_shifts(nc, s, x_rows, x_parts, a_t, best, eye, eye_bf, dots, a_b, s_cols, shift_scratch):
    rows_sb = s.sb("rows_sb", [P, 4, 2, D], FP32)
    split = RowSplit(s, [rows_sb[:, i] for i in range(4)], x_rows, x_parts, lambda tile: X_TOP)
    ab_all = s.sb("ab_all", [P, 1], FP32)
    s1b = s.sb("s1b", [P, NT], FP32)
    s1b_leak = s.sb("s1b_leak", [P, NT], FP32)
    z = s.sb("z", [P, NT], FP32)
    m = s.sb("m", [P, NT], FP32)
    shifts = s.sb("shifts", [P, 2 * NT], FP32)
    shifts_T = s.sb("shifts_T", [2 * NT, P], FP32)
    st_ps = s.ps("st_ps", [2 * NT, P])
    ab_loaded = s.sem("ab_loaded")
    chain = s.sem("chain")
    st_done = s.sem("st_done")
    st_copied = s.sem("st_copied")
    stored = s.sem("stored")
    block = s.block()

    @block.sync
    def _(sp):
        sp.dma_start(ab_all[:, :], a_b.partition_broadcast(P)).then_inc(ab_loaded, 16)

        def store_shifts():
            sp.wait_ge(st_copied, 1)
            sp.dma_start(shift_scratch.rearrange("(t p) -> t p", p=P), shifts_T[:, :]).then_inc(stored, 16)

        for b in range(split.ring):
            split.load(sp, b, b)
        store_shifts()
        with sp.Fori(1, NB // split.ring, 1) as n:
            for i in range(split.ring):
                split.load(sp, n * split.ring + i, i)
        for b in range(NB // split.ring * split.ring, NB):
            split.load(sp, b, b % split.ring)
        sp.wait_ge(stored, 16)

    @block.scalar
    def _(act):
        act.wait_ge(st_done, 1)
        act.activation(shifts_T[:, :], st_ps[:, :], ACT.Copy).then_inc(st_copied, 1)
        rings_of(act, NB, split.ring, lambda b, slot: split.high_parts(act, b, slot))

    @block.vector
    def _(dve):
        dve.sem_inc(split.low, 2 * split.ring)
        dve.wait_ge(ab_loaded, 16)
        dve.tensor_scalar(s1b[:, :], dots[:, 0, :], ab_all[:, :], None, ALU.add).then_inc(chain, 1)
        dve.wait_ge(chain, 1)
        dve.tensor_tensor(z[:, :], s1b[:, :], best[:, :], ALU.subtract).then_inc(chain, 1)
        dve.tensor_scalar(s1b_leak[:, :], s1b[:, :], LEAK, None, ALU.mult).then_inc(chain, 1)
        dve.wait_ge(chain, 2)
        dve.scalar_tensor_tensor(m[:, :], z[:, :], LEAK, z[:, :], ALU.mult, ALU.max).then_inc(chain, 1)
        dve.wait_ge(chain, 4)
        dve.tensor_tensor(shifts[:, 0:NT], s1b[:, :], m[:, :], ALU.subtract)
        dve.tensor_tensor(shifts[:, NT:2 * NT], s1b_leak[:, :], m[:, :], ALU.subtract).then_inc(chain, 1)
        dve.tensor_copy(s_cols[:, 0, :], dots[:, 1, :])
        dve.tensor_scalar(s_cols[:, 1, :], dots[:, 1, :], LEAK, None, ALU.mult)

        rings_of(dve, NB, split.ring, lambda b, slot: split.low_parts(dve, b, slot))

    @block.gpsimd
    def _(pool):
        for j in range(NT):
            diag = a_t[:, j, j * P:(j + 1) * P]
            pool.tensor_tensor(diag, diag, eye_bf, ALU.subtract)

    @block.tensor
    def _(pe):
        pe.wait_ge(chain, 5)
        pe.transpose(st_ps[:, :], shifts[:, :], eye).then_inc(st_done, 1)


PRODUCT_AT = (3, 6)
SUMS_AT = 3
FINISH_AT = (6, 9)


def attend(nc, s, a_t, x_parts, s_cols, shift_scratch, fc_w, fc_b, x_rows, out_rows, eps_half):
    RING = 3
    w_sb = s.sb("w_sb", [P, KT, D], FP32)
    fcb_all = s.sb("fcb_all", [P, D], FP32)
    shift = s.sb("shift", [P, 2, 2, BR], FP32)
    e_hi = s.sb("e_hi", [P, RING, 2, BR], FP32)
    e_leak = s.sb("e_leak", [P, 2, 2, BR], FP32)
    p_hi = s.sb("p_hi", [P, 2, 2, BR], FP16)
    p_lo = s.sb("p_lo", [P, 2, 2, BR], FP16)
    row_sum = s.sb("row_sum", [P, 2, 2, BR], FP32)
    ones = s.sb("ones", [P, 1], FP32)
    s_scaled = s.sb("s_scaled", [P, 2], FP32)
    s_inv = s.sb("s_inv", [P, 2], FP32)
    agg_sb = s.sb("agg_sb", [P, KT, BR], FP32)
    x_sb = s.sb("x_sb", [P, D], FP32)
    xn_sb = s.sb("xn_sb", [P, D], FP32)
    stats = s.sb("stats", [P, 6], FP32)
    mean_var = s.sb("mean_var", [P, 2], FP32)
    rstd = s.sb("rstd", [P, 1], FP32)
    agg_ps = [[s.ps(f"agg_ps{i}{j}", [P, D]) for j in range(2)] for i in range(2)]
    y_ps = [s.ps(f"y_ps{i}", [P, D]) for i in range(2)]
    sum_ps = s.ps("sum_ps", [P, 2])
    w_loaded = s.sem("w_loaded")
    shift_loaded = [s.sem(f"shift_loaded{i}") for i in range(2)]
    x_loaded = s.sem("x_loaded")
    exped = s.sem("exped")
    maxed = s.sem("maxed")
    weighed = s.sem("weighed")
    high = s.sem("high")
    split = s.sem("split")
    summed = s.sem("summed")
    used = s.sem("used")
    sums_done = s.sem("sums_done")
    copied = s.sem("copied")
    multiplied = s.sem("multiplied")
    taken = s.sem("taken")
    added = s.sem("added")
    inverse = s.sem("inverse")
    ones_set = s.sem("ones_set")
    normed = s.sem("normed")
    stored = s.sem("stored")
    block = s.block()
    GP = NT // 2

    def freed(g):
        return g + 1 if g < 2 else g

    def peeled(e, first, step):
        first()
        pairs_of(e, NB - 1, step)
        step(NB - 1, 0, last=True)

    @block.sync
    def _(sp):
        sp.sem_inc(stored, 16)

        def load_shift(b, slot):
            for i in range(2):
                sp.dma_start(shift[:, slot, i, :], shift_scratch[bass.ds(b * BR + i * NP, BR)].partition_broadcast(P))\
                  .then_inc(shift_loaded[slot], 16)

        def step(b, slot, last=False):
            if not last:
                sp.wait_ge(exped, b * GP + GP)
                load_shift(next_block(b + 2), slot)
            for t in range(2):
                sp.dma_start(x_sb[:, :], x_rows[bass.ds(b * BR + t * P, P), :]).then_inc(x_loaded, 16)
                sp.wait_ge(normed, b * (2 * NORM_STEPS) + (t + 1) * NORM_STEPS)
                sp.dma_start(out_rows[bass.ds(b * BR + t * P, P), :], xn_sb[:, :]).then_inc(stored, 16)

        load_shift(0, 0)
        load_shift(1, 1)
        sp.dma_start(w_sb[:, :, :], fc_w.rearrange("(k p) n -> p k n", p=P)).then_inc(w_loaded, 16)
        sp.dma_start(fcb_all[:, :], fc_b.partition_broadcast(P)).then_inc(w_loaded, 16)
        pairs_of(sp, NB - 1, step)
        step(NB - 1, 0, last=True)
        sp.wait_ge(stored, 32 * NB + 16)
        for i in range(2):
            sp.wait_ge(shift_loaded[i], 32 * (NB // 2 + 1))

    @block.scalar
    def _(act):
        act.sem_inc(copied, 4)

        def high_part(b, slot, g):
            ring = (slot + g) % 2
            act.wait_ge(weighed, b * GP + (g + 1))
            act.wait_ge(used, b * GP + (g + 1))
            act.activation(p_hi[:, ring, :, :], e_hi[:, g % RING, :, :], ACT.Copy, scale=P_TOP).then_inc(high, 1)

        def exps(b, slot, between=None):
            for g in range(GP):
                ring = (slot + g) % 2
                if g == 0:
                    act.wait_ge(shift_loaded[slot], (b - slot) * 16 + 32)
                act.wait_ge(split, b * GP + freed(g))
                act.wait_ge(summed, b * GP + freed(g))
                act.wait_ge(maxed, b * GP + (g + 1))
                for j in range(2):
                    for i, e in enumerate((e_hi[:, g % RING], e_leak[:, ring])):
                        done = act.activation(e[:, j, :], shift[:, slot, i, :], ACT.Exp,
                                              bias=s_cols[:, i, 2 * g + j:2 * g + j + 1])
                done.then_inc(exped, 1)
                if g > 0:
                    high_part(b, slot, g - 1)
                if g == 2 and between:
                    between()
            high_part(b, slot, GP - 1)

        def copy(b, slot):
            act.wait_ge(used, b * GP + (GP + 2))
            act.wait_ge(multiplied, b * 2 + 1)
            for i in range(2):
                act.activation(agg_sb[:, 2 * i:2 * i + 2, :].rearrange("p k n -> p (k n)"), agg_ps[slot][i][:, :],
                               ACT.Copy).then_inc(copied, 1)

        def step(b, slot, last=False):
            if last:
                copy(b, slot)
            else:
                exps(b + 1, 1 - slot, between=lambda: copy(b, slot))

        peeled(act, lambda: exps(0, 0), step)

    @block.gpsimd
    def _(pool):
        pool.sem_inc(summed, 2)

        def step(b, slot, between=None):
            flat = row_sum[:, slot]
            for g in range(GP):
                ring = (slot + g) % 2
                pool.wait_ge(weighed, b * GP + (g + 1))
                if g == 0:
                    if slot == 1 or not isinstance(b, int):
                        pool.wait_ge(sums_done, b)
                    pool.nop(nofuse=True)
                    pool.tensor_copy(flat, e_hi[:, g % RING, :, :]).then_inc(summed, 1)
                else:
                    pool.wait_ge(summed, b * GP + (g + 2))
                    pool.tensor_tensor(flat, flat, e_hi[:, g % RING, :, :], ALU.add).then_inc(summed, 1)
                if between:
                    between(g)

        def norm(b, t):
            inv_std(pool, mean_var[:, :], rstd[:, :], eps_half, normed, b * (2 * NORM_STEPS) + t * NORM_STEPS)

        def both(b, slot, last=False):
            if last:
                norm(b, 0)
                norm(b, 1)
            else:
                step(b + 1, 1 - slot, lambda g: norm(b, FINISH_AT.index(g)) if g in FINISH_AT else None)

        peeled(pool, lambda: step(0, 0), both)

    @block.vector
    def _(dve):
        dve.sem_inc(added, 1)
        dve.sem_inc(inverse, 1)
        dve.sem_inc(split, 2)
        dve.sem_inc(maxed, 2)
        dve.sem_inc(taken, 2)
        dve.memset(ones[:, :], 1.0).then_inc(ones_set, 1)

        def weigh(b, slot, g):
            ring = (slot + g) % 2
            dve.wait_ge(exped, b * GP + (g + 1))
            dve.tensor_tensor(e_hi[:, g % RING, :, :], e_hi[:, g % RING, :, :], e_leak[:, ring, :, :], ALU.max)\
               .then_inc(maxed, 1)
            dve.wait_ge(maxed, b * GP + (g + 3))
            dve.scalar_tensor_tensor(e_hi[:, g % RING, :, :], e_hi[:, g % RING, :, :], 1.0,
                                     a_t[:, 2 * g:2 * g + 2, bass.ds(b * BR, BR)], ALU.min, ALU.mult)\
               .then_inc(weighed, 1)

        def low_part(b, slot, g):
            ring = (slot + g) % 2
            dve.wait_ge(high, b * GP + (g + 1))
            dve.scalar_tensor_tensor(p_lo[:, ring, :, :], e_hi[:, g % RING, :, :], P_TOP, p_hi[:, ring, :, :], ALU.mult,
                                     ALU.subtract).then_inc(split, 1)

        def weights(b, slot, between=None):
            for g in range(GP):
                weigh(b, slot, g)
                if g > 0:
                    low_part(b, slot, g - 1)
                if between:
                    between(g)
            low_part(b, slot, GP - 1)

        def inverse_sums(b):
            dve.wait_ge(sums_done, b + 2)
            dve.tensor_scalar(s_scaled[:, :], sum_ps[:, :], P_TOP * X_TOP, None, ALU.mult).then_inc(inverse, 1)
            dve.wait_ge(inverse, b * 2 + 2)
            dve.reciprocal(s_inv[:, :], s_scaled[:, :]).then_inc(inverse, 1)
            dve.wait_ge(inverse, b * 2 + 3)

        def finish(b, t):
            dve.wait_ge(multiplied, b * 2 + (t + 2))
            dve.wait_ge(x_loaded, b * 32 + (t + 1) * 16)
            dve.scalar_tensor_tensor(x_sb[:, :], y_ps[t][:, :], s_inv[:, t:t + 1], x_sb[:, :], ALU.mult, ALU.add)\
               .then_inc(taken, 1)
            dve.wait_ge(taken, b * 2 + (t + 3))
            dve.tensor_tensor(x_sb[:, :], x_sb[:, :], fcb_all[:, :], ALU.add).then_inc(added, 1)
            dve.wait_ge(added, b * 2 + (t + 2))
            norm_moments(dve, x_sb[:, :], stats[:, :], mean_var[:, :], normed,
                         b * (2 * NORM_STEPS) + t * NORM_STEPS)

        def finish_norm(b, t):
            dve.wait_ge(stored, b * 32 + (t + 1) * 16)
            norm_apply(dve, x_sb[:, :], mean_var[:, :], rstd[:, :], xn_sb[:, :], normed,
                       b * (2 * NORM_STEPS) + t * NORM_STEPS)

        def step(b, slot, last=False):
            def between(g):
                if g == SUMS_AT:
                    inverse_sums(b)
                if g in FINISH_AT:
                    finish(b, FINISH_AT.index(g))
                if g - 1 in FINISH_AT:
                    finish_norm(b, FINISH_AT.index(g - 1))

            if last:
                inverse_sums(b)
                for t in range(2):
                    finish(b, t)
                    finish_norm(b, t)
            else:
                weights(b + 1, 1 - slot, between)

        def first():
            weights(0, 0)
            dve.wait_ge(w_loaded, 32)

        peeled(dve, first, step)

    @block.tensor
    def _(pe):
        pe.sem_inc(sums_done, 1)
        pe.sem_inc(multiplied, 1)
        pe.sem_inc(used, 2)
        pe.wait_ge(ones_set, 1)

        def gather(b, slot, between=None):
            pe.wait_ge(copied, b * 2 + 2)
            for g in range(GP):
                ring = (slot + g) % 2
                pe.wait_ge(split, b * GP + (g + 3))
                for c in range(KT):
                    for j in range(2):
                        for n, (x_part, p) in enumerate(((0, p_hi), (1, p_hi), (0, p_lo))):
                            first, last = (g == 0 and j == 0 and n == 0), (g == GP - 1 and j == 1 and n == 2)
                            mm = pe.matmul(agg_ps[slot][c // 2][:, (c % 2) * BR:(c % 2 + 1) * BR],
                                           x_parts[:, 2 * g + j, x_part, c * P:(c + 1) * P], p[:, ring, j, :],
                                           start=first and c % 2 == 0, stop=last, skip_group_check=True)
                mm.then_inc(used, 1)
                if between:
                    between(g)
            pe.wait_ge(inverse, b * 2 + 1)
            pe.wait_ge(summed, b * GP + (GP + 2))
            for t in range(2):
                for j in range(2):
                    mm = pe.matmul(sum_ps[:, t:t + 1], row_sum[:, slot, j, t * P:(t + 1) * P], ones[:, :],
                                   start=(j == 0), stop=(j == 1))
            mm.then_inc(sums_done, 1)

        def product(b, t):
            pe.wait_ge(copied, b * 2 + 6)
            pe.wait_ge(taken, b * 2 + (t + 1))
            for k in range(KT):
                mm = pe.matmul(y_ps[t][:, :], agg_sb[:, k, t * P:(t + 1) * P], w_sb[:, k, :],
                               start=(k == 0), stop=(k == KT - 1))
            mm.then_inc(multiplied, 1)

        def step(b, slot, last=False):
            if last:
                product(b, 0)
                product(b, 1)
            else:
                gather(b + 1, 1 - slot, lambda g: product(b, PRODUCT_AT.index(g)) if g in PRODUCT_AT else None)

        def first():
            gather(0, 0)
            pe.wait_ge(w_loaded, 32)

        peeled(pe, first, step)


def constants(nc, s, eye_in, fold_in, eye, eye_bf, fold, eps_half):
    loaded = s.sem("loaded")
    block = s.block()

    @block.sync
    def _(sp):
        sp.dma_start(eye, eye_in).then_inc(loaded, 16)
        sp.dma_start(fold, fold_in).then_inc(loaded, 16)

    @block.vector
    def _(dve):
        dve.memset(eps_half[:, 0:1], EPS)
        dve.memset(eps_half[:, 1:2], -0.5)
        dve.wait_ge(loaded, 32)
        dve.tensor_copy(eye_bf, eye)


def four_layers(nc, x, xT, adj, adjT, wqkv, wo, w1T, b1, w2T, b2, w_cat, a_w, a_b, fc_w, fc_b, w3, eye_in, fold_in,
                out):
    def scratch(name, shape, dt):
        return nc.dram_tensor(name, shape, dt, kind="Internal").ap()

    qk_parts = scratch("qk_parts", [2, 2, D, NP], FP32)
    v_parts = scratch("v_parts", [H, P, NT * P], FP16)
    o_rows = scratch("o_rows", [NP + BR, D], FP32)
    adjT_bf = scratch("adjT_bf", [NP, NP], BF16)
    x1, x2, x3 = (scratch(f"x{i}_rows", [NP, D], FP32) for i in (1, 2, 3))
    u_scratch = scratch("u_scratch", [2 * D], FP32)
    shift_scratch = scratch("shift_scratch", [2 * NP], FP32)

    with Scope(nc, "kept") as kept:
        eye = kept.sb("eye", [P, P], FP32)[:, :]
        eye_bf = kept.sb("eye_bf", [P, P], BF16)[:, :]
        fold = kept.sb("fold", [P, HD], FP32)[:, :]
        eps_half = kept.sb("eps_half", [P, 2], FP32)
        v_inv = kept.sb("v_inv", [P, 1], FP32)[:, :]
        deg = kept.sb("deg", [P, NT], FP32)[:, :]
        r = kept.sb("r", [P, NT], FP32)[:, :]
        r_in = kept.sb("r_in", [P, NT], FP32)[:, :]
        r_out = kept.sb("r_out", [P, NT], FP32)[:, :]
        dots = kept.sb("dots", [P, 2, NT], FP32)
        best = kept.sb("best", [P, NT], FP32)
        s_cols = kept.sb("s_cols", [P, 2, NT], FP32)
        with Scope(nc, "constants") as s:
            constants(nc, s, eye_in, fold_in, eye, eye_bf, fold, eps_half)

        with Scope(nc, "attention") as s:
            probs = s.sb("probs", [P, 2, 2, NP], FP32)
            v_all = probs[:, :, :, :].rearrange("p i t n -> p (i t n)")
            v_tops = s.sb("v_tops", [P, NB], FP32)[:, :]
            with Scope(nc, "project") as project:
                project_qkv(nc, project, xT, wqkv, qk_parts, v_all, v_tops, w_cat, a_w, u_scratch, eye)
            inputs = AttentionInputs(s, adj, qk_parts)
            with Scope(nc, "split_v") as split:
                split_values(nc, split, v_all, v_tops, v_parts, eye, v_inv, inputs)
            attention(nc, s, inputs, probs, v_parts, o_rows, eye, fold, v_inv, deg, adjT, adjT_bf)
        a_t = kept.sb("a_t", [P, NT, NP], BF16)
        with Scope(nc, "vectors") as vectors:
            u_all = vectors.sb("u_all", [P, 2, D], FP32)
            g_parts = vectors.sb("g_parts", [P, NT, 3, w1T.shape[1]], BF16)
            r_parts = vectors.sb("r_parts", [P, NT, 3], BF16)
            with Scope(nc, "first_rows") as s:
                first_rows(nc, s, x, o_rows, wo, w1T, b1, deg, r, r_in, r_out, u_scratch, u_all[:, :, :], x1,
                           g_parts, r_parts, adjT_bf, a_t, eye, eye_bf, eps_half)
            with Scope(nc, "linear") as s:
                aggregate(nc, s, "linear", a_t, g_parts, w2T, b2, x1, x2, r, r_parts, eps_half, u_all=u_all,
                          dots=dots, best=best, eye=eye)

        with Scope(nc, "rows") as rows:
            x_parts = rows.sb("x_parts", [P, NT, 2, D], FP16)
            with Scope(nc, "row_shifts") as s:
                row_shifts(nc, s, x2, x_parts, a_t, best, eye, eye_bf, dots, a_b, s_cols, shift_scratch)
            with Scope(nc, "attend") as s:
                attend(nc, s, a_t, x_parts, s_cols, shift_scratch, fc_w, fc_b, x2, x3, eps_half)

            with Scope(nc, "relu") as s:
                aggregate(nc, s, "relu", a_t, x_parts, w3, None, x3, out, r_out, None, eps_half, r_in=r_in,
                          eye_bf=eye_bf)


def kernel(**inputs):
    import numpy as _np
    import concourse.bacc as _bacc
    from concourse import mybir as _mybir
    from concourse.bass_utils import run_bass_kernel_spmd as _run

    a = {name: _np.asarray(value) for name, value in inputs.items()}
    f32 = _np.float32

    def rows_padded(m, columns):
        out = _np.zeros((NP, columns), f32)
        out[:m.shape[0], :m.shape[1]] = m
        return out

    adjT = rows_padded(a["adj"].T, NP)
    adjT[N:, N:] = _np.eye(NP - N, dtype=f32)
    x = rows_padded(a["x"], D)
    arrays = {
        "x": x,
        "xT": x.T,
        "adj": rows_padded(a["adj"], NP),
        "adjT": adjT,
        "wqkv": _np.stack([a[f"L0_gnn_{w}"].transpose(1, 0, 2).reshape(D, D) for w in ("Wqs", "Wks", "Wvs")]),
        "wo": a["L0_gnn_Wo"].reshape(D, D),
        "w1T": a["L1_gnn_W1"].T,
        "b1": a["L1_gnn_b1"],
        "w2T": a["L1_gnn_W2"].T,
        "b2": a["L1_gnn_b2"],
        "w_cat": a["L2_gnn_W"],
        "a_w": a["L2_gnn_a_w"],
        "a_b": a["L2_gnn_a_b"].reshape(1),
        "fc_w": a["L2_gnn_fc_w"],
        "fc_b": a["L2_gnn_fc_b"],
        "w3": a["L3_gnn_W"],
        "eye_in": _np.eye(P, dtype=f32),
        "fold_in": _np.vstack([_np.eye(HD, dtype=f32)] * 2),
    }
    arrays = {name: _np.ascontiguousarray(value) for name, value in arrays.items()}

    nc = _bacc.Bacc("TRN2", target_bir_lowering=False, num_devices=1)
    args = {name: nc.dram_tensor(name, v.shape, _mybir.dt.from_np(v.dtype), kind="ExternalInput").ap()
            for name, v in arrays.items()}
    out = nc.dram_tensor("out", (NP, D), _mybir.dt.float32, kind="ExternalOutput").ap()
    four_layers(nc, out=out, **args)
    result = _run(nc, [arrays], core_ids=[0])
    return result.results[0]["out"][:N]
```
